# Optimizing a Trainium2 kernel written in Bass

```python
import numpy as np
import jax
import jax.numpy as jnp

def _softmax(x, axis=-1):
    return jax.nn.softmax(x, axis=axis)

def _gelu(x):
    return jax.nn.gelu(x, approximate=True)

def _silu(x):
    return jax.nn.silu(x)

def _sigmoid(x):
    return jax.nn.sigmoid(x)

def _layernorm(x, axis=-1, eps=1e-05):
    m = jnp.mean(x, axis=axis, keepdims=True)
    v = jnp.var(x, axis=axis, keepdims=True)
    return (x - m) / jnp.sqrt(v + eps)

def _scatter_add(tgt, idx, src, axis=0):
    return tgt.at[idx].add(src)

def _segment_sum(src, seg, n):
    return jax.ops.segment_sum(src, seg, n)
kernel_name = 'mk_adaln_d2_jaxref_r4_c096ce'

def setup_inputs(seed: int=0):
    np.random.seed(seed)
    _w = jnp.asarray

    def _L0_attn_setup():
        import jax, jax.numpy as jnp
        import numpy as np
        DECAY = 0.99
        T_BLK = 128

        def _decay_mats(N_blk, dtype):
            i = jnp.arange(T_BLK, dtype=jnp.float32)[:, None]
            j = jnp.arange(T_BLK, dtype=jnp.float32)[None, :]
            decays = jnp.tril(jnp.asarray(DECAY, jnp.float32) ** (i - j)).astype(dtype)
            bi = jnp.arange(N_blk, dtype=jnp.float32)[:, None]
            bj = jnp.arange(N_blk, dtype=jnp.float32)[None, :]
            block_decay = DECAY ** T_BLK
            block_decays = jnp.tril(DECAY * jnp.asarray(block_decay, jnp.float32) ** (bi - bj)).astype(dtype)
            return (decays, block_decays)
        key = jax.random.key(seed)
        ks = jax.random.split(key, 8)
        B, T, E = (4, 1024, 256)
        Dk, Dv = (256, 256)
        s = 0.02
        return {'x': jax.random.normal(ks[0], (B, T, E), jnp.float32), 'Wv': jax.random.normal(ks[1], (E, Dv), jnp.float32) * s, 'Wk': jax.random.normal(ks[2], (E, Dk), jnp.float32) * s, 'bk': jax.random.normal(ks[3], (Dk,), jnp.float32) * s, 'Wq': jax.random.normal(ks[4], (E, Dk), jnp.float32) * s, 'bq': jax.random.normal(ks[5], (Dk,), jnp.float32) * s, 'Wo': jax.random.normal(ks[6], (Dv, E), jnp.float32) * s}
    _L0_attn_in = _L0_attn_setup()

    def _L0_ffn_setup():
        import jax, jax.numpy as jnp
        import numpy as np
        B, S, D = (4, 1024, 256)
        E, K, H = (8, 2, 512)
        key = jax.random.key(seed)
        ks = jax.random.split(key, 6)
        scale_g = 1.0 / np.sqrt(D)
        scale_1 = 1.0 / np.sqrt(D)
        scale_2 = 1.0 / np.sqrt(H)
        return {'x': jax.random.normal(ks[0], (B, S, D), dtype=jnp.float32), 'Wg': jax.random.uniform(ks[1], (D, E), jnp.float32, -scale_g, scale_g), 'W1': jax.random.uniform(ks[2], (E, D, H), jnp.float32, -scale_1, scale_1), 'b1': jax.random.uniform(ks[3], (E, H), jnp.float32, -scale_1, scale_1), 'W2': jax.random.uniform(ks[4], (E, H, D), jnp.float32, -scale_2, scale_2), 'b2': jax.random.uniform(ks[5], (E, D), jnp.float32, -scale_2, scale_2)}
    _L0_ffn_in = _L0_ffn_setup()
    _L0_c = _w((lambda *s: np.random.randn(*s).astype(np.float32) * 0.05)(1, 256))
    _L0_wmod = _w((lambda *s: np.random.randn(*s).astype(np.float32) * 0.05)(256, 6 * 256) * 256 ** (-0.5))

    def _L1_attn_setup():
        import jax, jax.numpy as jnp
        import numpy as np
        NUM_HEADS = 16
        EPS = 1e-06

        def _split_heads(t, h):
            b, s, d = t.shape
            return t.reshape(b, s, h, d // h).transpose(0, 2, 1, 3)
        key = jax.random.key(seed)
        ks = jax.random.split(key, 6)
        b, s, d = (4, 1024, 256)
        scale = 1.0 / np.sqrt(d)
        return {'x': jax.random.normal(ks[0], (b, s, d), dtype=jnp.float32), 'wq': jax.random.normal(ks[1], (d, d), dtype=jnp.float32) * scale, 'wk': jax.random.normal(ks[2], (d, d), dtype=jnp.float32) * scale, 'wv': jax.random.normal(ks[3], (d, d), dtype=jnp.float32) * scale, 'wo': jax.random.normal(ks[4], (d, d), dtype=jnp.float32) * scale, 'bo': jnp.zeros((d,), dtype=jnp.float32)}
    _L1_attn_in = _L1_attn_setup()

    def _L1_ffn_setup():
        import jax, jax.numpy as jnp
        import numpy as np
        DIM = 256
        HEADS = 16
        HD = DIM // HEADS
        M = 64
        E = 4
        K = 2
        HID = 512
        MID = 512
        LB = 0.01
        EPS = 1.1920929e-07

        def _rms(x, w):
            return x * jax.lax.rsqrt(jnp.mean(x * x, axis=-1, keepdims=True) + EPS) * w

        def _gelu(x):
            return jax.nn.gelu(x, approximate=False)
        key = jax.random.key(seed)
        ks = jax.random.split(key, 20)
        d = DIM
        w = lambda k, s: jax.random.normal(k, s, jnp.float32) * 0.02
        return {'x': jax.random.normal(ks[0], (4, 256, d), jnp.float32), 'n1_w': jnp.ones((d,), jnp.float32), 'n2_w': jnp.ones((d,), jnp.float32), 'wq': w(ks[1], (d, d)), 'wk': w(ks[2], (d, d)), 'wv': w(ks[3], (d, d)), 'wo': w(ks[4], (d, d)), 'qn_w': jnp.ones((HD,), jnp.float32), 'kn_w': jnp.ones((HD,), jnp.float32), 'gate_w': w(ks[5], (E, d)), 'e0_up': w(ks[6], (HID, d)), 'e0_down': w(ks[7], (d, HID)), 'e1_w1': w(ks[8], (HID, d)), 'e1_w2': w(ks[9], (HID, d)), 'e1_down': w(ks[10], (d, HID)), 'e2_l1': w(ks[11], (MID, d)), 'e2_l2': w(ks[12], (HID, MID)), 'e2_l3': w(ks[13], (MID, HID)), 'e2_l4': w(ks[14], (d, MID)), 'e3_down': w(ks[15], (d, d)), 'e3_up': w(ks[16], (HID, d)), 'e3_out': w(ks[17], (d, HID))}
    _L1_ffn_in = _L1_ffn_setup()
    _L1_c = _w((lambda *s: np.random.randn(*s).astype(np.float32) * 0.05)(1, 256))
    _L1_wmod = _w((lambda *s: np.random.randn(*s).astype(np.float32) * 0.05)(256, 6 * 256) * 256 ** (-0.5))
    _d = {'L0_attn_x': _L0_attn_in['x'], 'L0_attn_Wv': _L0_attn_in['Wv'], 'L0_attn_Wk': _L0_attn_in['Wk'], 'L0_attn_bk': _L0_attn_in['bk'], 'L0_attn_Wq': _L0_attn_in['Wq'], 'L0_attn_bq': _L0_attn_in['bq'], 'L0_attn_Wo': _L0_attn_in['Wo'], 'L0_ffn_Wg': _L0_ffn_in['Wg'], 'L0_ffn_W1': _L0_ffn_in['W1'], 'L0_ffn_b1': _L0_ffn_in['b1'], 'L0_ffn_W2': _L0_ffn_in['W2'], 'L0_ffn_b2': _L0_ffn_in['b2'], 'L0_c': _L0_c, 'L0_wmod': _L0_wmod, 'L1_attn_wq': _L1_attn_in['wq'], 'L1_attn_wk': _L1_attn_in['wk'], 'L1_attn_wv': _L1_attn_in['wv'], 'L1_attn_wo': _L1_attn_in['wo'], 'L1_attn_bo': _L1_attn_in['bo'], 'L1_ffn_n1_w': _L1_ffn_in['n1_w'], 'L1_ffn_n2_w': _L1_ffn_in['n2_w'], 'L1_ffn_wq': _L1_ffn_in['wq'], 'L1_ffn_wk': _L1_ffn_in['wk'], 'L1_ffn_wv': _L1_ffn_in['wv'], 'L1_ffn_wo': _L1_ffn_in['wo'], 'L1_ffn_qn_w': _L1_ffn_in['qn_w'], 'L1_ffn_kn_w': _L1_ffn_in['kn_w'], 'L1_ffn_gate_w': _L1_ffn_in['gate_w'], 'L1_ffn_e0_up': _L1_ffn_in['e0_up'], 'L1_ffn_e0_down': _L1_ffn_in['e0_down'], 'L1_ffn_e1_w1': _L1_ffn_in['e1_w1'], 'L1_ffn_e1_w2': _L1_ffn_in['e1_w2'], 'L1_ffn_e1_down': _L1_ffn_in['e1_down'], 'L1_ffn_e2_l1': _L1_ffn_in['e2_l1'], 'L1_ffn_e2_l2': _L1_ffn_in['e2_l2'], 'L1_ffn_e2_l3': _L1_ffn_in['e2_l3'], 'L1_ffn_e2_l4': _L1_ffn_in['e2_l4'], 'L1_ffn_e3_down': _L1_ffn_in['e3_down'], 'L1_ffn_e3_up': _L1_ffn_in['e3_up'], 'L1_ffn_e3_out': _L1_ffn_in['e3_out'], 'L1_c': _L1_c, 'L1_wmod': _L1_wmod}
    _x0 = _d['L0_attn_x']
    _d['L0_attn_x'] = jax.random.normal(jax.random.fold_in(jax.random.key(seed), 1), (1, 4096, 256), dtype=_x0.dtype)
    del _x0
    return _d

def reference(L0_attn_x, L0_attn_Wv, L0_attn_Wk, L0_attn_bk, L0_attn_Wq, L0_attn_bq, L0_attn_Wo, L0_ffn_Wg, L0_ffn_W1, L0_ffn_b1, L0_ffn_W2, L0_ffn_b2, L0_c, L0_wmod, L1_attn_wq, L1_attn_wk, L1_attn_wv, L1_attn_wo, L1_attn_bo, L1_ffn_n1_w, L1_ffn_n2_w, L1_ffn_wq, L1_ffn_wk, L1_ffn_wv, L1_ffn_wo, L1_ffn_qn_w, L1_ffn_kn_w, L1_ffn_gate_w, L1_ffn_e0_up, L1_ffn_e0_down, L1_ffn_e1_w1, L1_ffn_e1_w2, L1_ffn_e1_down, L1_ffn_e2_l1, L1_ffn_e2_l2, L1_ffn_e2_l3, L1_ffn_e2_l4, L1_ffn_e3_down, L1_ffn_e3_up, L1_ffn_e3_out, L1_c, L1_wmod):

    def _L0_attn_ref(x, Wv, Wk, bk, Wq, bq, Wo):
        import jax, jax.numpy as jnp
        import numpy as np
        DECAY = 0.99
        T_BLK = 128

        def _decay_mats(N_blk, dtype):
            i = jnp.arange(T_BLK, dtype=jnp.float32)[:, None]
            j = jnp.arange(T_BLK, dtype=jnp.float32)[None, :]
            decays = jnp.tril(jnp.asarray(DECAY, jnp.float32) ** (i - j)).astype(dtype)
            bi = jnp.arange(N_blk, dtype=jnp.float32)[:, None]
            bj = jnp.arange(N_blk, dtype=jnp.float32)[None, :]
            block_decay = DECAY ** T_BLK
            block_decays = jnp.tril(DECAY * jnp.asarray(block_decay, jnp.float32) ** (bi - bj)).astype(dtype)
            return (decays, block_decays)
        B, T, E = x.shape
        N_blk = T // T_BLK
        decays, block_decays = _decay_mats(N_blk, x.dtype)
        v = x @ Wv * (1.0 - DECAY)
        k = jax.nn.sigmoid(x @ Wk + bk)
        q = jax.nn.sigmoid(x @ Wq + bq)
        Dv, Dk = (v.shape[-1], k.shape[-1])
        v = v.reshape(B, N_blk, T_BLK, Dv)
        k = k.reshape(B, N_blk, T_BLK, Dk)
        q = q.reshape(B, N_blk, T_BLK, Dk)
        a = jnp.einsum('bntd,bnsd->bnts', q, k) * decays
        y = jnp.einsum('bnts,bnsv->bntv', a, v)
        kv_blk = jnp.einsum('bntd,bntv->bndv', k, v * decays[T_BLK - 1, :, None])
        kv2 = jnp.concatenate([jnp.zeros_like(kv_blk[:, :1]), kv_blk[:, :-1]], axis=1)
        kv = jnp.einsum('nm,bmdv->bndv', block_decays, kv2)
        y2 = jnp.einsum('bntd,bndv->bntv', q, kv) * decays[:, :1]
        y = (y + y2).reshape(B, T, Dv)
        return y @ Wo

    def _L0_ffn_ref(x, Wg, W1, b1, W2, b2):
        import jax, jax.numpy as jnp
        import numpy as np
        B, S, D = (4, 1024, 256)
        E, K, H = (8, 2, 512)
        logits = jnp.einsum('bsd,de->bse', x, Wg)
        probs = jax.nn.softmax(logits, axis=-1)
        topv, topi = jax.lax.top_k(probs, K)
        cw = topv / (jnp.sum(topv, axis=-1, keepdims=True) + 1e-09)
        we = jnp.sum(jax.nn.one_hot(topi, E, dtype=x.dtype) * cw[..., None], axis=-2)
        y = jnp.zeros_like(x)
        for e in range(E):
            h = jax.nn.relu(jnp.einsum('bsd,dh->bsh', x, W1[e]) + b1[e])
            out_e = jnp.einsum('bsh,hd->bsd', h, W2[e]) + b2[e]
            y = y + we[..., e:e + 1] * out_e
        return y

    def _L1_attn_ref(x, wq, wk, wv, wo, bo):
        import jax, jax.numpy as jnp
        import numpy as np
        NUM_HEADS = 16
        EPS = 1e-06

        def _split_heads(t, h):
            b, s, d = t.shape
            return t.reshape(b, s, h, d // h).transpose(0, 2, 1, 3)
        h = NUM_HEADS
        q = _split_heads(x @ wq.T, h)
        k = _split_heads(x @ wk.T, h)
        v = _split_heads(x @ wv.T, h)
        qf = jax.nn.elu(q) + 1.0
        kf = jax.nn.elu(k) + 1.0
        k_sum = jnp.sum(kf, axis=-2)
        denom = jnp.sum(qf * k_sum[:, :, None, :], axis=-1, keepdims=True) + EPS
        kv = jnp.einsum('bhsd,bhse->bhde', kf, v)
        q_kv = jnp.einsum('bhsd,bhde->bhse', qf, kv)
        out = q_kv / denom
        b, _, s, dh = out.shape
        out = out.transpose(0, 2, 1, 3).reshape(b, s, h * dh)
        return out @ wo.T + bo

    def _L1_ffn_ref(x, n1_w, n2_w, wq, wk, wv, wo, qn_w, kn_w, gate_w, e0_up, e0_down, e1_w1, e1_w2, e1_down, e2_l1, e2_l2, e2_l3, e2_l4, e3_down, e3_up, e3_out):
        import jax, jax.numpy as jnp
        import numpy as np
        DIM = 256
        HEADS = 16
        HD = DIM // HEADS
        M = 64
        E = 4
        K = 2
        HID = 512
        MID = 512
        LB = 0.01
        EPS = 1.1920929e-07

        def _rms(x, w):
            return x * jax.lax.rsqrt(jnp.mean(x * x, axis=-1, keepdims=True) + EPS) * w

        def _gelu(x):
            return jax.nn.gelu(x, approximate=False)
        B, T, C = x.shape
        h = _rms(x, n1_w)
        heads = lambda w_: (h @ w_.T).reshape(B, T, HEADS, HD).transpose(0, 2, 1, 3)
        q = _rms(heads(wq), qn_w)
        k = _rms(heads(wk), kn_w)
        v = heads(wv)
        scores = jnp.einsum('bhqd,bhkd->bhqk', q, k) * HD ** (-0.5)
        causal = jnp.tril(jnp.ones((T, T), bool))
        scores = jnp.where(causal[None, None], scores, -jnp.inf)
        attn = jax.nn.softmax(scores, axis=-1)
        ao = jnp.einsum('bhqk,bhkd->bhqd', attn, v).transpose(0, 2, 1, 3).reshape(B, T, C) @ wo.T
        ao = ao.at[:, :, :M].set(0.0)
        x = x + ao
        xf = _rms(x, n2_w).reshape(-1, C)
        N = xf.shape[0]
        logits = jnp.nan_to_num(xf @ gate_w.T)
        probs = jax.nn.softmax(logits, axis=-1)
        topv, topi = jax.lax.top_k(probs, K)
        topv = topv / (topv.sum(-1, keepdims=True) + 1e-08)
        wts = jnp.zeros((N, E), x.dtype).at[jnp.arange(N)[:, None], topi].add(topv)
        o0 = _gelu(xf @ e0_up.T) @ e0_down.T
        o1 = jax.nn.silu(xf @ e1_w1.T) * (xf @ e1_w2.T) @ e1_down.T
        o2 = _gelu(_gelu(_gelu(xf @ e2_l1.T) @ e2_l2.T) @ e2_l3.T) @ e2_l4.T
        o3 = _gelu(_gelu(xf @ e3_down.T) @ e3_up.T) @ e3_out.T
        moe = wts[:, 0:1] * o0 + wts[:, 1:2] * o1 + wts[:, 2:3] * o2 + wts[:, 3:4] * o3
        moe = moe.reshape(B, T, C).at[:, :, :M].set(0.0)
        return x + moe
    x = L0_attn_x
    mod = (_silu(L0_c) @ L0_wmod).reshape(L0_c.shape[0], 6, 1, -1)
    sa, ca, ga, sb, cb, gb = (mod[:, 0], mod[:, 1], mod[:, 2], mod[:, 3], mod[:, 4], mod[:, 5])
    ga = (2 * (ga >= 0) - 1) * jnp.maximum(jnp.abs(ga), 0.25)
    gb = (2 * (gb >= 0) - 1) * jnp.maximum(jnp.abs(gb), 0.25)
    h = _layernorm(x, axis=-1) * (1 + ca) + sa
    x = x + ga * _L0_attn_ref(h, L0_attn_Wv, L0_attn_Wk, L0_attn_bk, L0_attn_Wq, L0_attn_bq, L0_attn_Wo)
    h = _layernorm(x, axis=-1) * (1 + cb) + sb
    x = x + gb * _L0_ffn_ref(h, L0_ffn_Wg, L0_ffn_W1, L0_ffn_b1, L0_ffn_W2, L0_ffn_b2)
    mod = (_silu(L1_c) @ L1_wmod).reshape(L1_c.shape[0], 6, 1, -1)
    sa, ca, ga, sb, cb, gb = (mod[:, 0], mod[:, 1], mod[:, 2], mod[:, 3], mod[:, 4], mod[:, 5])
    ga = (2 * (ga >= 0) - 1) * jnp.maximum(jnp.abs(ga), 0.25)
    gb = (2 * (gb >= 0) - 1) * jnp.maximum(jnp.abs(gb), 0.25)
    h = _layernorm(x, axis=-1) * (1 + ca) + sa
    x = x + ga * _L1_attn_ref(h, L1_attn_wq, L1_attn_wk, L1_attn_wv, L1_attn_wo, L1_attn_bo)
    h = _layernorm(x, axis=-1) * (1 + cb) + sb
    x = x + gb * _L1_ffn_ref(h, L1_ffn_n1_w, L1_ffn_n2_w, L1_ffn_wq, L1_ffn_wk, L1_ffn_wv, L1_ffn_wo, L1_ffn_qn_w, L1_ffn_kn_w, L1_ffn_gate_w, L1_ffn_e0_up, L1_ffn_e0_down, L1_ffn_e1_w1, L1_ffn_e1_w2, L1_ffn_e1_down, L1_ffn_e2_l1, L1_ffn_e2_l2, L1_ffn_e2_l3, L1_ffn_e2_l4, L1_ffn_e3_down, L1_ffn_e3_up, L1_ffn_e3_out)
    return x

_drawn_inputs = setup_inputs


def setup_inputs(seed=0):
    import zlib

    import numpy as np

    out = dict(_drawn_inputs(seed))
    spreads = {'L1_attn_bo': (0.0, 0.331),
     'L1_ffn_n1_w': (1.0, 0.6),
     'L1_ffn_n2_w': (1.0, 0.6),
     'L1_ffn_qn_w': (1.0, 0.6),
     'L1_ffn_kn_w': (1.0, 0.6)}
    factors = {'L0_attn_Wk': 8.0,
     'L0_attn_bk': 200.0,
     'L0_attn_Wq': 163.298,
     'L0_attn_bq': 200.0,
     'L0_ffn_b1': 8.0,
     'L0_ffn_b2': 8.0,
     'L1_attn_wq': 8.0,
     'L1_attn_wk': 8.0,
     'L1_attn_wv': 7.213,
     'L1_attn_wo': 6.393,
     'L1_ffn_wq': 8.0,
     'L1_ffn_wk': 8.0,
     'L1_ffn_wv': 8.0,
     'L1_ffn_wo': 8.0,
     'L1_ffn_gate_w': 8.0,
     'L1_ffn_e0_up': 64.0,
     'L1_ffn_e0_down': 64.0,
     'L1_ffn_e1_w1': 25.865,
     'L1_ffn_e1_w2': 23.442,
     'L1_ffn_e1_down': 8.0,
     'L1_ffn_e2_l1': 8.0,
     'L1_ffn_e2_l2': 8.0,
     'L1_ffn_e2_l3': 8.0,
     'L1_ffn_e2_l4': 8.0,
     'L1_ffn_e3_down': 8.0,
     'L1_ffn_e3_up': 8.0,
     'L1_ffn_e3_out': 8.0}
    for name, (base, spread) in spreads.items():
        noise = np.random.default_rng([zlib.crc32(name.encode()), seed]).standard_normal(out[name].shape)
        drawn = base * np.exp(spread * noise) if base else spread * noise
        out[name] = jnp.asarray(drawn.astype(out[name].dtype))
    for name, factor in factors.items():
        out[name] = (out[name] * factor).astype(out[name].dtype)
    return out
```

```python
from contextlib import ExitStack

import numpy as np
import concourse.bass as bass
from concourse import mybir

ALU = mybir.AluOpType
ACT = mybir.ActivationFunctionType
F32 = mybir.dt.float32
BF16 = mybir.dt.bfloat16
U32 = mybir.dt.uint32
AX = mybir.AxisListType.X

P = 128
T = 4096
D = 256
KH = D // P
TILES = 4
CH = TILES * P
NC = T // CH
DECAY = 0.99
PRIMED = 1
E0, H0 = 8, 512
E1, H1 = 4, 512
HEADS, HD = 16, 16
GROUPS, GH = 4, 4
MASKED = 64
KEEP = D - MASKED
SPLIT = 6 * HD
ROWS = SPLIT + 3


class Tally:

    def __init__(self, base=0):
        self.base, self.n = base, 0

    def up(self, k=1):
        self.n += k
        return self.base + self.n


def wait_first(eng, sem, value, met=None):
    held = eng.alloc_register()
    eng.reg_mov(held, value)
    eng.wait_ge(met or sem, 1)
    eng.wait_ge(sem, held)
    eng.free_register(held)


def merged(ap):
    return ap.rearrange("p a b -> p (a b)")


def setup(nc, d, s):
    with ExitStack() as ctx:
        sb = lambda n, sh, dt=F32: ctx.enter_context(nc.sbuf_tensor(n, sh, dt))
        sem = lambda n: ctx.enter_context(nc.semaphore(n))
        psum = [ctx.enter_context(nc.psum_tensor(f"set_ps{i}", [P, 512], F32)) for i in range(8)]
        wmod = sb("wmod", [P, 2, KH, 6 * D])
        cvec = sb("cvec", [P, 2, KH])
        silu_c = sb("silu_c", [P, 2, KH])
        silu_rep = sb("silu_rep", [P, 2, KH, P])
        wvT = sb("wvT", [P, KH, D])
        wo0 = sb("wo0", [P, KH, D])
        raw = sb("gate_raw", [P, 4, D])
        sign = sb("gate_sign", [P, 4, D])
        size = sb("gate_size", [P, 4, D])
        loaded, silu_done, rep_done, mod_done, cols_done = (sem(x) for x in
            ("mod_loaded", "silu_done", "rep_done", "mod_done", "cols_done"))
        raw_done, sign_done, gates_done, wv_done, fold_done = (sem(x) for x in
            ("raw_done", "sign_done", "gates_done", "wv_done", "fold_done"))
        with nc.Block() as block:
            @block.sync
            def _(sp):
                for dst, src in ((cvec, d["cvec"]), (wmod, d["wmod"]), (wvT, d["wvT"]), (wo0, d["wo0"]),
                                 (s["wo1"], d["wo1"]), (s["bo1"], d["bo1"])):
                    sp.dma_start(dst[:], src).then_inc(loaded, 16)

            @block.scalar
            def _(act):
                act.wait_ge(loaded, 96)
                nc.scalar.activation(silu_c[:], cvec[:], ACT.Silu).then_inc(silu_done, 1)

            @block.tensor
            def _(pe):
                pe.wait_ge(rep_done, 1)
                for layer in range(2):
                    for n in range(3):
                        for k in range(KH):
                            last = nc.tensor.matmul(psum[3 * layer + n][:], silu_rep[:, layer, k, :],
                                                    wmod[:, layer, k, n * 512:(n + 1) * 512],
                                                    start=k == 0, stop=k == KH - 1)
                last.then_inc(mod_done, 1)
                for layer in range(2):
                    for i, m in enumerate((0, 1, 3, 4)):
                        for h in range(KH):
                            col = (layer * 4 + i) * KH + h
                            for k in range(KH):
                                last = nc.tensor.matmul(
                                    psum[6][:, col:col + 1],
                                    wmod[:, layer, k, m * D + h * P:m * D + (h + 1) * P],
                                    silu_c[:, layer, k:k + 1], start=k == 0, stop=k == KH - 1)
                last.then_inc(mod_done, 1)
                for h in range(KH):
                    for k in range(KH):
                        last = nc.tensor.matmul(psum[7][:, h * D:(h + 1) * D], wvT[:, k, h * P:(h + 1) * P],
                                                wo0[:, k, :], start=k == 0, stop=k == KH - 1)
                last.then_inc(wv_done, 1)

            @block.vector
            def _(v):
                v.wait_ge(silu_done, 1)
                nc.vector.tensor_copy(silu_rep[:].rearrange("p a b c -> p (a b) c"),
                                      merged(silu_c[:]).unsqueeze(2).to_broadcast([P, 2 * KH, P])).then_inc(rep_done, 1)
                v.wait_ge(mod_done, 1)
                nc.vector.tensor_copy(raw[:, 0, :], psum[1][:, 0:D])
                nc.vector.tensor_copy(raw[:, 1, :], psum[2][:, D:2 * D])
                nc.vector.tensor_copy(raw[:, 2, :], psum[4][:, 0:D])
                nc.vector.tensor_copy(raw[:, 3, :], psum[5][:, D:2 * D])
                nc.vector.tensor_copy(s["sb1"][:], psum[4][:, D:2 * D])
                nc.vector.tensor_scalar(s["cb1"][:], psum[5][:, 0:D], 1.0, None, ALU.add).then_inc(raw_done, 1)
                v.wait_ge(raw_done, 1)
                nc.vector.tensor_scalar(sign[:], raw[:], 0.0, 2.0, ALU.is_ge, ALU.mult)
                nc.vector.tensor_scalar(size[:], raw[:], -1.0, None, ALU.mult).then_inc(sign_done, 1)
                v.wait_ge(sign_done, 1)
                nc.vector.tensor_tensor(size[:], size[:], raw[:], ALU.max).then_inc(sign_done, 1)
                v.wait_ge(sign_done, 2)
                nc.vector.tensor_scalar(size[:], size[:], 0.25, None, ALU.max).then_inc(sign_done, 1)
                v.wait_ge(sign_done, 3)
                nc.vector.scalar_tensor_tensor(s["gates"][:].rearrange("p a b -> p (a b)"), merged(sign[:]), -1.0,
                                               merged(size[:]), ALU.add, ALU.mult).then_inc(gates_done, 1)
                v.wait_ge(mod_done, 2)
                nc.vector.tensor_copy(s["modc"][:], psum[6][:, 0:16]).then_inc(cols_done, 1)
                v.wait_ge(cols_done, 1)
                for i in (1, 3, 5, 7):
                    nc.vector.tensor_scalar(s["modc"][:, KH * i:KH * i + KH], s["modc"][:, KH * i:KH * i + KH], 1.0, None, ALU.add)
                v.wait_ge(gates_done, 1)
                v.wait_ge(wv_done, 1)
                for h in range(KH):
                    nc.vector.scalar_tensor_tensor(s["wv0"][:, h, :], psum[7][:, h * D:(h + 1) * D], 1.0 - DECAY,
                                                   s["gates"][:, 0, :], ALU.mult, ALU.mult)
                for k in range(KH):
                    nc.vector.tensor_tensor(s["wo1"][:, k, :], s["wo1"][:, k, :], s["gates"][:, 2, :], ALU.mult)
                nc.vector.tensor_tensor(s["bo1"][:], s["bo1"][:], s["gates"][:, 2, :], ALU.mult)
                nc.vector.tensor_copy(s["gb1"][:], s["gates"][:, 3, :]).then_inc(fold_done, 1)
                v.wait_ge(fold_done, 1)


def attn0(nc, d, s):
    with ExitStack() as ctx:
        sb = lambda n, sh, dt=F32: ctx.enter_context(nc.sbuf_tensor(n, sh, dt))
        sem = lambda n: ctx.enter_context(nc.semaphore("a0_" + n))
        bank = [ctx.enter_context(nc.psum_tensor(f"a0_ps{i}", [P, 512], F32)) for i in range(8)]
        wkq = sb("wkq", [P, 2, KH, D])
        bkq = sb("bkq", [P, 2, KH])
        wg = sb("wg0", [P, KH, E0])
        b2 = sb("b2_0", [E0, D])
        maskT = sb("maskT", [P, P])
        dcol = sb("dcol", [P, 2])
        iota = sb("iota0", [P, E0])
        stats = sb("a0_stats", [P, TILES, 6])
        mv = sb("a0_mv", [P, TILES, 2])
        rstd = sb("a0_rstd", [P, TILES])
        halfneg = sb("a0_halfneg", [P, TILES])
        xh = sb("a0_xh", [P, TILES, D])
        hT = sb("a0_hT", [P, KH, CH])
        kqT = sb("a0_kqT", [P, 2, KH, CH])
        vt = sb("a0_v", [P, TILES, D])
        vk = sb("a0_vk", [P, TILES, D])
        ktok = sb("a0_ktok", [P, TILES, D])
        aT = sb("a0_aT", [P, TILES, P])
        state = sb("a0_state", [P, TILES + 1, KH * D])
        logT = sb("a0_logT", [E0, CH])
        log = sb("a0_log", [P, TILES, E0])
        mx = sb("a0_mx", [P, TILES])
        pr = sb("a0_pr", [P, TILES, E0])
        z = sb("a0_z", [P, TILES])
        top = sb("a0_top", [P, TILES, 8])
        idx = sb("a0_idx", [P, TILES, 8], U32)
        idf = sb("a0_idf", [P, TILES, 8])
        cw = sb("a0_cw", [P, TILES, 2])
        eq = sb("a0_eq", [P, 2, TILES, E0])
        weC = sb("a0_we", [P, TILES, E0])
        weT = sb("a0_weT", [E0, CH])
        (loaded, w_loaded, const_set, stats_ready, rstd_ready, xhat_ready, trans_done, hT_act, hT_dve, proj_done,
         sig_done, v_ready, ktrans_done, ktok_ready, score_done, aT_ready, kv_done, state_ready, y_done,
         x1_ready, log_done, logT_ready, ltr_done, shifted, exp_done, we_ready, wetr_done, weT_ready,
         b2_done, b2_added, dve_seq, pool_seq) = (sem(x) for x in
            ("loaded", "w_loaded", "const_set", "stats_ready", "rstd_ready", "xhat_ready", "trans_done", "hT_act",
             "hT_dve", "proj_done", "sig_done", "v_ready", "ktrans_done", "ktok_ready", "score_done", "aT_ready",
             "kv_done", "state_ready", "y_done", "x1_ready", "log_done", "logT_ready", "ltr_done", "shifted",
             "exp_done", "we_ready", "wetr_done", "weT_ready", "b2_done", "b2_added", "dve_seq", "pool_seq"))
        X = s["xres"]
        small = ((wkq, d["wkq"]), (bkq, d["bkq"]), (wg, d["wg0"]), (b2, d["b2_0"]), (maskT, d["maskT"]), (dcol, d["dcol"]),
                 (iota, d["iota"]), (s["ident"], d["ident"]))
        with nc.Block() as block:
            @block.sync
            def _(sp):
                for dst, src in small:
                    sp.dma_start(dst[:], src).then_inc(loaded, 16)
                for c in range(NC):
                    sp.dma_start(X[:, c], d["x"][c * CH:(c + 1) * CH, :].rearrange("(t p) n -> p t n", p=P)).then_inc(loaded, 16)
                for dst, src in ((s["w1"], d["w1"]), (s["w2"], d["w2"]), (s["b1"], d["b1"])):
                    sp.dma_start(dst[:], src).then_inc(w_loaded, 16)

            @block.gpsimd
            def _(g):
                g.memset(halfneg[:], -0.5).then_inc(const_set, 1)
                g.memset(state[:, TILES, :], 0.0).then_inc(const_set, 1)
                g.wait_ge(const_set, 2)
                g.wait_ge(w_loaded, 48)
                g.wait_ge(loaded, 16 * (len(small) + NC))
                nc.gpsimd.tensor_tensor(b2[:], b2[:], s["gates"][0:E0, 1, :], ALU.mult).then_inc(const_set, 1)
                with g.Fori(0, NC) as c:
                    for half in range(2):
                        seq = Tally(c * 2 + half)
                        wait_first(g, stats_ready, c * 2 + half + 1)
                        nc.gpsimd.tensor_scalar(rstd[:], mv[:, :, 1], 1e-5, None, ALU.add).then_inc(pool_seq, 1)
                        wait_first(g, pool_seq, seq.up())
                        nc.gpsimd.tensor_tensor(rstd[:], rstd[:], halfneg[:], ALU.pow).then_inc(rstd_ready, 1)
                    wait_first(g, rstd_ready, c * 2 + 2)
                    nc.gpsimd.tensor_tensor(s["w2"][:, c], s["w2"][:, c], s["gates"][:, 1:2, :].to_broadcast([P, H0 // P, D]), ALU.mult)

            @block.tensor
            def _(pe):
                pe.wait_ge(loaded, 16 * (len(small) + NC))

                def transposes(c, k, b):
                    pe.wait_ge(xhat_ready, c * 2 + k + 1)
                    for h in range(KH):
                        for t in range(TILES):
                            last = nc.tensor.transpose(bank[b + h][:, t * P:(t + 1) * P], xh[:, t, h * P:(h + 1) * P], s["ident"][:])
                        last.then_inc(trans_done, 1)

                with pe.Fori(0, NC) as c:
                    pe.wait_ge(b2_added, c * 2 + PRIMED)
                    transposes(c, 0, 0)
                    pe.wait_ge(hT_act, c * 2 + 1)
                    pe.wait_ge(hT_dve, c * 2 + 1)
                    for w in range(2):
                        for h in range(KH):
                            for k in range(KH):
                                last = nc.tensor.matmul(bank[2 + 2 * w + h][:], wkq[:, w, k, h * P:(h + 1) * P], hT[:, k, :],
                                                        start=k == 0, stop=k == KH - 1)
                            last.then_inc(proj_done, 1)
                    for p in range(2):
                        for t in (2 * p, 2 * p + 1):
                            for k in range(KH):
                                last = nc.tensor.matmul(bank[6 + p][:, (t % 2) * D:(t % 2 + 1) * D], hT[:, k, t * P:(t + 1) * P],
                                                        s["wv0"][:, k, :], start=k == 0, stop=k == KH - 1)
                        last.then_inc(proj_done, 1)
                    pe.wait_ge(sig_done, c * 4 + 2)
                    for p in range(2):
                        for t in (2 * p, 2 * p + 1):
                            for h in range(KH):
                                last = nc.tensor.transpose(bank[p][:, (t % 2) * D + h * P:(t % 2) * D + (h + 1) * P],
                                                           kqT[:, 0, h, t * P:(t + 1) * P], s["ident"][:])
                        last.then_inc(ktrans_done, 1)
                    pe.wait_ge(sig_done, c * 4 + 4)
                    for t in range(TILES):
                        for k in range(KH):
                            last = nc.tensor.matmul(bank[2][:, t * P:(t + 1) * P], kqT[:, 0, k, t * P:(t + 1) * P],
                                                    kqT[:, 1, k, t * P:(t + 1) * P], start=k == 0, stop=k == KH - 1)
                    last.then_inc(score_done, 1)
                    pe.wait_ge(v_ready, c * 2 + 2)
                    for t in range(TILES):
                        if t % 2 == 0:
                            pe.wait_ge(ktok_ready, c * 2 + t // 2 + 1)
                        for h in range(KH):
                            last = nc.tensor.matmul(bank[3 + t][:, h * D:(h + 1) * D], ktok[:, t, h * P:(h + 1) * P], vk[:, t, :],
                                                    start=True, stop=True)
                        last.then_inc(kv_done, 1)
                    pe.wait_ge(aT_ready, c + 1)
                    for t in range(TILES):
                        y = bank[(7, 0)[t // 2]][:, (t % 2) * D:(t % 2 + 1) * D]
                        nc.tensor.matmul(y, aT[:, t, :], vt[:, t, :], start=True, stop=False)
                        pe.wait_ge(state_ready, c * 5 + t + 1)
                        for k in range(KH):
                            last = nc.tensor.matmul(y, kqT[:, 1, k, t * P:(t + 1) * P], state[:, t, k * D:(k + 1) * D],
                                                    start=False, stop=k == KH - 1)
                        if t % 2:
                            last.then_inc(y_done, 1)
                    transposes(c, 1, 3)
                    pe.wait_ge(hT_act, c * 2 + 2)
                    pe.wait_ge(hT_dve, c * 2 + 2)
                    for k in range(KH):
                        last = nc.tensor.matmul(bank[5][0:E0, :], wg[:, k, :], s["h2T"][:, c, k, :], start=k == 0, stop=k == KH - 1)
                    last.then_inc(log_done, 1)
                    wait_first(pe, logT_ready, c + 1)
                    for t in range(TILES):
                        last = nc.tensor.transpose(bank[6][:, t * E0:(t + 1) * E0], logT[:, t * P:(t + 1) * P], s["ident"][0:E0, 0:E0])
                    last.then_inc(ltr_done, 1)
                    pe.wait_ge(we_ready, c + 1)
                    for t in range(TILES):
                        last = nc.tensor.transpose(bank[1][0:E0, t * P:(t + 1) * P], weC[:, t, :], s["ident"][:])
                    last.then_inc(wetr_done, 1)
                    pe.wait_ge(weT_ready, c + 1)
                    for t in range(TILES):
                        last = nc.tensor.matmul(bank[2 + t // 2][:, (t % 2) * D:(t % 2 + 1) * D], weT[:, t * P:(t + 1) * P], b2[:],
                                                start=True, stop=True)
                        if t % 2:
                            last.then_inc(b2_done, 1)

            @block.scalar
            def _(act):
                act.wait_ge(loaded, 16 * (len(small) + NC))
                with act.Fori(0, NC) as c:
                    act.wait_ge(trans_done, c * 4 + 1)
                    nc.scalar.activation(hT[:, 0, :], bank[0][:], ACT.Identity, bias=s["modc"][:, 0:1], scale=s["modc"][:, 2:3]).then_inc(hT_act, 1)
                    for w in range(2):
                        for h in range(KH):
                            act.wait_ge(proj_done, c * 6 + 2 * w + h + 1)
                            nc.scalar.activation(kqT[:, w, h, :], bank[2 + 2 * w + h][:], ACT.Sigmoid, bias=bkq[:, w, h:h + 1]).then_inc(sig_done, 1)
                    for p in range(2):
                        act.wait_ge(ktrans_done, c * 2 + p + 1)
                        nc.scalar.activation(merged(ktok[:, 2 * p:2 * p + 2, :]), bank[p][:], ACT.Copy).then_inc(ktok_ready, 1)
                    act.wait_ge(trans_done, c * 4 + 3)
                    nc.scalar.activation(s["h2T"][:, c, 0, :], bank[3][:], ACT.Identity, bias=s["modc"][:, 4:5], scale=s["modc"][:, 6:7]).then_inc(hT_act, 1)
                    act.wait_ge(log_done, c + 1)
                    nc.scalar.activation(logT[:], bank[5][0:E0, :], ACT.Copy).then_inc(logT_ready, 1)
                    act.wait_ge(shifted, c + 1)
                    nc.scalar.activation(pr[:], log[:], ACT.Exp).then_inc(exp_done, 1)
                    act.wait_ge(wetr_done, c + 1)
                    nc.scalar.activation(weT[:], bank[1][0:E0, :], ACT.Copy).then_inc(weT_ready, 1)

            @block.vector
            def _(v):
                v.sem_inc(b2_added, PRIMED)
                v.wait_ge(loaded, 16 * (len(small) + NC))
                v.wait_ge(const_set, 3)
                v.wait_ge(w_loaded, 48)

                def normalise(c, k, seq):
                    for t in range(TILES):
                        last = nc.vector.bn_stats(stats[:, t, :], X[:, c, t, :])
                    last.then_inc(dve_seq, 1)
                    wait_first(v, dve_seq, seq.up())
                    for t in range(TILES):
                        last = nc.vector.bn_aggr(mv[:, t, :], stats[:, t, :])
                    last.then_inc(stats_ready, 1)
                    v.wait_ge(stats_ready, c * 2 + k + 1)
                    v.wait_ge(rstd_ready, c * 2 + k + 1)
                    for t in range(TILES):
                        last = nc.vector.tensor_scalar(xh[:, t, :], X[:, c, t, :], mv[:, t, 0:1], rstd[:, t:t + 1], ALU.subtract, ALU.mult)
                    last.then_inc(xhat_ready, 1)

                STEPS = 13
                with v.Fori(0, NC) as c:
                    seq = Tally(c * STEPS)
                    nc.vector.tensor_copy(state[:, 0, :], state[:, TILES, :]).then_inc(state_ready, 1)
                    normalise(c, 0, seq)
                    v.wait_ge(trans_done, c * 4 + 2)
                    nc.vector.tensor_scalar(hT[:, 1, :], bank[1][:], s["modc"][:, 3:4], s["modc"][:, 1:2], ALU.mult, ALU.add).then_inc(hT_dve, 1)
                    for p in range(2):
                        v.wait_ge(proj_done, c * 6 + 4 + p + 1)
                        nc.vector.tensor_scalar(merged(vk[:, 2 * p:2 * p + 2, :]), bank[6 + p][:], dcol[:, 1:2], None, ALU.mult)
                        nc.vector.tensor_copy(merged(vt[:, 2 * p:2 * p + 2, :]), bank[6 + p][:]).then_inc(v_ready, 1)
                    v.wait_ge(score_done, c + 1)
                    nc.vector.tensor_tensor(aT[:], bank[2][:].rearrange("p (t n) -> p t n", t=TILES),
                                            maskT[:].unsqueeze(1).to_broadcast([P, TILES, P]), ALU.mult).then_inc(aT_ready, 1)
                    for t in range(TILES):
                        v.wait_ge(kv_done, c * 4 + t + 1)
                        v.wait_ge(state_ready, c * 5 + t + 1)
                        nc.vector.scalar_tensor_tensor(state[:, t + 1, :], state[:, t, :], DECAY ** P, bank[3 + t][:],
                                                       ALU.mult, ALU.add).then_inc(state_ready, 1)
                    for p in range(2):
                        v.wait_ge(y_done, c * 2 + p + 1)
                        nc.vector.scalar_tensor_tensor(merged(X[:, c, 2 * p:2 * p + 2, :]), bank[(7, 0)[p]][:], dcol[:, 0:1],
                                                       merged(X[:, c, 2 * p:2 * p + 2, :]), ALU.mult, ALU.add).then_inc(x1_ready, 1)
                    v.wait_ge(x1_ready, c * 2 + 2)
                    wait_first(v, state_ready, c * 5 + 5)
                    normalise(c, 1, seq)
                    v.wait_ge(trans_done, c * 4 + 4)
                    nc.vector.tensor_scalar(s["h2T"][:, c, 1, :], bank[4][:], s["modc"][:, 7:8], s["modc"][:, 5:6], ALU.mult, ALU.add).then_inc(hT_dve, 1)
                    v.wait_ge(ltr_done, c + 1)
                    lg = bank[6][:, 0:TILES * E0].rearrange("p (t e) -> p t e", e=E0)
                    top_two(nc, v, lg, dict(mx=mx, log=log, pr=pr, z=z, top=top, idx=idx, idf=idf, cw=cw, eq=eq,
                                            iota=iota, out=weC, probs=pr), TILES, E0, 1e-9, dve_seq, seq, shifted, exp_done, c, we_ready)
                    v.wait_ge(we_ready, c + 1)
                    nc.vector.tensor_copy(s["we0"][:, c], weC[:]).then_inc(dve_seq, 1)
                    seq.up()
                    for p in range(2):
                        v.wait_ge(b2_done, c * 2 + p + 1)
                        nc.vector.tensor_tensor(merged(X[:, c, 2 * p:2 * p + 2, :]), merged(X[:, c, 2 * p:2 * p + 2, :]), bank[2 + p][:],
                                                ALU.add).then_inc(b2_added, 1)
                    v.wait_ge(b2_added, c * 2 + 2 + PRIMED)
                    assert seq.n == STEPS, seq.n


def top_two(nc, v, lg, b, tiles, experts, eps, dve_seq, seq, shifted, exp_done, c, ready):
    wide = lambda ap: ap.unsqueeze(2).to_broadcast([P, tiles, experts])
    nc.vector.tensor_reduce(b["mx"][:], lg, AX, ALU.max).then_inc(dve_seq, 1)
    v.wait_ge(dve_seq, seq.up())
    nc.vector.tensor_tensor(b["log"][:], lg, wide(b["mx"][:]), ALU.subtract).then_inc(shifted, 1)
    v.wait_ge(exp_done, c + 1)
    nc.vector.tensor_reduce(b["z"][:], b["pr"][:], AX, ALU.add).then_inc(dve_seq, 1)
    v.wait_ge(dve_seq, seq.up())
    nc.vector.reciprocal(b["z"][:], b["z"][:]).then_inc(dve_seq, 1)
    v.wait_ge(dve_seq, seq.up())
    nc.vector.tensor_tensor(b["probs"][:, :, 0:experts], b["pr"][:], wide(b["z"][:]), ALU.mult).then_inc(dve_seq, 1)
    wait_first(v, dve_seq, seq.up())
    for t in range(tiles):
        last = nc.vector.max(b["top"][:, t, :], b["probs"][:, t, :])
    last.then_inc(dve_seq, 1)
    wait_first(v, dve_seq, seq.up())
    for t in range(tiles):
        nc.vector.max_index(b["idx"][:, t, :], b["top"][:, t, :], b["probs"][:, t, :])
    nc.vector.tensor_tensor(b["z"][:], b["top"][:, :, 0], b["top"][:, :, 1], ALU.add).then_inc(dve_seq, 1)
    v.wait_ge(dve_seq, seq.up())
    nc.vector.tensor_copy(b["idf"][:], b["idx"][:])
    nc.vector.tensor_scalar(b["z"][:], b["z"][:], eps, None, ALU.add).then_inc(dve_seq, 1)
    v.wait_ge(dve_seq, seq.up())
    nc.vector.reciprocal(b["z"][:], b["z"][:]).then_inc(dve_seq, 1)
    v.wait_ge(dve_seq, seq.up())
    for r in range(2):
        nc.vector.tensor_tensor(b["cw"][:, :, r], b["top"][:, :, r], b["z"][:], ALU.mult)
        last = nc.vector.tensor_tensor(b["eq"][:, r], b["iota"][:, 0:experts].unsqueeze(1).to_broadcast([P, tiles, experts]),
                                       wide(b["idf"][:, :, r]), ALU.is_equal)
    last.then_inc(dve_seq, 1)
    v.wait_ge(dve_seq, seq.up())
    for r in range(2):
        last = nc.vector.tensor_tensor(b["eq"][:, r], b["eq"][:, r], wide(b["cw"][:, :, r]), ALU.mult)
    last.then_inc(dve_seq, 1)
    v.wait_ge(dve_seq, seq.up())
    nc.vector.tensor_tensor(b["out"][:], b["eq"][:, 0], b["eq"][:, 1], ALU.add).then_inc(ready, 1)


def ffn0(nc, d, s):
    HT = H0 // P
    with ExitStack() as ctx:
        sem = lambda n: ctx.enter_context(nc.semaphore("f0_" + n))
        up_ps = [ctx.enter_context(nc.psum_tensor(f"f0_up{i}", [P, CH], F32)) for i in range(4)]
        down_ps = [ctx.enter_context(nc.psum_tensor(f"f0_dn{i}", [P, 2, D], F32)) for i in range(4)]
        hid = ctx.enter_context(nc.sbuf_tensor("f0_hid", [P, 2, HT, CH], F32))
        up_done, hid_ready, down_done, added = (sem(x) for x in ("up_done", "hid_ready", "down_done", "added"))
        X = s["xres"]
        with nc.Block() as block:
            @block.tensor
            def _(pe):
                pe.sem_inc(down_done, PRIMED)
                def up(c, e):
                    for j in range(HT):
                        if e > 0:
                            pe.wait_ge(hid_ready, c * E0 * HT + (e - 1) * HT + j + 1 + PRIMED)
                        else:
                            pe.wait_ge(hid_ready, c * E0 * HT + PRIMED)
                        for k in range(KH):
                            last = nc.tensor.matmul(up_ps[j][:], s["w1"][:, e, k, j * P:(j + 1) * P], s["h2T"][:, c, k, :],
                                                    start=k == 0, stop=k == KH - 1)
                        last.then_inc(up_done, 1)

                def down(c, e):
                    pe.wait_ge(hid_ready, c * E0 * HT + (e + 1) * HT + PRIMED)
                    for p in range(2):
                        if e >= 2:
                            pe.wait_ge(added, c * E0 * 2 + (e - 2) * 2 + p + 1 + PRIMED)
                        else:
                            pe.wait_ge(added, c * E0 * 2 + PRIMED)
                        for t in (2 * p, 2 * p + 1):
                            for k in range(HT):
                                last = nc.tensor.matmul(down_ps[2 * (e % 2) + p][:, t % 2, :], hid[:, e % 2, k, t * P:(t + 1) * P],
                                                        s["w2"][:, e, k, :], start=k == 0, stop=k == HT - 1)
                        last.then_inc(down_done, 1)

                with pe.Fori(0, NC) as c:
                    up(c, 0)
                    for e in range(E0):
                        if e + 1 < E0:
                            up(c, e + 1)
                        down(c, e)

            @block.scalar
            def _(act):
                act.sem_inc(hid_ready, PRIMED)
                with act.Fori(0, NC) as c:
                    for e in range(E0):
                        act.wait_ge(down_done, c * E0 * 2 + max(0, (e - 1) * 2) + PRIMED)
                        for j in range(HT):
                            act.wait_ge(up_done, c * E0 * HT + e * HT + j + 1)
                            nc.scalar.activation(hid[:, e % 2, j, :], up_ps[j][:], ACT.Relu, bias=s["b1"][:, e, j:j + 1]).then_inc(hid_ready, 1)

            @block.vector
            def _(v):
                v.sem_inc(added, PRIMED)
                with v.Fori(0, NC) as c:
                    for e in range(E0):
                        for p in range(2):
                            v.wait_ge(down_done, c * E0 * 2 + e * 2 + p + 1 + PRIMED)
                            v.wait_ge(added, c * E0 * 2 + max(0, e * 2 + p - 1) + PRIMED)
                            for t in (2 * p, 2 * p + 1):
                                last = nc.vector.scalar_tensor_tensor(X[:, c, t, :], down_ps[2 * (e % 2) + p][:, t % 2, :],
                                                                      s["we0"][:, c, t, e:e + 1], X[:, c, t, :], ALU.mult, ALU.add)
                            last.then_inc(added, 1)

def lin_keys(nc, d, s):
    with ExitStack() as ctx:
        sb = lambda n, sh, dt=F32: ctx.enter_context(nc.sbuf_tensor("lk_" + n, sh, dt))
        sem = lambda n: ctx.enter_context(nc.semaphore("lk_" + n))
        bank = [ctx.enter_context(nc.psum_tensor(f"lk_ps{i}", [P, 512], F32)) for i in range(8)]
        wkv = sb("wkv", [P, KH, 2 * D])
        wq = sb("wq", [P, KH, D])
        same_head = sb("same_head", [P, P])
        stats = sb("stats", [P, TILES, 6])
        mv = sb("mv", [P, TILES, 2])
        rstd = sb("rstd", [P, TILES])
        halfneg = sb("halfneg", [P, TILES])
        zero = sb("zero", [P, P])
        xh = sb("xh", [P, TILES, D])
        hT = sb("hT", [P, KH, CH])
        kneg = sb("kneg", [P, TILES, D])
        kf = sb("kf", [P, TILES, D])
        vt = sb("vt", [P, TILES, KH, P + 1])
        qneg = sb("qneg", [P, KH, CH])
        (loaded, const_set, stats_ready, rstd_ready, xhat_ready, trans_done, hT_act, hT_dve, kv_proj, q_proj, neg_ready,
         exp_ready, v_ready, kf_ready, qf_ready, sum_done, dve_seq, pool_seq) = (sem(x) for x in
            ("loaded", "const_set", "stats_ready", "rstd_ready", "xhat_ready", "trans_done", "hT_act", "hT_dve", "kv_proj",
             "q_proj", "neg_ready", "exp_ready", "v_ready", "kf_ready", "qf_ready", "sum_done", "dve_seq", "pool_seq"))
        X = s["xres"]
        with nc.Block() as block:
            @block.sync
            def _(sp):
                for dst, src in ((wkv, d["wkv1"]), (wq, d["wq1"]), (same_head, d["same_head"])):
                    sp.dma_start(dst[:], src).then_inc(loaded, 16)

            @block.gpsimd
            def _(g):
                g.memset(halfneg[:], -0.5).then_inc(const_set, 1)
                g.memset(zero[:], 0.0).then_inc(const_set, 1)
                g.memset(vt[:], 1.0).then_inc(const_set, 1)
                g.wait_ge(const_set, 3)
                with g.Fori(0, NC) as c:
                    wait_first(g, stats_ready, c + 1)
                    nc.gpsimd.tensor_scalar(rstd[:], mv[:, :, 1], 1e-5, None, ALU.add).then_inc(pool_seq, 1)
                    wait_first(g, pool_seq, c + 1)
                    nc.gpsimd.tensor_tensor(rstd[:], rstd[:], halfneg[:], ALU.pow).then_inc(rstd_ready, 1)

            @block.tensor
            def _(pe):
                pe.sem_inc(sum_done, PRIMED)
                pe.wait_ge(loaded, 48)
                pe.wait_ge(const_set, 3)
                for h in range(KH):
                    nc.tensor.matmul(bank[6 + h][:, 0:P], zero[:], zero[:], start=True, stop=False, skip_group_check=True)
                    nc.tensor.matmul(bank[6 + h][:, P:P + 1], zero[:], zero[:, 0:1], start=False, stop=False, skip_group_check=True)
                with pe.Fori(0, NC) as c:
                    pe.wait_ge(xhat_ready, c + 1)
                    pe.wait_ge(qf_ready, c * 2 + PRIMED)
                    for h in range(KH):
                        for t in range(TILES):
                            last = nc.tensor.transpose(bank[h][:, t * P:(t + 1) * P], xh[:, t, h * P:(h + 1) * P], s["ident"][:])
                        last.then_inc(trans_done, 1)
                    pe.wait_ge(hT_act, c + 1)
                    pe.wait_ge(hT_dve, c + 1)
                    for t in range(TILES):
                        pe.wait_ge(kf_ready, c * 4 + PRIMED)
                        for k in range(KH):
                            last = nc.tensor.matmul(bank[2 + t][:], hT[:, k, t * P:(t + 1) * P], wkv[:, k, :], start=k == 0, stop=k == KH - 1)
                        last.then_inc(kv_proj, 1)
                    for h in range(KH):
                        for k in range(KH):
                            last = nc.tensor.matmul(bank[h][:], wq[:, k, h * P:(h + 1) * P], hT[:, k, :], start=k == 0, stop=k == KH - 1)
                        last.then_inc(q_proj, 1)
                    for t in range(TILES):
                        pe.wait_ge(kf_ready, c * 4 + t + 1 + PRIMED)
                        pe.wait_ge(v_ready, c * 4 + t + 1)
                        for h in range(KH):
                            last = nc.tensor.matmul(bank[6 + h][:, 0:P + 1], kf[:, t, h * P:(h + 1) * P], vt[:, t, h, :],
                                                    start=False, stop=True, skip_group_check=True)
                    last.then_inc(sum_done, 1)

            @block.scalar
            def _(act):
                with act.Fori(0, NC) as c:
                    act.wait_ge(trans_done, c * 2 + 1)
                    nc.scalar.activation(hT[:, 0, :], bank[0][:], ACT.Identity, bias=s["modc"][:, 8:9], scale=s["modc"][:, 10:11]).then_inc(hT_act, 1)
                    for t in range(TILES):
                        act.wait_ge(kv_proj, c * 4 + t + 1)
                        act.wait_ge(sum_done, c + PRIMED)
                        act.wait_ge(neg_ready, c * 6 + t + 1)
                        nc.scalar.activation(vt[:, t, :, 0:P], bank[2 + t][:, D:2 * D].rearrange("p (h n) -> p h n", h=KH), ACT.Copy).then_inc(v_ready, 1)
                        nc.scalar.activation(kneg[:, t, :], kneg[:, t, :], ACT.Exp).then_inc(exp_ready, 1)
                    for h in range(KH):
                        act.wait_ge(neg_ready, c * 6 + 4 + h + 1)
                        nc.scalar.activation(qneg[:, h, :], qneg[:, h, :], ACT.Exp).then_inc(exp_ready, 1)

            @block.vector
            def _(v):
                v.sem_inc(qf_ready, PRIMED)
                v.sem_inc(kf_ready, PRIMED)
                with v.Fori(0, NC) as c:
                    for t in range(TILES):
                        last = nc.vector.bn_stats(stats[:, t, :], X[:, c, t, :])
                    last.then_inc(dve_seq, 1)
                    wait_first(v, dve_seq, c + 1)
                    for t in range(TILES):
                        last = nc.vector.bn_aggr(mv[:, t, :], stats[:, t, :])
                    last.then_inc(stats_ready, 1)
                    v.wait_ge(stats_ready, c + 1)
                    v.wait_ge(rstd_ready, c + 1)
                    for t in range(TILES):
                        last = nc.vector.tensor_scalar(xh[:, t, :], X[:, c, t, :], mv[:, t, 0:1], rstd[:, t:t + 1], ALU.subtract, ALU.mult)
                    last.then_inc(xhat_ready, 1)
                    v.wait_ge(trans_done, c * 2 + 2)
                    nc.vector.tensor_scalar(hT[:, 1, :], bank[1][:], s["modc"][:, 11:12], s["modc"][:, 9:10], ALU.mult, ALU.add).then_inc(hT_dve, 1)
                    for t in range(TILES):
                        v.wait_ge(kv_proj, c * 4 + t + 1)
                        v.wait_ge(kf_ready, c * 4 + PRIMED)
                        nc.vector.tensor_scalar(kneg[:, t, :], bank[2 + t][:, 0:D], 0.0, None, ALU.min).then_inc(neg_ready, 1)
                    for h in range(KH):
                        v.wait_ge(q_proj, c * 2 + h + 1)
                        nc.vector.tensor_scalar(qneg[:, h, :], bank[h][:], 0.0, None, ALU.min).then_inc(neg_ready, 1)
                    v.wait_ge(sum_done, c + PRIMED)
                    for t in range(TILES):
                        v.wait_ge(exp_ready, c * 6 + t + 1)
                        v.wait_ge(v_ready, c * 4 + t + 1)
                        nc.vector.scalar_tensor_tensor(kf[:, t, :], bank[2 + t][:, 0:D], 0.0, kneg[:, t, :], ALU.max, ALU.add).then_inc(kf_ready, 1)
                    for h in range(KH):
                        v.wait_ge(exp_ready, c * 6 + 4 + h + 1)
                        nc.vector.scalar_tensor_tensor(s["qfT"][:, c, h, :], bank[h][:], 0.0, qneg[:, h, :], ALU.max, ALU.add).then_inc(qf_ready, 1)
                v.wait_ge(sum_done, NC + PRIMED)
                for h in range(KH):
                    nc.vector.tensor_tensor(s["kvb"][:, h, :], bank[6 + h][:, 0:P], same_head[:], ALU.mult)
                    nc.vector.tensor_scalar(s["ksb"][:, h, :], same_head[:], bank[6 + h][:, P:P + 1], None, ALU.mult)


def lin_out(nc, d, s):
    with ExitStack() as ctx:
        sb = lambda n, sh, dt=F32: ctx.enter_context(nc.sbuf_tensor("lo_" + n, sh, dt))
        sem = lambda n: ctx.enter_context(nc.semaphore("lo_" + n))
        bank = [ctx.enter_context(nc.psum_tensor(f"lo_ps{i}", [P, 512], F32)) for i in range(8)]
        wqkv = sb("wqkv", [P, KH, 3 * D])
        qkw2 = sb("qkw2", [P, 2, HD])
        qkw = sb("qkw", [P, HD])
        nw = sb("nw", [P, 2, KH])
        stats = sb("stats", [P, TILES, 6])
        mv = sb("mv", [P, TILES, 2])
        rstd = sb("rstd", [P, TILES])
        ssq = sb("ssq", [P, TILES])
        rms = sb("rms", [P, TILES])
        halfneg = sb("halfneg", [P, TILES * 2 * HEADS])
        den = sb("den", [P, KH, CH])
        oT = sb("oT", [P, KH, CH])
        xh = sb("xh", [P, TILES, D])
        hT = den
        sq = oT[:].rearrange("p a b -> p (a b)").rearrange("p (a b) -> p a b", b=D)
        headsq = sb("headsq", [P, TILES, 2 * HEADS])
        headr = sb("headr", [P, TILES, 2 * HEADS])
        kn2 = sb("kn2", [P, HEADS])
        kq2 = sb("kq2", [P, TILES, HEADS])
        kmax = sb("kmax", [P, HEADS])
        (loaded, const_set, bo_added, num_done, den_ready, oT_ready, out_done, x3_ready, x3_stored, stats_ready, rstd_ready,
         h4_ready, ssq_ready, rms_ready, xhat_ready, trans_done, hT_act, hT_dve, qk_proj, v_proj, v_ready, sq_ready, headsq_ready,
         headr_ready, qk_ready, q_weighed, dve_seq, pool_seq, square_done, x4_ready) = (sem(x) for x in
            ("loaded", "const_set", "bo_added", "num_done", "den_ready", "oT_ready", "out_done", "x3_ready", "x3_stored",
             "stats_ready", "rstd_ready", "h4_ready", "ssq_ready", "rms_ready", "xhat_ready", "trans_done", "hT_act", "hT_dve",
             "qk_proj", "v_proj", "v_ready", "sq_ready", "headsq_ready", "headr_ready", "qk_ready", "q_weighed", "dve_seq",
             "pool_seq", "square_done", "x4_ready"))
        X = s["xres"]
        with nc.Block() as block:
            @block.sync
            def _(sp):
                for dst, src in ((wqkv, d["wqkv"]), (qkw2, d["qkw"]), (nw, d["nw"])):
                    sp.dma_start(dst[:], src).then_inc(loaded, 16)
                x3 = d["x3"].rearrange("(c t p) n -> c p t n", t=TILES, p=P)
                with sp.Fori(0, NC) as c:
                    sp.wait_ge(x3_ready, c * 2 + 2)
                    sp.dma_start(x3[c], X[:, c]).then_inc(x3_stored, 16)

            @block.gpsimd
            def _(g):
                g.memset(halfneg[:], -0.5).then_inc(const_set, 1)
                g.memset(s["vx"][:].rearrange("p c t n -> p (c t) n").rearrange("p a (h n) -> p a h n", h=HEADS)[:, :, :, HD], 1.0).then_inc(const_set, 1)
                g.memset(kn2[:], 0.0).then_inc(const_set, 1)
                g.wait_ge(loaded, 48)
                nc.gpsimd.tensor_tensor(qkw[:], qkw2[:, 0, :], qkw2[:, 1, :], ALU.mult).then_inc(const_set, 1)
                g.wait_ge(const_set, 4)
                nc.gpsimd.tensor_scalar(qkw[:], qkw[:], HD ** -0.5, None, ALU.mult).then_inc(const_set, 1)
                g.wait_ge(const_set, 5)
                with g.Fori(0, NC) as c:
                    seq = Tally(c * 3)
                    nc.gpsimd.tensor_tensor(X[:, c], X[:, c], s["bo1"][:].unsqueeze(1).to_broadcast([P, TILES, D]), ALU.add).then_inc(bo_added, 1)
                    wait_first(g, stats_ready, c + 1)
                    nc.gpsimd.tensor_scalar(rstd[:], mv[:, :, 1], 1e-5, None, ALU.add).then_inc(pool_seq, 1)
                    wait_first(g, pool_seq, seq.up())
                    nc.gpsimd.tensor_tensor(rstd[:], rstd[:], halfneg[:, 0:TILES], ALU.pow).then_inc(rstd_ready, 1)
                    wait_first(g, ssq_ready, c + 1)
                    nc.gpsimd.tensor_scalar(rms[:], ssq[:], 1.0 / D, RMS_EPS, ALU.mult, ALU.add).then_inc(pool_seq, 1)
                    wait_first(g, pool_seq, seq.up())
                    nc.gpsimd.tensor_tensor(rms[:], rms[:], halfneg[:, 0:TILES], ALU.pow).then_inc(rms_ready, 1)
                    wait_first(g, headsq_ready, c * 4 + 4)
                    nc.gpsimd.tensor_scalar(merged(headr[:]), merged(headsq[:]), 1.0 / HD, RMS_EPS, ALU.mult, ALU.add).then_inc(pool_seq, 1)
                    wait_first(g, pool_seq, seq.up())
                    nc.gpsimd.tensor_tensor(merged(headr[:]), merged(headr[:]), halfneg[:], ALU.pow).then_inc(headr_ready, 1)
                    for t in range(TILES):
                        wait_first(g, qk_ready, c * 4 + t + 1 + PRIMED)
                        q = s["qk"][:, c, t, 0:D].rearrange("p (h n) -> p h n", h=HEADS)
                        nc.gpsimd.tensor_tensor(q, q, qkw[:].unsqueeze(1).to_broadcast([P, HEADS, HD]), ALU.mult).then_inc(q_weighed, 1)

            @block.tensor
            def _(pe):
                pe.wait_ge(loaded, 48)
                with pe.Fori(0, NC) as c:
                    pe.wait_ge(qk_ready, c * 4 + PRIMED)
                    for h in range(KH):
                        nc.tensor.matmul(bank[h][:], s["kvb"][:, h, :], s["qfT"][:, c, h, :], start=True, stop=True)
                        nc.tensor.matmul(bank[2 + h][:], s["ksb"][:, h, :], s["qfT"][:, c, h, :], start=True, stop=True).then_inc(num_done, 1)
                    pe.wait_ge(v_ready, c * 2 + PRIMED)
                    pe.wait_ge(oT_ready, c * 2 + 2)
                    for t in range(TILES):
                        for k in range(KH):
                            last = nc.tensor.matmul(bank[4 + t // 2][:, (t % 2) * D:(t % 2 + 1) * D], oT[:, k, t * P:(t + 1) * P], s["wo1"][:, k, :],
                                                    start=k == 0, stop=k == KH - 1)
                        if t % 2:
                            last.then_inc(out_done, 1)
                    pe.wait_ge(xhat_ready, c * 2 + 2)
                    for h in range(KH):
                        for t in range(TILES):
                            last = nc.tensor.transpose(bank[6 + h][:, t * P:(t + 1) * P], xh[:, t, h * P:(h + 1) * P], s["ident"][:])
                        last.then_inc(trans_done, 1)
                    pe.wait_ge(hT_act, c + 1)
                    pe.wait_ge(hT_dve, c + 1)
                    for t in range(TILES):
                        for k in range(KH):
                            last = nc.tensor.matmul(bank[t][:], hT[:, k, t * P:(t + 1) * P], wqkv[:, k, 0:2 * D], start=k == 0, stop=k == KH - 1)
                        last.then_inc(qk_proj, 1)
                    for t in range(TILES):
                        for k in range(KH):
                            last = nc.tensor.matmul(bank[4 + t // 2][:, (t % 2) * D:(t % 2 + 1) * D], hT[:, k, t * P:(t + 1) * P],
                                                    wqkv[:, k, 2 * D:3 * D], start=k == 0, stop=k == KH - 1)
                        if t % 2:
                            last.then_inc(v_proj, 1)

            @block.scalar
            def _(act):
                act.sem_inc(v_ready, PRIMED)
                act.wait_ge(const_set, 3)
                with act.Fori(0, NC) as c:
                    for h in range(KH):
                        act.wait_ge(num_done, c * 2 + h + 1)
                        nc.scalar.activation(den[:, h, :], bank[2 + h][:], ACT.Copy, bias=1e-6).then_inc(den_ready, 1)
                    act.wait_ge(h4_ready, c + 1)
                    for t in range(TILES):
                        last = nc.scalar.activation(sq[:, t, :], X[:, c, t, :], ACT.Square, accum_out=ssq[:, t:t + 1])
                    last.then_inc(ssq_ready, 1)
                    act.wait_ge(trans_done, c * 2 + 1)
                    nc.scalar.activation(hT[:, 0, :], bank[6][:], ACT.Identity, scale=nw[:, 0, 0:1]).then_inc(hT_act, 1)
                    for t in range(TILES):
                        act.wait_ge(qk_proj, c * 4 + t + 1)
                        if t >= 2:
                            act.wait_ge(headsq_ready, c * 4 + t - 1)
                        nc.scalar.activation(merged(sq[:, 2 * (t % 2):2 * (t % 2) + 2, :]), bank[t][:], ACT.Square).then_inc(square_done, 1)
                    for p in range(2):
                        act.wait_ge(v_proj, c * 2 + p + 1)
                        dst = s["vx"][:, c, 2 * p:2 * p + 2, :].rearrange("p t (h n) -> p (t h) n", h=HEADS)[:, :, 0:HD]
                        nc.scalar.activation(dst, bank[4 + p][:].rearrange("p (a n) -> p a n", n=HD), ACT.Copy).then_inc(v_ready, 1)

            @block.vector
            def _(v):
                v.sem_inc(qk_ready, PRIMED)
                v.wait_ge(const_set, 3)
                v.wait_ge(loaded, 48)
                with v.Fori(0, NC) as c:
                    seq = Tally(c * 8)
                    for h in range(KH):
                        v.wait_ge(den_ready, c * 2 + h + 1)
                        nc.vector.reciprocal(den[:, h, :], den[:, h, :]).then_inc(dve_seq, 1)
                        v.wait_ge(dve_seq, seq.up())
                        nc.vector.tensor_tensor(oT[:, h, :], bank[h][:], den[:, h, :], ALU.mult).then_inc(oT_ready, 1)
                    v.wait_ge(bo_added, c + 1)
                    for p in range(2):
                        v.wait_ge(out_done, c * 2 + p + 1)
                        nc.vector.tensor_tensor(merged(X[:, c, 2 * p:2 * p + 2, :]), merged(X[:, c, 2 * p:2 * p + 2, :]), bank[4 + p][:],
                                                ALU.add).then_inc(x3_ready, 1)
                    wait_first(v, x3_ready, c * 2 + 2)
                    for t in range(TILES):
                        last = nc.vector.bn_stats(stats[:, t, :], X[:, c, t, :])
                    last.then_inc(dve_seq, 1)
                    wait_first(v, dve_seq, seq.up())
                    for t in range(TILES):
                        last = nc.vector.bn_aggr(mv[:, t, :], stats[:, t, :])
                    last.then_inc(stats_ready, 1)
                    v.wait_ge(stats_ready, c + 1)
                    v.wait_ge(rstd_ready, c + 1)
                    for t in range(TILES):
                        last = nc.vector.tensor_scalar(xh[:, t, :], X[:, c, t, :], mv[:, t, 0:1], rstd[:, t:t + 1], ALU.subtract, ALU.mult)
                    last.then_inc(xhat_ready, 1)
                    v.wait_ge(xhat_ready, c * 2 + 1)
                    wide = lambda ap: ap.unsqueeze(1).to_broadcast([P, TILES, D])
                    nc.vector.tensor_tensor(xh[:], xh[:], wide(s["cb1"][:]), ALU.mult).then_inc(dve_seq, 1)
                    v.wait_ge(dve_seq, seq.up())
                    v.wait_ge(x3_stored, c * 16 + 16)
                    nc.vector.tensor_tensor(X[:, c], xh[:], wide(s["sb1"][:]), ALU.add).then_inc(h4_ready, 1)
                    v.wait_ge(h4_ready, c + 1)
                    v.wait_ge(rms_ready, c + 1)
                    for t in range(TILES):
                        last = nc.vector.tensor_scalar(xh[:, t, :], X[:, c, t, :], rms[:, t:t + 1], None, ALU.mult)
                    last.then_inc(xhat_ready, 1)
                    v.wait_ge(trans_done, c * 2 + 2)
                    nc.vector.tensor_scalar(hT[:, 1, :], bank[7][:], nw[:, 0, 1:2], None, ALU.mult).then_inc(hT_dve, 1)
                    for t in range(TILES):
                        v.wait_ge(square_done, c * 4 + t + 1)
                        nc.vector.tensor_reduce(headsq[:, t, :], merged(sq[:, 2 * (t % 2):2 * (t % 2) + 2, :]).rearrange("p (h n) -> p h n", n=HD),
                                                AX, ALU.add).then_inc(headsq_ready, 1)
                    v.wait_ge(headr_ready, c + 1)
                    for t in range(TILES):
                        nc.vector.tensor_tensor(s["qk"][:, c, t, :].rearrange("p (h n) -> p h n", n=HD), bank[t][:].rearrange("p (h n) -> p h n", n=HD),
                                                headr[:, t, :].unsqueeze(2).to_broadcast([P, 2 * HEADS, HD]), ALU.mult).then_inc(qk_ready, 1)
                    nc.vector.tensor_tensor(kq2[:], headsq[:, :, HEADS:], headr[:, :, HEADS:], ALU.mult).then_inc(dve_seq, 1)
                    v.wait_ge(dve_seq, seq.up())
                    nc.vector.tensor_tensor(kq2[:], kq2[:], headr[:, :, HEADS:], ALU.mult).then_inc(dve_seq, 1)
                    v.wait_ge(dve_seq, seq.up())
                    nc.vector.tensor_reduce(kmax[:], kq2[:].rearrange("p t h -> p h t"), AX, ALU.max).then_inc(dve_seq, 1)
                    v.wait_ge(dve_seq, seq.up())
                    nc.vector.tensor_tensor(kn2[:], kn2[:], kmax[:], ALU.max).then_inc(dve_seq, 1)
                    v.wait_ge(dve_seq, seq.up())
                    assert seq.n == 8, seq.n
                nc.vector.tensor_copy(s["knorm"][:], kn2[:])


RMS_EPS = 1.1920929e-07


def shifts(nc, d, s):
    TT = NC * TILES
    with ExitStack() as ctx:
        sb = lambda n, sh, dt=F32: ctx.enter_context(nc.sbuf_tensor("sh_" + n, sh, dt))
        sem = lambda n: ctx.enter_context(nc.semaphore("sh_" + n))
        ps = [ctx.enter_context(nc.psum_tensor(f"sh_ps{i}", [P, 512], F32)) for i in range(2)]
        prod = sb("prod", [P, 2, TILES, D])
        own = sb("own", [P, NC, TILES, HEADS])
        qn2 = sb("qn2", [P, NC, TILES, HEADS])
        km = sb("km", [HEADS, 1])
        kdiag = sb("kdiag", [HEADS, HEADS])
        ones = sb("ones", [HEADS, P])
        ones_set, km_t, kdiag_ready, km_all, upper2, upper, seq, done = (sem(x) for x in
            ("ones_set", "km_t", "kdiag_ready", "km_all", "upper2", "upper", "seq", "done"))
        prod_ready = sem("prod_ready")
        with nc.Block() as block:
            @block.gpsimd
            def _(g):
                g.memset(ones[:], 1.0).then_inc(ones_set, 1)

            @block.tensor
            def _(pe):
                nc.tensor.transpose(ps[0][0:HEADS, 0:P], s["knorm"][:], s["ident"][:]).then_inc(km_t, 1)
                pe.wait_ge(kdiag_ready, 1)
                pe.wait_ge(ones_set, 1)
                nc.tensor.matmul(ps[1][:, 0:HEADS], ones[:], kdiag[:], start=True, stop=True).then_inc(km_all, 1)

            @block.scalar
            def _(act):
                act.wait_ge(upper2, 1)
                nc.scalar.activation(qn2[:], qn2[:], ACT.Sqrt).then_inc(upper, 1)

            @block.vector
            def _(v):
                v.sem_inc(done, PRIMED)
                v.wait_ge(km_t, 1)
                nc.vector.tensor_reduce(km[:], ps[0][0:HEADS, 0:P], AX, ALU.max).then_inc(seq, 1)
                v.wait_ge(seq, 1)
                nc.vector.tensor_scalar(kdiag[:], s["ident"][0:HEADS, 0:HEADS], km[:], None, ALU.mult).then_inc(kdiag_ready, 1)
                by_head = lambda ap: ap.rearrange("p t (h n) -> p (t h) n", n=HD)
                with v.Fori(0, NC) as c:
                    v.wait_ge(done, c * 2 + PRIMED)
                    for i in range(2):
                        nc.vector.tensor_tensor(prod[:, i], s["qk"][:, c, :, 0:D], s["qk"][:, c, :, (1 - i) * D:(2 - i) * D], ALU.mult).then_inc(prod_ready, 1)
                    for i, dst in enumerate((own, qn2)):
                        v.wait_ge(prod_ready, c * 2 + i + 1)
                        nc.vector.tensor_reduce(merged(dst[:, c]), by_head(prod[:, i]), AX, ALU.add).then_inc(done, 1)
                v.wait_ge(done, NC * 2 + PRIMED)
                v.wait_ge(km_all, 1)
                every = lambda t: t[:].rearrange("p c t h -> p (c t) h")
                nc.vector.tensor_tensor(every(qn2), every(qn2), ps[1][:, 0:HEADS].unsqueeze(1).to_broadcast([P, TT, HEADS]), ALU.mult).then_inc(upper2, 1)
                nc.vector.tensor_scalar(own[:], own[:], -1.0, None, ALU.mult).then_inc(seq, 1)
                v.wait_ge(upper, 1)
                nc.vector.tensor_scalar(qn2[:], qn2[:], -1.0, 80.0, ALU.mult, ALU.add).then_inc(seq, 1)
                v.wait_ge(seq, 3)
                nc.vector.tensor_tensor(own[:], own[:], qn2[:], ALU.min).then_inc(seq, 1)
                v.wait_ge(seq, 4)
                sh = s["shift"][:].rearrange("p c t h k -> p (c t h) k")
                flat = lambda t: t[:].rearrange("p c t h -> p (c t h)")
                nc.vector.tensor_copy(sh[:, :, 0], flat(own)).then_inc(seq, 1)
                v.wait_ge(seq, 5)
                nc.vector.tensor_tensor(flat(own), flat(own), sh[:, :, 0], ALU.subtract).then_inc(seq, 1)
                v.wait_ge(seq, 6)
                nc.vector.tensor_copy(sh[:, :, 1], flat(own)).then_inc(seq, 1)
                v.wait_ge(seq, 7)
                nc.vector.tensor_tensor(sh[:, :, 2], flat(own), sh[:, :, 1], ALU.subtract)


def softmax(nc, d, s):
    PER_G = sum(TILES * (c + 1) for c in range(NC))
    before = lambda c: 2 * c * (c + 1)
    assert before(NC) == PER_G
    VW = HD + 1
    order = [("Q0", 0), ("Q1", 0), ("K0", 0), ("K1", 0)]
    for c in range(NC):
        order += [("D", c - 1)] if c else []
        order += [("Q0", c + 1), ("Q1", c + 1), ("K0", c + 1), ("K1", c + 1)] if c + 1 < NC else []
        order += [("A0", c - 1), ("A1", c - 1)] if c else []
    order += [("D", NC - 1), ("A0", NC - 1), ("A1", NC - 1)]
    number = {job: i for i, job in enumerate(order)}
    JOBS = len(order)
    assert JOBS % 2 == 0
    with ExitStack() as ctx:
        sb = lambda n, sh, dt=F32: ctx.enter_context(nc.sbuf_tensor("sm_" + n, sh, dt))
        sem = lambda n: ctx.enter_context(nc.semaphore("sm_" + n))
        ps_s = [ctx.enter_context(nc.psum_tensor(f"sm_s{i}", [P, 2, CH], F32)) for i in range(2)]
        ps_o = [ctx.enter_context(nc.psum_tensor(f"sm_o{i}", [P, CH], F32)) for i in range(2)]
        side = [ctx.enter_context(nc.psum_tensor(f"sm_j{i}", [P, 512], F32)) for i in range(2)]
        kst = sb("kst", [P, GH, NC, CH], BF16)
        qst = sb("qst", [P, 2, GH, CH], BF16)
        stage = [sb("stage_q", [P, TILES, GH, ROWS], BF16), sb("stage_k", [P, TILES, GH, ROWS], BF16)]
        part_h = sb("part_h", [P, TILES * GH, HD], BF16)
        part_m = sb("part_m", [P, TILES * GH, HD], BF16)
        rest = sb("rest", [P, TILES * GH, HD])
        prob = sb("prob", [P, 2, GH, CH])
        vst = sb("vst", [P, TILES, GH * VW])
        o_sb = sb("o_sb", [P, CH])
        o_n = sb("o_n", [P, CH])
        zero = sb("zero", [P, P], BF16)
        identb = sb("identb", [P, P], BF16)
        den_row = sb("den_row", [P, P])
        wo_pad = sb("wo_pad", [P, GROUPS, KEEP])
        (loaded, zero_set, const_set, split_seq, staged, side_done, side_read, s_done, exp_done, masked, v_staged, pv_done,
         o_read, on_ready, rec_ready) = (sem(x) for x in
            ("loaded", "zero_set", "const_set", "split_seq", "staged", "side_done", "side_read", "s_done", "exp_done", "masked",
             "v_staged", "pv_done", "o_read", "on_ready", "rec_ready"))
        X = s["xres"]
        qk = s["qk"][:].rearrange("p c t (w g n) -> p c t w g n", w=2, g=GROUPS)
        vx = s["vx"][:].rearrange("p c t (g n) -> p c t g n", g=GROUPS)
        with nc.Block() as block:
            @block.sync
            def _(sp):
                for dst, src in ((den_row, d["den_row"]), (wo_pad, d["wo_pad"])):
                    sp.dma_start(dst[:], src).then_inc(loaded, 16)

            @block.gpsimd
            def _(g_):
                g_.memset(zero[:], 0.0).then_inc(zero_set, 1)
                g_.memset(stage[1][:, :, :, SPLIT:ROWS], 1.0).then_inc(const_set, 1)
                with g_.Fori(0, GROUPS) as g:
                    for c in range(NC):
                        n0 = g * PER_G + before(c)

                        def stage_v(n, kc, j):
                            wait_first(g_, pv_done, (g * PER_G if c == 0 else n - 3) + PRIMED, met=zero_set)
                            nc.gpsimd.tensor_copy(vst[:, j, :], vx[:, kc, j, g, :]).then_inc(v_staged, 1)

                        if c:
                            with g_.Fori(0, c) as kc:
                                for j in range(TILES):
                                    stage_v(n0 + kc * TILES + j, kc, j)
                        for j in range(TILES):
                            stage_v(n0 + c * TILES + j, c, j)
                        for j in range(TILES):
                            n = n0 + c * TILES + j
                            wait_first(g_, exp_done, n * 2 + 2 + PRIMED)
                            blk = prob[:, j % 2, :, j * P:(j + 1) * P]
                            nc.gpsimd.affine_select(out=blk, in_=blk, compare_op=ALU.is_ge, fill=0.0, base=0,
                                                    pattern=[[0, GH], [1, P]], channel_multiplier=-1).then_inc(masked, 1)

            @block.tensor
            def _(pe):
                pe.sem_inc(pv_done, PRIMED)
                pe.sem_inc(side_done, PRIMED)
                pe.wait_ge(loaded, 32)
                pe.wait_ge(zero_set, 1)
                pe.wait_ge(const_set, 2)

                with pe.Fori(0, GROUPS) as g:
                    def side_job(kind, c):
                        i = number[kind, c]
                        b = side[i % 2]
                        pe.wait_ge(side_read, g * JOBS + max(i - 1, 0) + PRIMED)
                        if kind in ("Q0", "Q1", "K0", "K1"):
                            w, p = "QK".index(kind[0]), int(kind[1])
                            pe.wait_ge(staged, (g * NC + c) * 2 + w + 1)
                            for t in range(2):
                                for h in range(GH):
                                    m = (t * GH + h) * P
                                    last = nc.tensor.transpose(b[:].bitcast(BF16)[0:ROWS, m:m + P], stage[w][:, 2 * p + t, h, 0:ROWS], identb[:])
                        elif kind == "D":
                            pe.wait_ge(o_read, g * NC + c + 1 + PRIMED)
                            last = nc.tensor.matmul(b[:], den_row[:], o_sb[:], start=True, stop=True)
                        else:
                            pe.wait_ge(on_ready, g * NC + c + 1 + PRIMED)
                            for t in range(2):
                                col = (2 * int(kind[1]) + t) * P
                                last = nc.tensor.matmul(b[:, t * KEEP:(t + 1) * KEEP], o_n[:, col:col + P], wo_pad[:, g, :], start=True, stop=True)
                        last.then_inc(side_done, 1)

                    def scores(n, c, kc, j, q0, first=False):
                        for pair in range(2):
                            pe.wait_ge(exp_done, (n * 2 if first else n * 2 - 1 + pair) + PRIMED)
                            for h in range(2):
                                hh = 2 * pair + h
                                last = nc.tensor.matmul(ps_s[pair][:, h, q0:], kst[0:ROWS, hh, kc, j * P:(j + 1) * P],
                                                        qst[0:ROWS, c % 2, hh, q0:], start=True, stop=True)
                            last.then_inc(s_done, 1)

                    def values(n, c, j, q0, diagonal=False):
                        pe.wait_ge(exp_done, n * 2 + 2 + PRIMED)
                        pe.wait_ge(v_staged, n + 1)
                        if diagonal:
                            pe.wait_ge(masked, (g * NC + c) * TILES + j + 1)
                        for h in range(GH):
                            last = nc.tensor.matmul(ps_o[c % 2][32 * h:32 * h + VW, q0:], vst[:, j, h * VW:(h + 1) * VW],
                                                    prob[:, j % 2, h, q0:], start=False, stop=True, skip_group_check=True)
                        last.then_inc(pv_done, 1)

                    for job in order[:4]:
                        side_job(*job)
                    for c in range(NC):
                        n0 = g * PER_G + before(c)
                        pe.wait_ge(o_read, g * NC + max(c - 1, 0) + PRIMED)
                        nc.tensor.matmul(ps_o[c % 2][:].rearrange("p (t n) -> p t n", t=TILES), zero[:], zero[:].unsqueeze(1).to_broadcast([P, TILES, P]), start=True, stop=False, skip_group_check=True)
                        if c == 0:
                            pe.wait_ge(side_read, g * JOBS + 4 + PRIMED)
                            scores(n0, 0, 0, 0, 0, first=True)
                        if c:
                            with pe.Fori(0, c) as kc:
                                for j in range(TILES):
                                    n = n0 + kc * TILES + j
                                    scores(n + 1, c, kc if j < 3 else kc + 1, (j + 1) % TILES, 0)
                                    values(n, c, j, 0)
                        for j in range(TILES):
                            n = n0 + c * TILES + j
                            if j < 3:
                                scores(n + 1, c, c, j + 1, (j + 1) * P)
                            elif c + 1 < NC:
                                pe.wait_ge(side_read, g * JOBS + number["K1", c + 1] + 1 + PRIMED)
                                scores(n + 1, c + 1, 0, 0, 0)
                            values(n, c, j, j * P, diagonal=True)
                            if j == 0:
                                if c:
                                    side_job("D", c - 1)
                                if c + 1 < NC:
                                    side_job("Q0", c + 1)
                                    side_job("Q1", c + 1)
                            if j == 1:
                                if c + 1 < NC:
                                    side_job("K0", c + 1)
                                    side_job("K1", c + 1)
                                if c:
                                    side_job("A0", c - 1)
                                    side_job("A1", c - 1)
                    for job in order[-3:]:
                        side_job(*job)

            @block.scalar
            def _(act):
                act.sem_inc(exp_done, PRIMED)
                with act.Fori(0, GROUPS) as g:
                    for c in range(NC):
                        n0 = g * PER_G + before(c)

                        def exps(n, j, q0, wait_pv=True):
                            for pair in range(2):
                                act.wait_ge(s_done, n * 2 + pair + 1)
                                if pair == 0:
                                    act.wait_ge(pv_done, (n - 1 if wait_pv else g * PER_G) + PRIMED)
                                nc.scalar.activation(prob[:, j % 2, 2 * pair:2 * pair + 2, q0:], ps_s[pair][:, :, q0:], ACT.Exp).then_inc(exp_done, 1)

                        if c:
                            with act.Fori(0, c) as kc:
                                for j in range(TILES):
                                    exps(n0 + kc * TILES + j, j, 0)
                        for j in range(TILES):
                            exps(n0 + c * TILES + j, j, j * P, wait_pv=c > 0 or j > 0)

            @block.vector
            def _(v):
                v.sem_inc(side_read, PRIMED)
                v.sem_inc(o_read, PRIMED)
                v.sem_inc(on_ready, PRIMED)
                nc.vector.tensor_copy(identb[:], s["ident"][:]).then_inc(const_set, 1)
                with v.Fori(0, GROUPS) as g:
                    seq = Tally(g * NC * 6)

                    def split(w, c):
                        src = qk[:, c, :, w, g, :]
                        slots = stage[w][:, :, :, 0:SPLIT].rearrange("p t h (k n) -> p (t h) k n", n=HD)
                        small = lambda t: t[:].rearrange("p (t h) n -> p t (h n)", t=TILES)
                        copies = lambda t, k: t[:].unsqueeze(2).to_broadcast([P, TILES * GH, k, HD])
                        nc.vector.tensor_copy(small(part_h), src).then_inc(split_seq, 1)
                        v.wait_ge(split_seq, seq.up())
                        nc.vector.tensor_tensor(small(rest), src, small(part_h), ALU.subtract).then_inc(split_seq, 1)
                        v.wait_ge(split_seq, seq.up())
                        nc.vector.tensor_copy(part_m[:], rest[:]).then_inc(split_seq, 1)
                        v.wait_ge(split_seq, seq.up())
                        if c:
                            v.wait_ge(side_done, g * JOBS + number["QK"[w] + "1", c - 1] + 1 + PRIMED)
                        else:
                            v.wait_ge(side_done, g * JOBS + PRIMED)
                        if w == 0:
                            nc.vector.tensor_copy(slots[:, :, 1:4, :], copies(part_h, 3))
                            nc.vector.tensor_copy(slots[:, :, 0:5:4, :], copies(part_m, 2))
                            nc.vector.tensor_copy(stage[0][:, :, :, SPLIT:ROWS], s["shift"][:, c, :, :, :].rearrange("p t (g h) k -> p g t h k", g=GROUPS)[:, g])
                        else:
                            nc.vector.tensor_copy(slots[:, :, 3:6, :], copies(part_h, 3))
                            nc.vector.tensor_copy(slots[:, :, 0:2, :], copies(part_m, 2))
                        nc.vector.tensor_tensor(slots[:, :, 5 if w == 0 else 2, :], rest[:], part_m[:], ALU.subtract).then_inc(staged, 1)
                        v.wait_ge(staged, (g * NC + c) * 2 + w + 1)

                    def read_side(kind, c):
                        i = number[kind, c]
                        b = side[i % 2]
                        v.wait_ge(side_done, g * JOBS + i + 1 + PRIMED)
                        p = int(kind[1:] or 0)
                        if kind[0] in "QK":
                            src = b[:].bitcast(BF16)[0:ROWS, :].rearrange("p (t h n) -> p t h n", t=2, h=GH)
                            dst = (qst[:, c % 2] if kind[0] == "Q" else kst[:, :, c]).rearrange("p h (t n) -> p t h n", t=TILES)
                            nc.vector.tensor_copy(dst[0:ROWS, 2 * p:2 * p + 2], src).then_inc(side_read, 1)
                        elif kind == "D":
                            nc.vector.reciprocal(o_n[:], b[:]).then_inc(side_read, 1)
                            v.wait_ge(side_read, g * JOBS + i + 1 + PRIMED)
                            nc.vector.tensor_tensor(o_n[:], o_n[:], o_sb[:], ALU.mult).then_inc(on_ready, 1)
                        else:
                            x = X[:, c, 2 * p:2 * p + 2, MASKED:]
                            nc.vector.tensor_tensor(x, x, b[:, 0:2 * KEEP].rearrange("p (t n) -> p t n", t=2), ALU.add).then_inc(side_read, 1)

                    def read_out(c):
                        v.wait_ge(pv_done, g * PER_G + before(c + 1) + PRIMED)
                        v.wait_ge(on_ready, g * NC + c + PRIMED)
                        nc.vector.tensor_copy(o_sb[:], ps_o[c % 2][:]).then_inc(o_read, 1)

                    split(0, 0)
                    split(1, 0)
                    for job in order[:4]:
                        read_side(*job)
                    for c in range(NC):
                        if c:
                            read_out(c - 1)
                        if c + 1 < NC:
                            split(0, c + 1)
                            split(1, c + 1)
                        for kind, cc in order:
                            if (kind in ("D", "A0", "A1") and cc == c - 1) or (kind[0] in "QK" and cc == c + 1):
                                read_side(kind, cc)
                    read_out(NC - 1)
                    for job in order[-3:]:
                        read_side(*job)
                    assert seq.n == 6 * NC


def ffn1(nc, d, s):
    HT = H1 // P
    stages = [("e2_l1", KH, HT, "hT", "gelu", "ha"), ("e0_up", KH, HT, "hT", "gelu", "hb"),
              ("e2_l2", HT, HT, "ha", "gelu", "hc"), ("down", 0, "hb"),
              ("e3_down", KH, KH, "hT", "gelu", "hz"), ("e2_l3", HT, HT, "hc", "gelu", "ha"),
              ("e3_up", KH, HT, "hz", "gelu", "hb"), ("e1_w1", KH, HT, "hT", "silu", "hs"), ("down", 2, "ha"),
              ("e1_w2", KH, HT, "hT", "times", "hc"), ("down", 3, "hb"), ("down", 1, "hc")]
    jobs, of_stage = [], {}
    for st in stages:
        if st[0] != "down":
            of_stage[st[0]] = len(jobs)
            jobs += [(st, j) for j in range(st[2])]
    by_act = [st[4] != "times" for st, _ in jobs]
    JOBS, ACTS = len(jobs), sum(by_act)
    DVES = JOBS - ACTS
    last_writer = {}
    with ExitStack() as ctx:
        sb = lambda n, sh, dt=F32: ctx.enter_context(nc.sbuf_tensor("f1_" + n, sh, dt))
        sem = lambda n: ctx.enter_context(nc.semaphore("f1_" + n))
        up_ps = [ctx.enter_context(nc.psum_tensor(f"f1_up{i}", [P, CH], F32)) for i in range(4)]
        down_ps = [ctx.enter_context(nc.psum_tensor(f"f1_dn{i}", [P, 2, KEEP], F32)) for i in range(2)]
        tp = [ctx.enter_context(nc.psum_tensor(f"f1_tp{i}", [P, CH], F32)) for i in range(2)]
        w = {n: sb("w_" + n, list(d["m_" + n].shape)) for n in UPS}
        downs = sb("downs", [P, E1, HT, KEEP])
        wg = sb("wg", [P, KH, E1])
        nw = sb("nw", [P, 2, KH])
        iota = sb("iota", [P, E0])
        halfneg = sb("halfneg", [P, TILES])
        ssq, rms, mx, z = (sb(n, [P, TILES]) for n in ("ssq", "rms", "mx", "z"))
        junk = sb("junk", [P, TILES, D])
        xh = sb("xh", [P, TILES, D])
        x3 = sb("x3", [P, TILES, D])
        buf = dict(hT=sb("hT", [P, KH, CH]), ha=sb("ha", [P, HT, CH]), hb=sb("hb", [P, HT, CH]), hc=sb("hc", [P, HT, CH]),
                   hz=sb("hz", [P, KH, CH]), hs=sb("hs", [P, HT, CH]))
        hT = buf["hT"]
        lgs, notnan, log, pr = (sb(n, [P, TILES, E1]) for n in ("lgs", "notnan", "log", "pr"))
        probs = sb("probs", [P, TILES, 8])
        top = sb("top", [P, TILES, 8])
        idx = sb("idx", [P, TILES, 8], U32)
        idf = sb("idf", [P, TILES, 8])
        cw = sb("cw", [P, TILES, 2])
        eq = sb("eq", [P, 2, TILES, E1])
        we = sb("we", [P, TILES, E1])
        (small_loaded, loaded, const_set, x3_loaded, x3_used, base_ready, ssq_ready, rms_ready, xhat_ready, trans_done, hT_act, hT_dve,
         log_done, log_copied, shifted, exp_done, we_ready, up_done, act_read, dve_read, down_done, added, stored,
         dve_seq, pool_seq) = (sem(x) for x in
            ("small_loaded", "loaded", "const_set", "x3_loaded", "x3_used", "base_ready", "ssq_ready", "rms_ready", "xhat_ready", "trans_done",
             "hT_act", "hT_dve", "log_done", "log_copied", "shifted", "exp_done", "we_ready", "up_done", "act_read", "dve_read",
             "down_done", "added", "stored", "dve_seq", "pool_seq"))
        X = s["xres"]
        small = [(wg, d["wg1"]), (nw, d["nw"]), (iota, d["iota"])]
        large = [(w[st[0]], d["m_" + st[0]]) for st in stages if st[0] != "down"] + [(downs, d["downs"])]

        def read_by(c, u):
            if by_act[u]:
                return act_read, c * ACTS + sum(by_act[:u + 1])
            return dve_read, c * DVES + u + 1 - sum(by_act[:u + 1]) + PRIMED

        with nc.Block() as block:
            @block.sync
            def _(sp):
                for dst, src in small:
                    sp.dma_start(dst[:], src).then_inc(small_loaded, 16)
                for dst, src in large:
                    sp.dma_start(dst[:], src).then_inc(loaded, 16)
                x3_d = d["x3"].rearrange("(c t p) n -> c p t n", t=TILES, p=P)
                out_d = d["out"].rearrange("(c t p) n -> c p t n", t=TILES, p=P)
                with sp.Fori(0, NC) as c:
                    sp.wait_ge(x3_used, c + PRIMED)
                    sp.dma_start(x3[:], x3_d[c]).then_inc(x3_loaded, 16)
                    sp.wait_ge(added, (c + 1) * E1 * 2 + PRIMED)
                    sp.dma_start(out_d[c], X[:, c]).then_inc(stored, 16)
                sp.wait_ge(stored, NC * 16)

            @block.gpsimd
            def _(g):
                g.sem_inc(x3_used, PRIMED)
                g.memset(halfneg[:], -0.5).then_inc(const_set, 1)
                g.memset(probs[:], -1.0).then_inc(const_set, 1)
                g.wait_ge(const_set, 2)
                g.wait_ge(loaded, 16 * len(large))
                nc.gpsimd.tensor_tensor(downs[:].rearrange("p e k n -> p (e k) n"), downs[:].rearrange("p e k n -> p (e k) n"),
                                        s["gb1"][:, MASKED:].unsqueeze(1).to_broadcast([P, E1 * HT, KEEP]), ALU.mult).then_inc(const_set, 1)
                with g.Fori(0, NC) as c:
                    wait_first(g, ssq_ready, c + 1)
                    nc.gpsimd.tensor_scalar(rms[:], ssq[:], 1.0 / D, RMS_EPS, ALU.mult, ALU.add).then_inc(pool_seq, 1)
                    wait_first(g, pool_seq, c * 2 + 1)
                    nc.gpsimd.tensor_tensor(rms[:], rms[:], halfneg[:], ALU.pow).then_inc(rms_ready, 1)
                    wait_first(g, xhat_ready, c + 1)
                    nc.gpsimd.tensor_tensor(X[:, c], X[:, c], s["gb1"][:].unsqueeze(1).to_broadcast([P, TILES, D]), ALU.mult).then_inc(pool_seq, 1)
                    g.wait_ge(pool_seq, c * 2 + 2)
                    wait_first(g, x3_loaded, c * 16 + 16)
                    nc.gpsimd.tensor_tensor(X[:, c], X[:, c], x3[:], ALU.add).then_inc(x3_used, 1)

            @block.tensor
            def _(pe):
                pe.sem_inc(down_done, PRIMED)
                pe.sem_inc(up_done, PRIMED)
                pe.wait_ge(small_loaded, 16 * len(small))
                pe.wait_ge(loaded, 16 * len(large))
                pe.wait_ge(const_set, 3)
                with pe.Fori(0, NC) as c:
                    pe.wait_ge(xhat_ready, c + 1)
                    pe.wait_ge(log_copied, c + PRIMED)
                    for h in range(KH):
                        for t in range(TILES):
                            last = nc.tensor.transpose(tp[h][:, t * P:(t + 1) * P], xh[:, t, h * P:(h + 1) * P], s["ident"][:])
                        last.then_inc(trans_done, 1)
                    pe.wait_ge(hT_act, c + 1)
                    pe.wait_ge(hT_dve, c + 1)
                    for t in range(TILES):
                        for k in range(KH):
                            last = nc.tensor.matmul(tp[0][:, t * E1:(t + 1) * E1], hT[:, k, t * P:(t + 1) * P], wg[:, k, :], start=k == 0, stop=k == KH - 1)
                    last.then_inc(log_done, 1)
                    u = dn = 0
                    for st in stages:
                        if st[0] == "down":
                            _, e, src = st
                            pe.wait_ge(*read_by(c, last_writer[src]))
                            for p in range(2):
                                pe.wait_ge(added, c * E1 * 2 + max(0, dn - 1) + PRIMED)
                                for t in (2 * p, 2 * p + 1):
                                    for k in range(HT):
                                        last = nc.tensor.matmul(down_ps[p][:, t % 2, :], buf[src][:, k, t * P:(t + 1) * P], downs[:, e, k, :],
                                                                start=k == 0, stop=k == HT - 1)
                                last.then_inc(down_done, 1)
                                dn += 1
                            continue
                        name, kt, outs, src, _, dst = st
                        if src != "hT":
                            pe.wait_ge(*read_by(c, last_writer[src]))
                        for j in range(outs):
                            if u >= 4:
                                pe.wait_ge(*read_by(c, u - 4))
                            for k in range(kt):
                                last = nc.tensor.matmul(up_ps[u % 4][:], w[name][:, k, j * P:(j + 1) * P], buf[src][:, k, :],
                                                        start=k == 0, stop=k == kt - 1)
                            last.then_inc(up_done, 1)
                            last_writer[dst] = u
                            u += 1

            free_after = {"e2_l3": ("up", of_stage["e2_l2"] + HT), "e3_up": ("down", 2), "e1_w2": ("up", of_stage["e2_l3"] + HT),
                          "e2_l1": ("down", 0), "e0_up": ("down", 0), "e2_l2": ("down", 0), "e3_down": ("up", 0), "e1_w1": ("up", 0)}

            def target_free(eng, c, name):
                kind, n = free_after[name]
                eng.wait_ge(*((up_done, c * JOBS + n + PRIMED) if kind == "up" else (down_done, c * E1 * 2 + n + PRIMED)))

            @block.scalar
            def _(act):
                act.sem_inc(log_copied, PRIMED)
                act.wait_ge(small_loaded, 16 * len(small))
                with act.Fori(0, NC) as c:
                    for t in range(TILES):
                        last = nc.scalar.activation(junk[:, t, :], X[:, c, t, :], ACT.Square, accum_out=ssq[:, t:t + 1])
                    last.then_inc(ssq_ready, 1)
                    act.wait_ge(trans_done, c * 2 + 1)
                    nc.scalar.activation(hT[:, 0, :], tp[0][:], ACT.Identity, scale=nw[:, 1, 0:1]).then_inc(hT_act, 1)
                    act.wait_ge(log_done, c + 1)
                    nc.scalar.activation(lgs[:], tp[0][:, 0:TILES * E1].rearrange("p (t e) -> p t e", e=E1), ACT.Copy).then_inc(log_copied, 1)
                    act.wait_ge(shifted, c + 1)
                    nc.scalar.activation(pr[:], log[:], ACT.Exp).then_inc(exp_done, 1)
                    for u, (st, j) in enumerate(jobs):
                        name, _, _, _, fn, dst = st
                        if fn == "times":
                            continue
                        if j == 0:
                            target_free(act, c, name)
                            if name == "e1_w1":
                                act.wait_ge(dve_read, c * DVES + PRIMED)
                        act.wait_ge(up_done, c * JOBS + u + 1 + PRIMED)
                        nc.scalar.activation(buf[dst][:, j, :], up_ps[u % 4][:], ACT.Silu if fn == "silu" else ACT.Gelu).then_inc(act_read, 1)

            @block.vector
            def _(v):
                v.sem_inc(added, PRIMED)
                v.sem_inc(dve_read, PRIMED)
                v.wait_ge(small_loaded, 16 * len(small))
                v.wait_ge(const_set, 2)
                STEPS = 12
                with v.Fori(0, NC) as c:
                    seq = Tally(c * STEPS)
                    v.wait_ge(rms_ready, c + 1)
                    for t in range(TILES):
                        last = nc.vector.tensor_scalar(xh[:, t, :], X[:, c, t, :], rms[:, t:t + 1], None, ALU.mult)
                    last.then_inc(xhat_ready, 1)
                    v.wait_ge(trans_done, c * 2 + 2)
                    nc.vector.tensor_scalar(hT[:, 1, :], tp[1][:], nw[:, 1, 1:2], None, ALU.mult).then_inc(hT_dve, 1)
                    v.wait_ge(log_copied, c + 1 + PRIMED)
                    nc.vector.tensor_tensor(notnan[:], lgs[:], lgs[:], ALU.is_equal)
                    nc.vector.tensor_scalar(log[:], lgs[:], -FLT_MAX, FLT_MAX, ALU.max, ALU.min).then_inc(dve_seq, 1)
                    v.wait_ge(dve_seq, seq.up())
                    nc.vector.tensor_tensor(lgs[:], log[:], notnan[:], ALU.mult).then_inc(dve_seq, 1)
                    v.wait_ge(dve_seq, seq.up())
                    top_two(nc, v, lgs[:], dict(mx=mx, log=log, pr=pr, z=z, top=top, idx=idx, idf=idf, cw=cw, eq=eq, iota=iota,
                                                out=we, probs=probs), TILES, E1, 1e-8, dve_seq, seq, shifted, exp_done, c, we_ready)
                    v.wait_ge(we_ready, c + 1)
                    v.wait_ge(x3_used, c + 1 + PRIMED)
                    dn = 0
                    for st in stages:
                        if st[0] == "e1_w2":
                            for j in range(HT):
                                u = of_stage["e1_w2"] + j
                                if j == 0:
                                    target_free(v, c, "e1_w2")
                                v.wait_ge(*read_by(c, of_stage["e1_w1"] + j))
                                v.wait_ge(up_done, c * JOBS + u + 1 + PRIMED)
                                nc.vector.tensor_tensor(buf["hc"][:, j, :], up_ps[u % 4][:], buf["hs"][:, j, :], ALU.mult).then_inc(dve_read, 1)
                        elif st[0] == "down":
                            for p in range(2):
                                v.wait_ge(down_done, c * E1 * 2 + dn + 1 + PRIMED)
                                v.wait_ge(added, c * E1 * 2 + max(0, dn - 1) + PRIMED)
                                for t in (2 * p, 2 * p + 1):
                                    last = nc.vector.scalar_tensor_tensor(X[:, c, t, MASKED:], down_ps[p][:, t % 2, :], we[:, t, st[1]:st[1] + 1],
                                                                          X[:, c, t, MASKED:], ALU.mult, ALU.add)
                                last.then_inc(added, 1)
                                dn += 1
                    assert seq.n == STEPS, seq.n


FLT_MAX = float(np.finfo(np.float32).max)


def rows(a, k):
    return np.ascontiguousarray(a.reshape(k, P, -1).transpose(1, 0, 2))


def layout(i):
    f = {k: np.asarray(v) for k, v in i.items()}
    a = {}
    a["x"] = f["L0_attn_x"].reshape(T, D)
    a["cvec"] = np.stack([f["L0_c"].reshape(KH, P).T, f["L1_c"].reshape(KH, P).T], axis=1)
    a["wmod"] = np.stack([rows(f["L0_wmod"], KH), rows(f["L1_wmod"], KH)], axis=1)
    a["wvT"] = rows(f["L0_attn_Wv"].T, KH)
    a["wo0"] = rows(f["L0_attn_Wo"], KH)
    a["wkq"] = np.stack([rows(f["L0_attn_Wk"], KH), rows(f["L0_attn_Wq"], KH)], axis=1)
    a["bkq"] = np.stack([f["L0_attn_bk"].reshape(KH, P).T, f["L0_attn_bq"].reshape(KH, P).T], axis=1)
    a["wg0"] = rows(f["L0_ffn_Wg"], KH)
    a["w1"] = np.stack([rows(w, KH) for w in f["L0_ffn_W1"]], axis=1)
    a["b1"] = f["L0_ffn_b1"].reshape(E0, H0 // P, P).transpose(2, 0, 1)
    a["w2"] = np.stack([rows(w, H0 // P) for w in f["L0_ffn_W2"]], axis=1)
    a["b2_0"] = f["L0_ffn_b2"]
    a["wo1"] = rows(f["L1_attn_wo"].T, KH)
    a["bo1"] = np.broadcast_to(f["L1_attn_bo"], (P, D))
    a["wkv1"] = rows(np.concatenate([f["L1_attn_wk"].T, f["L1_attn_wv"].T], axis=1), KH)
    a["wq1"] = rows(f["L1_attn_wq"].T, KH)
    a["nw"] = np.stack([f["L1_ffn_n1_w"].reshape(KH, P).T, f["L1_ffn_n2_w"].reshape(KH, P).T], axis=1)
    a["qkw"] = np.broadcast_to(np.stack([f["L1_ffn_qn_w"], f["L1_ffn_kn_w"]]), (P, 2, HD))
    a["wqkv"] = rows(np.concatenate([f["L1_ffn_wq"].T, f["L1_ffn_wk"].T, f["L1_ffn_wv"].T], axis=1), KH)
    wo = np.zeros((GROUPS, GH, 32, KEEP), np.float32)
    wo[:, :, :HD, :] = f["L1_ffn_wo"].T.reshape(GROUPS, GH, HD, D)[..., MASKED:]
    a["wo_pad"] = wo.reshape(GROUPS, P, KEEP).transpose(1, 0, 2)
    a["wg1"] = rows(f["L1_ffn_gate_w"].T, KH)
    up = lambda n: rows(f["L1_ffn_" + n].T, f["L1_ffn_" + n].shape[1] // P)
    down = lambda n: rows(f["L1_ffn_" + n].T[:, MASKED:], f["L1_ffn_" + n].shape[1] // P)
    for n in UPS:
        a["m_" + n] = up(n)
    a["downs"] = np.stack([down(n) for n in DOWNS], axis=1)
    t = np.arange(P, dtype=np.float64)
    a["maskT"] = np.where(t[:, None] <= t[None, :], DECAY ** -t[:, None], 0.0).astype(np.float32)
    a["dcol"] = np.stack([DECAY ** t, DECAY ** (P - t)], axis=1).astype(np.float32)
    a["iota"] = np.broadcast_to(np.arange(E0, dtype=np.float32), (P, E0))
    a["ident"] = np.eye(P, dtype=np.float32)
    head = np.arange(P) // HD
    a["same_head"] = (head[:, None] == head[None, :]).astype(np.float32)
    m = np.arange(P)
    a["den_row"] = (m[:, None] == 32 * (m[None, :] // 32) + HD).astype(np.float32)
    return {k: np.ascontiguousarray(v) for k, v in a.items()}


UPS = ("e0_up", "e1_w1", "e1_w2", "e2_l1", "e2_l2", "e2_l3", "e3_down", "e3_up")
DOWNS = ("e0_down", "e1_down", "e2_l4", "e3_out")


def program(nc, shapes, out, upto=99):
    d = {}
    for name, shape in shapes.items():
        d[name] = nc.dram_tensor(f"in_{name}", shape, F32, kind="ExternalInput").ap()
    d["out"] = out
    d["x3"] = nc.dram_tensor("x3", [T, D], F32, kind="Internal").ap()
    s = {}

    def keep(c, name, shape, dt=F32, side="left"):
        s[name] = c.enter_context(nc.sbuf_tensor("s_" + name, shape, dt, side=side))

    with ExitStack() as base:
        keep(base, "xres", [P, NC, TILES, D])
        keep(base, "ident", [P, P])
        keep(base, "gb1", [P, D])
        mods = ExitStack()
        keep(mods, "modc", [P, 16], side="right")
        keep(mods, "gates", [P, 4, D], side="right")
        keep(mods, "sb1", [P, D], side="right")
        keep(mods, "cb1", [P, D], side="right")
        keep(mods, "wo1", [P, KH, D], side="right")
        keep(mods, "bo1", [P, D], side="right")
        with ExitStack() as layer0:
            keep(layer0, "wv0", [P, KH, D], side="right")
            keep(layer0, "h2T", [P, NC, KH, CH], side="right")
            keep(layer0, "we0", [P, NC, TILES, E0], side="right")
            keep(layer0, "w1", [P, E0, KH, H0], side="right")
            keep(layer0, "w2", [P, E0, H0 // P, D], side="right")
            keep(layer0, "b1", [P, E0, H0 // P], side="right")
            setup(nc, d, s)
            if upto > 1:
                attn0(nc, d, s)
            if upto > 2:
                ffn0(nc, d, s)
        lin = ExitStack()
        keep(lin, "qfT", [P, NC, KH, CH], side="right")
        keep(lin, "kvb", [P, KH, P], side="right")
        keep(lin, "ksb", [P, KH, P], side="right")
        if upto > 3:
            lin_keys(nc, d, s)
        with ExitStack() as mid:
            keep(mid, "qk", [P, NC, TILES, 2 * D])
            keep(mid, "vx", [P, NC, TILES, HEADS * (HD + 1)])
            keep(mid, "shift", [P, NC, TILES, HEADS, 3], BF16)
            keep(mid, "knorm", [P, HEADS])
            if upto > 4:
                lin_out(nc, d, s)
            lin.close()
            mods.close()
            if upto > 5:
                shifts(nc, d, s)
                softmax(nc, d, s)
        if upto > 6:
            ffn1(nc, d, s)


def kernel(**inputs):
    import concourse.bacc as _bacc
    from concourse.bass_utils import run_bass_kernel_spmd as _run

    nc = _bacc.Bacc("TRN2", target_bir_lowering=False, num_devices=1)
    arrays = layout(inputs)
    out = nc.dram_tensor("out_0_dram", (T, D), F32, kind="ExternalOutput").ap()
    program(nc, {k: v.shape for k, v in arrays.items()}, out)
    r = _run(nc, [{f"in_{k}": v for k, v in arrays.items()}], core_ids=[0])
    return r.results[0]["out_0_dram"].reshape(1, T, D)
```

```python
from contextlib import ExitStack

import numpy as np
import concourse.bass as bass
from concourse import mybir

ALU = mybir.AluOpType
ACT = mybir.ActivationFunctionType
F32 = mybir.dt.float32
BF16 = mybir.dt.bfloat16
U32 = mybir.dt.uint32
AX = mybir.AxisListType.X

P = 128
T = 4096
D = 256
KH = D // P
TILES = 4
CH = TILES * P
NC = T // CH
DECAY = 0.99
PRIMED = 1
E0, H0 = 8, 512
E1, H1 = 4, 512
HEADS, HD = 16, 16
GROUPS, GH = 4, 4
MASKED = 64
KEEP = D - MASKED
SPLIT = 6 * HD
ROWS = SPLIT + 3


class Tally:

    def __init__(self, base=0):
        self.base, self.n = base, 0

    def up(self, k=1):
        self.n += k
        return self.base + self.n


def wait_first(eng, sem, value, met=None):
    held = eng.alloc_register()
    eng.reg_mov(held, value)
    eng.wait_ge(met or sem, 1)
    eng.wait_ge(sem, held)
    eng.free_register(held)


def merged(ap):
    return ap.rearrange("p a b -> p (a b)")


def setup(nc, d, s):
    with ExitStack() as ctx:
        sb = lambda n, sh, dt=F32: ctx.enter_context(nc.sbuf_tensor(n, sh, dt))
        sem = lambda n: ctx.enter_context(nc.semaphore(n))
        psum = [ctx.enter_context(nc.psum_tensor(f"set_ps{i}", [P, 512], F32)) for i in range(8)]
        wmod = sb("wmod", [P, 2, KH, 6 * D])
        cvec = sb("cvec", [P, 2, KH])
        silu_c = sb("silu_c", [P, 2, KH])
        silu_rep = sb("silu_rep", [P, 2, KH, P])
        wvT = sb("wvT", [P, KH, D])
        wo0 = sb("wo0", [P, KH, D])
        raw = sb("gate_raw", [P, 4, D])
        sign = sb("gate_sign", [P, 4, D])
        size = sb("gate_size", [P, 4, D])
        loaded, silu_done, rep_done, mod_done, cols_done = (sem(x) for x in
            ("mod_loaded", "silu_done", "rep_done", "mod_done", "cols_done"))
        raw_done, sign_done, gates_done, wv_done, fold_done = (sem(x) for x in
            ("raw_done", "sign_done", "gates_done", "wv_done", "fold_done"))
        with nc.Block() as block:
            @block.sync
            def _(sp):
                for dst, src in ((cvec, d["cvec"]), (wmod, d["wmod"]), (wvT, d["wvT"]), (wo0, d["wo0"]),
                                 (s["wo1"], d["wo1"]), (s["bo1"], d["bo1"])):
                    sp.dma_start(dst[:], src).then_inc(loaded, 16)

            @block.scalar
            def _(act):
                act.wait_ge(loaded, 96)
                nc.scalar.activation(silu_c[:], cvec[:], ACT.Silu).then_inc(silu_done, 1)

            @block.tensor
            def _(pe):
                pe.wait_ge(rep_done, 1)
                for layer in range(2):
                    for n in range(3):
                        for k in range(KH):
                            last = nc.tensor.matmul(psum[3 * layer + n][:], silu_rep[:, layer, k, :],
                                                    wmod[:, layer, k, n * 512:(n + 1) * 512],
                                                    start=k == 0, stop=k == KH - 1)
                last.then_inc(mod_done, 1)
                for layer in range(2):
                    for i, m in enumerate((0, 1, 3, 4)):
                        for h in range(KH):
                            col = (layer * 4 + i) * KH + h
                            for k in range(KH):
                                last = nc.tensor.matmul(
                                    psum[6][:, col:col + 1],
                                    wmod[:, layer, k, m * D + h * P:m * D + (h + 1) * P],
                                    silu_c[:, layer, k:k + 1], start=k == 0, stop=k == KH - 1)
                last.then_inc(mod_done, 1)
                for h in range(KH):
                    for k in range(KH):
                        last = nc.tensor.matmul(psum[7][:, h * D:(h + 1) * D], wvT[:, k, h * P:(h + 1) * P],
                                                wo0[:, k, :], start=k == 0, stop=k == KH - 1)
                last.then_inc(wv_done, 1)

            @block.vector
            def _(v):
                v.wait_ge(silu_done, 1)
                nc.vector.tensor_copy(silu_rep[:].rearrange("p a b c -> p (a b) c"),
                                      merged(silu_c[:]).unsqueeze(2).to_broadcast([P, 2 * KH, P])).then_inc(rep_done, 1)
                v.wait_ge(mod_done, 1)
                nc.vector.tensor_copy(raw[:, 0, :], psum[1][:, 0:D])
                nc.vector.tensor_copy(raw[:, 1, :], psum[2][:, D:2 * D])
                nc.vector.tensor_copy(raw[:, 2, :], psum[4][:, 0:D])
                nc.vector.tensor_copy(raw[:, 3, :], psum[5][:, D:2 * D])
                nc.vector.tensor_copy(s["sb1"][:], psum[4][:, D:2 * D])
                nc.vector.tensor_scalar(s["cb1"][:], psum[5][:, 0:D], 1.0, None, ALU.add).then_inc(raw_done, 1)
                v.wait_ge(raw_done, 1)
                nc.vector.tensor_scalar(sign[:], raw[:], 0.0, 2.0, ALU.is_ge, ALU.mult)
                nc.vector.tensor_scalar(size[:], raw[:], -1.0, None, ALU.mult).then_inc(sign_done, 1)
                v.wait_ge(sign_done, 1)
                nc.vector.tensor_tensor(size[:], size[:], raw[:], ALU.max).then_inc(sign_done, 1)
                v.wait_ge(sign_done, 2)
                nc.vector.tensor_scalar(size[:], size[:], 0.25, None, ALU.max).then_inc(sign_done, 1)
                v.wait_ge(sign_done, 3)
                nc.vector.scalar_tensor_tensor(s["gates"][:].rearrange("p a b -> p (a b)"), merged(sign[:]), -1.0,
                                               merged(size[:]), ALU.add, ALU.mult).then_inc(gates_done, 1)
                v.wait_ge(mod_done, 2)
                nc.vector.tensor_copy(s["modc"][:], psum[6][:, 0:16]).then_inc(cols_done, 1)
                v.wait_ge(cols_done, 1)
                for i in (1, 3, 5, 7):
                    nc.vector.tensor_scalar(s["modc"][:, KH * i:KH * i + KH], s["modc"][:, KH * i:KH * i + KH], 1.0, None, ALU.add)
                v.wait_ge(gates_done, 1)
                v.wait_ge(wv_done, 1)
                for h in range(KH):
                    nc.vector.scalar_tensor_tensor(s["wv0"][:, h, :], psum[7][:, h * D:(h + 1) * D], 1.0 - DECAY,
                                                   s["gates"][:, 0, :], ALU.mult, ALU.mult)
                for k in range(KH):
                    nc.vector.tensor_tensor(s["wo1"][:, k, :], s["wo1"][:, k, :], s["gates"][:, 2, :], ALU.mult)
                nc.vector.tensor_tensor(s["bo1"][:], s["bo1"][:], s["gates"][:, 2, :], ALU.mult)
                nc.vector.tensor_copy(s["gb1"][:], s["gates"][:, 3, :]).then_inc(fold_done, 1)
                v.wait_ge(fold_done, 1)


def layer0_pass(nc, d, s):
    HT = H0 // P
    with ExitStack() as ctx:
        sb = lambda n, sh, dt=F32: ctx.enter_context(nc.sbuf_tensor(n, sh, dt))
        sem = lambda n: ctx.enter_context(nc.semaphore("l0_" + n))
        bank = [ctx.enter_context(nc.psum_tensor(f"l0_ps{i}", [P, 512], F32)) for i in range(4)]
        up_ps = [ctx.enter_context(nc.psum_tensor(f"l0_up{i}", [P, CH], F32)) for i in range(2)]
        down_ps = [ctx.enter_context(nc.psum_tensor(f"l0_dn{i}", [P, 2, D], F32)) for i in range(2)]
        wkq = sb("wkq", [P, 2, KH, D])
        bkq = sb("bkq", [P, 2, KH])
        wg = sb("wg0", [P, KH, E0])
        b2 = sb("b2_0", [E0, D])
        maskT = sb("maskT", [P, P])
        dcol = sb("dcol", [P, 2])
        iota = sb("iota0", [P, E0])
        stats = sb("l0_stats", [P, TILES, 6])
        mv = sb("l0_mv", [P, TILES, 2])
        rstd = sb("l0_rstd", [P, TILES])
        halfneg = sb("l0_halfneg", [P, TILES])
        xh = sb("l0_xh", [P, TILES, D])
        hT = sb("l0_hT", [P, KH, CH])
        kqT = sb("l0_kqT", [P, 2, KH, CH])
        vt = sb("l0_v", [P, TILES, D])
        vk = sb("l0_vk", [P, TILES, D])
        ktok = sb("l0_ktok", [P, TILES, D])
        aT = sb("l0_aT", [P, TILES, P])
        state = sb("l0_state", [P, TILES + 1, KH * D])
        hid = sb("l0_hid", [P, 2, HT, CH])
        logT = sb("l0_logT", [E0, CH])
        log = sb("l0_log", [P, TILES, E0])
        mx = sb("l0_mx", [P, TILES])
        pr = sb("l0_pr", [P, TILES, E0])
        z = sb("l0_z", [P, TILES])
        top = sb("l0_top", [P, TILES, 8])
        idx = sb("l0_idx", [P, TILES, 8], U32)
        idf = sb("l0_idf", [P, TILES, 8])
        cw = sb("l0_cw", [P, TILES, 2])
        eq = sb("l0_eq", [P, 2, TILES, E0])
        weC = sb("l0_we", [P, TILES, E0])
        weT = logT
        (loaded, w_loaded, const_set, stats_ready, rstd_ready, xhat_ready, trans_done, hT_act, hT_dve, proj_done,
         sig_done, v_ready, ktrans_done, ktok_ready, score_done, aT_ready, kv_done, state_ready, y_done,
         x1_ready, log_done, logT_ready, ltr_done, shifted, exp_done, we_ready, wetr_done, weT_ready,
         b2_done, b2_added, dve_seq, pool_seq, scaled, up_done, hid_ready, down_done, added) = (sem(x) for x in
            ("loaded", "w_loaded", "const_set", "stats_ready", "rstd_ready", "xhat_ready", "trans_done", "hT_act",
             "hT_dve", "proj_done", "sig_done", "v_ready", "ktrans_done", "ktok_ready", "score_done", "aT_ready",
             "kv_done", "state_ready", "y_done", "x1_ready", "log_done", "logT_ready", "ltr_done", "shifted",
             "exp_done", "we_ready", "wetr_done", "weT_ready", "b2_done", "b2_added", "dve_seq", "pool_seq", "scaled",
             "up_done", "hid_ready", "down_done", "added"))
        x_loaded = [sem(f"x_loaded{c}") for c in range(2)]
        X = s["xres"]
        small = ((wkq, d["wkq"]), (bkq, d["bkq"]), (wg, d["wg0"]), (b2, d["b2_0"]), (maskT, d["maskT"]), (dcol, d["dcol"]),
                 (iota, d["iota"]), (s["ident"], d["ident"]))
        Y_BANK = (3, 0)
        KV_BANK = (3, 0, 1, 2)
        with nc.Block() as block:
            @block.sync
            def _(sp):
                x_dram = d["x"].rearrange("(c t p) n -> p c t n", t=TILES, p=P)
                sp.dma_start(X[:, 0], x_dram[:, 0]).then_inc(x_loaded[0], 16)
                for dst, src in small:
                    sp.dma_start(dst[:], src).then_inc(loaded, 16)
                for c in range(1, NC):
                    sp.dma_start(X[:, c], x_dram[:, c]).then_inc(x_loaded[1], 16)
                for dst, src in ((s["w1"], d["w1"]), (s["w2"], d["w2"]), (s["b1"], d["b1"])):
                    sp.dma_start(dst[:], src).then_inc(w_loaded, 16)

            @block.gpsimd
            def _(g):
                g.memset(halfneg[:], -0.5).then_inc(const_set, 1)
                g.memset(state[:, TILES, :], 0.0).then_inc(const_set, 1)
                g.wait_ge(const_set, 2)
                g.wait_ge(loaded, 16 * len(small))
                nc.gpsimd.tensor_tensor(b2[:], b2[:], s["gates"][0:E0, 1, :], ALU.mult).then_inc(const_set, 1)

                def rstds(f, half):
                    wait_first(g, stats_ready, f * 2 + half + 1)
                    nc.gpsimd.tensor_scalar(rstd[:], mv[:, :, 1], 1e-5, None, ALU.add).then_inc(pool_seq, 1)
                    wait_first(g, pool_seq, f * 2 + half + 1)
                    nc.gpsimd.tensor_tensor(rstd[:], rstd[:], halfneg[:], ALU.pow).then_inc(rstd_ready, 1)

                rstds(0, 0)
                rstds(0, 1)
                g.wait_ge(w_loaded, 48)
                for e in range(E0):
                    nc.gpsimd.tensor_tensor(s["w2"][:, e], s["w2"][:, e], s["gates"][:, 1:2, :].to_broadcast([P, HT, D]), ALU.mult).then_inc(scaled, 1)
                with g.Fori(1, NC) as f:
                    rstds(f, 0)
                    rstds(f, 1)

            @block.tensor
            def _(pe):
                pe.sem_inc(down_done, PRIMED)
                pe.wait_ge(loaded, 16 * len(small))
                pe.wait_ge(const_set, 3)

                def transposes(f, k, b):
                    pe.wait_ge(xhat_ready, f * 2 + k + 1)
                    for h in range(KH):
                        for t in range(TILES):
                            last = nc.tensor.transpose(bank[b + h][:, t * P:(t + 1) * P], xh[:, t, h * P:(h + 1) * P], s["ident"][:])
                        last.then_inc(trans_done, 1)

                def front(stage, f):
                    if stage == 0:
                        pe.wait_ge(b2_added, f * 2 + PRIMED)
                        transposes(f, 0, 0)
                    if stage == 1:
                        pe.wait_ge(hT_act, f * 2 + 1)
                        pe.wait_ge(hT_dve, f * 2 + 1)
                        for w in range(2):
                            for h in range(KH):
                                for k in range(KH):
                                    last = nc.tensor.matmul(bank[(2 - 2 * w) + h][:], wkq[:, w, k, h * P:(h + 1) * P], hT[:, k, :],
                                                            start=k == 0, stop=k == KH - 1)
                                last.then_inc(proj_done, 1)
                        pe.wait_ge(sig_done, f * 4 + 2)
                        for p in range(2):
                            for t in (2 * p, 2 * p + 1):
                                for k in range(KH):
                                    last = nc.tensor.matmul(bank[2 + p][:, (t % 2) * D:(t % 2 + 1) * D], hT[:, k, t * P:(t + 1) * P],
                                                            s["wv0"][:, k, :], start=k == 0, stop=k == KH - 1)
                            last.then_inc(proj_done, 1)
                    if stage == 2:
                        pe.wait_ge(sig_done, f * 4 + 4)
                        for p in range(2):
                            for t in (2 * p, 2 * p + 1):
                                for h in range(KH):
                                    last = nc.tensor.transpose(bank[p][:, (t % 2) * D + h * P:(t % 2) * D + (h + 1) * P],
                                                               kqT[:, 0, h, t * P:(t + 1) * P], s["ident"][:])
                            last.then_inc(ktrans_done, 1)
                        pe.wait_ge(v_ready, f * 2 + 2)
                        for t in range(TILES):
                            for k in range(KH):
                                last = nc.tensor.matmul(bank[2][:, t * P:(t + 1) * P], kqT[:, 0, k, t * P:(t + 1) * P],
                                                        kqT[:, 1, k, t * P:(t + 1) * P], start=k == 0, stop=k == KH - 1)
                        last.then_inc(score_done, 1)
                    if stage == 3:
                        pe.wait_ge(aT_ready, f + 1)
                        pe.wait_ge(ktok_ready, f * 2 + 2)
                        for t in range(TILES):
                            for h in range(KH):
                                last = nc.tensor.matmul(bank[KV_BANK[t]][:, h * D:(h + 1) * D], ktok[:, t, h * P:(h + 1) * P], vk[:, t, :],
                                                        start=True, stop=True)
                            last.then_inc(kv_done, 1)
                    if stage == 4:
                        for t in range(TILES):
                            y = bank[Y_BANK[t // 2]][:, (t % 2) * D:(t % 2 + 1) * D]
                            pe.wait_ge(state_ready, f * 5 + max(t + 1, 2 + t // 2))
                            nc.tensor.matmul(y, aT[:, t, :], vt[:, t, :], start=True, stop=False)
                            for k in range(KH):
                                last = nc.tensor.matmul(y, kqT[:, 1, k, t * P:(t + 1) * P], state[:, t, k * D:(k + 1) * D],
                                                        start=False, stop=k == KH - 1)
                            if t % 2:
                                last.then_inc(y_done, 1)
                    if stage == 5:
                        pe.wait_ge(state_ready, f * 5 + 5)
                        transposes(f, 1, 1)
                    if stage == 6:
                        pe.wait_ge(hT_act, f * 2 + 2)
                        pe.wait_ge(hT_dve, f * 2 + 2)
                        for k in range(KH):
                            last = nc.tensor.matmul(bank[3][0:E0, :], wg[:, k, :], s["h2T"][:, f, k, :], start=k == 0, stop=k == KH - 1)
                        last.then_inc(log_done, 1)
                        wait_first(pe, logT_ready, f + 1)
                        for t in range(TILES):
                            last = nc.tensor.transpose(bank[0][:, t * E0:(t + 1) * E0], logT[:, t * P:(t + 1) * P], s["ident"][0:E0, 0:E0])
                        last.then_inc(ltr_done, 1)
                    if stage == 7:
                        pe.wait_ge(we_ready, f + 1)
                        for t in range(TILES):
                            last = nc.tensor.transpose(bank[1][0:E0, t * P:(t + 1) * P], weC[:, t, :], s["ident"][:])
                        last.then_inc(wetr_done, 1)
                        pe.wait_ge(weT_ready, f + 1)
                        for t in range(TILES):
                            last = nc.tensor.matmul(bank[2 + t // 2][:, (t % 2) * D:(t % 2 + 1) * D], weT[:, t * P:(t + 1) * P], b2[:],
                                                    start=True, stop=True)
                            if t % 2:
                                last.then_inc(b2_done, 1)

                def up(c, e):
                    for j in range(HT):
                        if e > 0 or j > 1:
                            pe.wait_ge(hid_ready, c * E0 * HT + e * HT + j - 1 + PRIMED)
                        else:
                            pe.wait_ge(hid_ready, c * E0 * HT + PRIMED)
                        for k in range(KH):
                            last = nc.tensor.matmul(up_ps[j % 2][:], s["w1"][:, e, k, j * P:(j + 1) * P], s["h2T"][:, c, k, :],
                                                    start=k == 0, stop=k == KH - 1)
                        last.then_inc(up_done, 1)

                def down(c, e):
                    pe.wait_ge(hid_ready, c * E0 * HT + (e + 1) * HT + PRIMED)
                    for p in range(2):
                        if e:
                            pe.wait_ge(added, c * E0 * 2 + (e - 1) * 2 + p + 1 + PRIMED)
                        else:
                            pe.wait_ge(added, c * E0 * 2 + PRIMED)
                        for t in (2 * p, 2 * p + 1):
                            for k in range(HT):
                                last = nc.tensor.matmul(down_ps[p][:, t % 2, :], hid[:, e % 2, k, t * P:(t + 1) * P],
                                                        s["w2"][:, e, k, :], start=k == 0, stop=k == HT - 1)
                        last.then_inc(down_done, 1)

                for stage in range(8):
                    front(stage, 0)
                pe.wait_ge(w_loaded, 48)
                pe.wait_ge(scaled, E0)
                with pe.Fori(0, NC - 1) as c:
                    up(c, 0)
                    for e in range(E0):
                        if e + 1 < E0:
                            up(c, e + 1)
                        down(c, e)
                        front(e, c + 1)
                up(NC - 1, 0)
                for e in range(E0):
                    if e + 1 < E0:
                        up(NC - 1, e + 1)
                    down(NC - 1, e)

            @block.scalar
            def _(act):
                act.sem_inc(hid_ready, PRIMED)
                act.wait_ge(loaded, 16 * len(small))

                def front(stage, f):
                    if stage == 0:
                        act.wait_ge(trans_done, f * 4 + 1)
                        nc.scalar.activation(hT[:, 0, :], bank[0][:], ACT.Identity, bias=s["modc"][:, 0:1], scale=s["modc"][:, 2:3]).then_inc(hT_act, 1)
                    if stage == 1:
                        for w in range(2):
                            for h in range(KH):
                                act.wait_ge(proj_done, f * 6 + 2 * w + h + 1)
                                nc.scalar.activation(kqT[:, w, h, :], bank[(2 - 2 * w) + h][:], ACT.Sigmoid, bias=bkq[:, w, h:h + 1]).then_inc(sig_done, 1)
                    if stage == 2:
                        for p in range(2):
                            act.wait_ge(ktrans_done, f * 2 + p + 1)
                            nc.scalar.activation(merged(ktok[:, 2 * p:2 * p + 2, :]), bank[p][:], ACT.Copy).then_inc(ktok_ready, 1)
                    if stage == 5:
                        act.wait_ge(trans_done, f * 4 + 3)
                        nc.scalar.activation(s["h2T"][:, f, 0, :], bank[1][:], ACT.Identity, bias=s["modc"][:, 4:5], scale=s["modc"][:, 6:7]).then_inc(hT_act, 1)
                    if stage == 6:
                        act.wait_ge(log_done, f + 1)
                        nc.scalar.activation(logT[:], bank[3][0:E0, :], ACT.Copy).then_inc(logT_ready, 1)
                        act.wait_ge(shifted, f + 1)
                        nc.scalar.activation(pr[:], log[:], ACT.Exp).then_inc(exp_done, 1)
                    if stage == 7:
                        act.wait_ge(wetr_done, f + 1)
                        nc.scalar.activation(weT[:], bank[1][0:E0, :], ACT.Copy).then_inc(weT_ready, 1)

                def relus(c, e):
                    act.wait_ge(down_done, c * E0 * 2 + max(0, (e - 1) * 2) + PRIMED)
                    for j in range(HT):
                        act.wait_ge(up_done, c * E0 * HT + e * HT + j + 1)
                        nc.scalar.activation(hid[:, e % 2, j, :], up_ps[j % 2][:], ACT.Relu, bias=s["b1"][:, e, j:j + 1]).then_inc(hid_ready, 1)

                for stage in range(8):
                    front(stage, 0)
                act.wait_ge(w_loaded, 48)
                with act.Fori(0, NC - 1) as c:
                    relus(c, 0)
                    for e in range(E0):
                        if e + 1 < E0:
                            relus(c, e + 1)
                        front(e, c + 1)
                for e in range(E0):
                    relus(NC - 1, e)

            @block.vector
            def _(v):
                v.sem_inc(b2_added, PRIMED)
                v.sem_inc(added, PRIMED)
                v.wait_ge(loaded, 16 * len(small))
                v.wait_ge(const_set, 3)
                v.wait_ge(x_loaded[0], 16)

                def normalise(f, k, seq):
                    for t in range(TILES):
                        last = nc.vector.bn_stats(stats[:, t, :], X[:, f, t, :])
                    last.then_inc(dve_seq, 1)
                    wait_first(v, dve_seq, seq.up())
                    for t in range(TILES):
                        last = nc.vector.bn_aggr(mv[:, t, :], stats[:, t, :])
                    last.then_inc(stats_ready, 1)
                    v.wait_ge(stats_ready, f * 2 + k + 1)
                    v.wait_ge(rstd_ready, f * 2 + k + 1)
                    for t in range(TILES):
                        last = nc.vector.tensor_scalar(xh[:, t, :], X[:, f, t, :], mv[:, t, 0:1], rstd[:, t:t + 1], ALU.subtract, ALU.mult)
                    last.then_inc(xhat_ready, 1)

                STEPS = 13

                def front(stage, f, seq):
                    if stage == 0:
                        nc.vector.tensor_copy(state[:, 0, :], state[:, TILES, :]).then_inc(state_ready, 1)
                        v.wait_ge(trans_done, f * 4 + 2)
                        nc.vector.tensor_scalar(hT[:, 1, :], bank[1][:], s["modc"][:, 3:4], s["modc"][:, 1:2], ALU.mult, ALU.add).then_inc(hT_dve, 1)
                    if stage == 1:
                        for p in range(2):
                            v.wait_ge(proj_done, f * 6 + 4 + p + 1)
                            nc.vector.tensor_scalar(merged(vk[:, 2 * p:2 * p + 2, :]), bank[2 + p][:], dcol[:, 1:2], None, ALU.mult)
                            nc.vector.tensor_copy(merged(vt[:, 2 * p:2 * p + 2, :]), bank[2 + p][:]).then_inc(v_ready, 1)
                    if stage == 2:
                        v.wait_ge(score_done, f + 1)
                        nc.vector.tensor_tensor(aT[:], bank[2][:].rearrange("p (t n) -> p t n", t=TILES),
                                                maskT[:].unsqueeze(1).to_broadcast([P, TILES, P]), ALU.mult).then_inc(aT_ready, 1)
                    if stage == 3:
                        for t in range(TILES):
                            v.wait_ge(kv_done, f * 4 + t + 1)
                            v.wait_ge(state_ready, f * 5 + t + 1)
                            nc.vector.scalar_tensor_tensor(state[:, t + 1, :], state[:, t, :], DECAY ** P, bank[KV_BANK[t]][:],
                                                           ALU.mult, ALU.add).then_inc(state_ready, 1)
                    if stage == 4:
                        v.wait_ge(state_ready, f * 5 + 5)
                        for p in range(2):
                            v.wait_ge(y_done, f * 2 + p + 1)
                            nc.vector.scalar_tensor_tensor(merged(X[:, f, 2 * p:2 * p + 2, :]), bank[Y_BANK[p]][:], dcol[:, 0:1],
                                                           merged(X[:, f, 2 * p:2 * p + 2, :]), ALU.mult, ALU.add).then_inc(x1_ready, 1)
                        wait_first(v, x1_ready, f * 2 + 2)
                        normalise(f, 1, seq)
                    if stage == 5:
                        v.wait_ge(trans_done, f * 4 + 4)
                        nc.vector.tensor_scalar(s["h2T"][:, f, 1, :], bank[2][:], s["modc"][:, 7:8], s["modc"][:, 5:6], ALU.mult, ALU.add).then_inc(hT_dve, 1)
                    if stage == 6:
                        v.wait_ge(ltr_done, f + 1)
                        lg = bank[0][:, 0:TILES * E0].rearrange("p (t e) -> p t e", e=E0)
                        top_two(nc, v, lg, dict(mx=mx, log=log, pr=pr, z=z, top=top, idx=idx, idf=idf, cw=cw, eq=eq,
                                                iota=iota, out=weC, probs=pr), TILES, E0, 1e-9, dve_seq, seq, shifted, exp_done, f, we_ready)
                        v.wait_ge(we_ready, f + 1)
                        nc.vector.tensor_copy(s["we0"][:, f], weC[:]).then_inc(dve_seq, 1)
                        seq.up()
                    if stage == 7:
                        for p in range(2):
                            v.wait_ge(b2_done, f * 2 + p + 1)
                            nc.vector.tensor_tensor(merged(X[:, f, 2 * p:2 * p + 2, :]), merged(X[:, f, 2 * p:2 * p + 2, :]), bank[2 + p][:],
                                                    ALU.add).then_inc(b2_added, 1)
                        v.wait_ge(b2_added, f * 2 + 2 + PRIMED)
                        assert seq.n == STEPS, seq.n

                def shares(c, e):
                    for p in range(2):
                        v.wait_ge(down_done, c * E0 * 2 + e * 2 + p + 1 + PRIMED)
                        v.wait_ge(added, c * E0 * 2 + max(0, e * 2 + p - 1) + PRIMED)
                        for t in (2 * p, 2 * p + 1):
                            last = nc.vector.scalar_tensor_tensor(X[:, c, t, :], down_ps[p][:, t % 2, :], s["we0"][:, c, t, e:e + 1],
                                                                  X[:, c, t, :], ALU.mult, ALU.add)
                        last.then_inc(added, 1)

                seq = Tally(0)
                normalise(0, 0, seq)
                for stage in range(8):
                    front(stage, 0, seq)
                v.wait_ge(x_loaded[1], 16 * (NC - 1))
                with v.Fori(0, NC - 1) as c:
                    seq = Tally((c + 1) * STEPS)
                    normalise(c + 1, 0, seq)
                    for e in range(E0):
                        shares(c, e)
                        front(e, c + 1, seq)
                for e in range(E0):
                    shares(NC - 1, e)


def top_two(nc, v, lg, b, tiles, experts, eps, dve_seq, seq, shifted, exp_done, c, ready):
    wide = lambda ap: ap.unsqueeze(2).to_broadcast([P, tiles, experts])
    nc.vector.tensor_reduce(b["mx"][:], lg, AX, ALU.max).then_inc(dve_seq, 1)
    v.wait_ge(dve_seq, seq.up())
    nc.vector.tensor_tensor(b["log"][:], lg, wide(b["mx"][:]), ALU.subtract).then_inc(shifted, 1)
    v.wait_ge(exp_done, c + 1)
    nc.vector.tensor_reduce(b["z"][:], b["pr"][:], AX, ALU.add).then_inc(dve_seq, 1)
    v.wait_ge(dve_seq, seq.up())
    nc.vector.reciprocal(b["z"][:], b["z"][:]).then_inc(dve_seq, 1)
    v.wait_ge(dve_seq, seq.up())
    nc.vector.tensor_tensor(b["probs"][:, :, 0:experts], b["pr"][:], wide(b["z"][:]), ALU.mult).then_inc(dve_seq, 1)
    wait_first(v, dve_seq, seq.up())
    for t in range(tiles):
        last = nc.vector.max(b["top"][:, t, :], b["probs"][:, t, :])
    last.then_inc(dve_seq, 1)
    wait_first(v, dve_seq, seq.up())
    for t in range(tiles):
        nc.vector.max_index(b["idx"][:, t, :], b["top"][:, t, :], b["probs"][:, t, :])
    nc.vector.tensor_tensor(b["z"][:], b["top"][:, :, 0], b["top"][:, :, 1], ALU.add).then_inc(dve_seq, 1)
    v.wait_ge(dve_seq, seq.up())
    nc.vector.tensor_copy(b["idf"][:], b["idx"][:])
    nc.vector.tensor_scalar(b["z"][:], b["z"][:], eps, None, ALU.add).then_inc(dve_seq, 1)
    v.wait_ge(dve_seq, seq.up())
    nc.vector.reciprocal(b["z"][:], b["z"][:]).then_inc(dve_seq, 1)
    v.wait_ge(dve_seq, seq.up())
    for r in range(2):
        nc.vector.tensor_tensor(b["cw"][:, :, r], b["top"][:, :, r], b["z"][:], ALU.mult)
        last = nc.vector.tensor_tensor(b["eq"][:, r], b["iota"][:, 0:experts].unsqueeze(1).to_broadcast([P, tiles, experts]),
                                       wide(b["idf"][:, :, r]), ALU.is_equal)
    last.then_inc(dve_seq, 1)
    v.wait_ge(dve_seq, seq.up())
    for r in range(2):
        last = nc.vector.tensor_tensor(b["eq"][:, r], b["eq"][:, r], wide(b["cw"][:, :, r]), ALU.mult)
    last.then_inc(dve_seq, 1)
    v.wait_ge(dve_seq, seq.up())
    nc.vector.tensor_tensor(b["out"][:], b["eq"][:, 0], b["eq"][:, 1], ALU.add).then_inc(ready, 1)


def lin_keys(nc, d, s):
    with ExitStack() as ctx:
        sb = lambda n, sh, dt=F32: ctx.enter_context(nc.sbuf_tensor("lk_" + n, sh, dt))
        sem = lambda n: ctx.enter_context(nc.semaphore("lk_" + n))
        bank = [ctx.enter_context(nc.psum_tensor(f"lk_ps{i}", [P, 512], F32)) for i in range(8)]
        wkv = sb("wkv", [P, KH, 2 * D])
        wq = sb("wq", [P, KH, D])
        same_head = sb("same_head", [P, P])
        stats = sb("stats", [P, TILES, 6])
        mv = sb("mv", [P, TILES, 2])
        rstd = sb("rstd", [P, TILES])
        halfneg = sb("halfneg", [P, TILES])
        zero = sb("zero", [P, P])
        xh = sb("xh", [P, TILES, D])
        hT = sb("hT", [P, KH, CH])
        kneg = sb("kneg", [P, TILES, D])
        kf = sb("kf", [P, TILES, D])
        vt = sb("vt", [P, TILES, KH, P + 1])
        qneg = sb("qneg", [P, KH, CH])
        (loaded, const_set, stats_ready, rstd_ready, xhat_ready, trans_done, hT_act, hT_dve, kv_proj, q_proj, neg_ready,
         exp_ready, v_ready, kf_ready, qf_ready, sum_done, dve_seq, pool_seq) = (sem(x) for x in
            ("loaded", "const_set", "stats_ready", "rstd_ready", "xhat_ready", "trans_done", "hT_act", "hT_dve", "kv_proj",
             "q_proj", "neg_ready", "exp_ready", "v_ready", "kf_ready", "qf_ready", "sum_done", "dve_seq", "pool_seq"))
        X = s["xres"]
        with nc.Block() as block:
            @block.sync
            def _(sp):
                for dst, src in ((wkv, d["wkv1"]), (wq, d["wq1"]), (same_head, d["same_head"])):
                    sp.dma_start(dst[:], src).then_inc(loaded, 16)

            @block.gpsimd
            def _(g):
                g.memset(halfneg[:], -0.5).then_inc(const_set, 1)
                g.memset(zero[:], 0.0).then_inc(const_set, 1)
                g.memset(vt[:], 1.0).then_inc(const_set, 1)
                g.wait_ge(const_set, 3)
                with g.Fori(0, NC) as c:
                    wait_first(g, stats_ready, c + 1)
                    nc.gpsimd.tensor_scalar(rstd[:], mv[:, :, 1], 1e-5, None, ALU.add).then_inc(pool_seq, 1)
                    wait_first(g, pool_seq, c + 1)
                    nc.gpsimd.tensor_tensor(rstd[:], rstd[:], halfneg[:], ALU.pow).then_inc(rstd_ready, 1)

            @block.tensor
            def _(pe):
                pe.sem_inc(sum_done, PRIMED)
                pe.wait_ge(loaded, 48)
                pe.wait_ge(const_set, 3)
                for h in range(KH):
                    nc.tensor.matmul(bank[6 + h][:, 0:P], zero[:], zero[:], start=True, stop=False, skip_group_check=True)
                    nc.tensor.matmul(bank[6 + h][:, P:P + 1], zero[:], zero[:, 0:1], start=False, stop=False, skip_group_check=True)
                with pe.Fori(0, NC) as c:
                    pe.wait_ge(xhat_ready, c + 1)
                    pe.wait_ge(qf_ready, c * 2 + PRIMED)
                    for h in range(KH):
                        for t in range(TILES):
                            last = nc.tensor.transpose(bank[h][:, t * P:(t + 1) * P], xh[:, t, h * P:(h + 1) * P], s["ident"][:])
                        last.then_inc(trans_done, 1)
                    pe.wait_ge(hT_act, c + 1)
                    pe.wait_ge(hT_dve, c + 1)
                    for t in range(TILES):
                        pe.wait_ge(kf_ready, c * 4 + PRIMED)
                        for k in range(KH):
                            last = nc.tensor.matmul(bank[2 + t][:], hT[:, k, t * P:(t + 1) * P], wkv[:, k, :], start=k == 0, stop=k == KH - 1)
                        last.then_inc(kv_proj, 1)
                    for h in range(KH):
                        for k in range(KH):
                            last = nc.tensor.matmul(bank[h][:], wq[:, k, h * P:(h + 1) * P], hT[:, k, :], start=k == 0, stop=k == KH - 1)
                        last.then_inc(q_proj, 1)
                    for t in range(TILES):
                        pe.wait_ge(kf_ready, c * 4 + t + 1 + PRIMED)
                        pe.wait_ge(v_ready, c * 4 + t + 1)
                        for h in range(KH):
                            last = nc.tensor.matmul(bank[6 + h][:, 0:P + 1], kf[:, t, h * P:(h + 1) * P], vt[:, t, h, :],
                                                    start=False, stop=True, skip_group_check=True)
                    last.then_inc(sum_done, 1)

            @block.scalar
            def _(act):
                with act.Fori(0, NC) as c:
                    act.wait_ge(trans_done, c * 2 + 1)
                    nc.scalar.activation(hT[:, 0, :], bank[0][:], ACT.Identity, bias=s["modc"][:, 8:9], scale=s["modc"][:, 10:11]).then_inc(hT_act, 1)
                    for t in range(TILES):
                        act.wait_ge(kv_proj, c * 4 + t + 1)
                        act.wait_ge(sum_done, c + PRIMED)
                        act.wait_ge(neg_ready, c * 6 + t + 1)
                        nc.scalar.activation(vt[:, t, :, 0:P], bank[2 + t][:, D:2 * D].rearrange("p (h n) -> p h n", h=KH), ACT.Copy).then_inc(v_ready, 1)
                        nc.scalar.activation(kneg[:, t, :], kneg[:, t, :], ACT.Exp).then_inc(exp_ready, 1)
                    for h in range(KH):
                        act.wait_ge(neg_ready, c * 6 + 4 + h + 1)
                        nc.scalar.activation(qneg[:, h, :], qneg[:, h, :], ACT.Exp).then_inc(exp_ready, 1)

            @block.vector
            def _(v):
                v.sem_inc(qf_ready, PRIMED)
                v.sem_inc(kf_ready, PRIMED)
                with v.Fori(0, NC) as c:
                    for t in range(TILES):
                        last = nc.vector.bn_stats(stats[:, t, :], X[:, c, t, :])
                    last.then_inc(dve_seq, 1)
                    wait_first(v, dve_seq, c + 1)
                    for t in range(TILES):
                        last = nc.vector.bn_aggr(mv[:, t, :], stats[:, t, :])
                    last.then_inc(stats_ready, 1)
                    v.wait_ge(stats_ready, c + 1)
                    v.wait_ge(rstd_ready, c + 1)
                    for t in range(TILES):
                        last = nc.vector.tensor_scalar(xh[:, t, :], X[:, c, t, :], mv[:, t, 0:1], rstd[:, t:t + 1], ALU.subtract, ALU.mult)
                    last.then_inc(xhat_ready, 1)
                    v.wait_ge(trans_done, c * 2 + 2)
                    nc.vector.tensor_scalar(hT[:, 1, :], bank[1][:], s["modc"][:, 11:12], s["modc"][:, 9:10], ALU.mult, ALU.add).then_inc(hT_dve, 1)
                    for t in range(TILES):
                        v.wait_ge(kv_proj, c * 4 + t + 1)
                        v.wait_ge(kf_ready, c * 4 + PRIMED)
                        nc.vector.tensor_scalar(kneg[:, t, :], bank[2 + t][:, 0:D], 0.0, None, ALU.min).then_inc(neg_ready, 1)
                    for h in range(KH):
                        v.wait_ge(q_proj, c * 2 + h + 1)
                        nc.vector.tensor_scalar(qneg[:, h, :], bank[h][:], 0.0, None, ALU.min).then_inc(neg_ready, 1)
                    v.wait_ge(sum_done, c + PRIMED)
                    for t in range(TILES):
                        v.wait_ge(exp_ready, c * 6 + t + 1)
                        v.wait_ge(v_ready, c * 4 + t + 1)
                        nc.vector.scalar_tensor_tensor(kf[:, t, :], bank[2 + t][:, 0:D], 0.0, kneg[:, t, :], ALU.max, ALU.add).then_inc(kf_ready, 1)
                    for h in range(KH):
                        v.wait_ge(exp_ready, c * 6 + 4 + h + 1)
                        nc.vector.scalar_tensor_tensor(s["qfT"][:, c, h, :], bank[h][:], 0.0, qneg[:, h, :], ALU.max, ALU.add).then_inc(qf_ready, 1)
                v.wait_ge(sum_done, NC + PRIMED)
                for h in range(KH):
                    nc.vector.tensor_tensor(s["kvb"][:, h, :], bank[6 + h][:, 0:P], same_head[:], ALU.mult)
                    nc.vector.tensor_scalar(s["ksb"][:, h, :], same_head[:], bank[6 + h][:, P:P + 1], None, ALU.mult)


def lin_out(nc, d, s):
    with ExitStack() as ctx:
        sb = lambda n, sh, dt=F32: ctx.enter_context(nc.sbuf_tensor("lo_" + n, sh, dt))
        sem = lambda n: ctx.enter_context(nc.semaphore("lo_" + n))
        bank = [ctx.enter_context(nc.psum_tensor(f"lo_ps{i}", [P, 512], F32)) for i in range(8)]
        wqkv = sb("wqkv", [P, KH, 3 * D])
        qkw2 = sb("qkw2", [P, 2, HD])
        qkw = sb("qkw", [P, HD])
        nw = sb("nw", [P, 2, KH])
        stats = sb("stats", [P, TILES, 6])
        mv = sb("mv", [P, TILES, 2])
        rstd = sb("rstd", [P, TILES])
        ssq = sb("ssq", [P, TILES])
        rms = sb("rms", [P, TILES])
        halfneg = sb("halfneg", [P, TILES])
        den = sb("den", [P, KH, CH])
        oT = sb("oT", [P, KH, CH])
        xh = sb("xh", [P, TILES, D])
        hT = den
        sq = oT[:].rearrange("p a b -> p (a b)").rearrange("p (a b) -> p a b", b=D)
        headsq = sb("headsq", [P, TILES, 2 * HEADS])
        headr = sb("headr", [P, TILES, 2 * HEADS])
        kn2 = sb("kn2", [P, HEADS])
        kq2 = sb("kq2", [P, TILES, HEADS])
        kmax = sb("kmax", [P, HEADS])
        (loaded, const_set, bo_added, num_done, den_ready, oT_ready, out_done, x3_ready, x3_stored, stats_ready, rstd_ready,
         h4_ready, ssq_ready, rms_ready, xhat_ready, trans_done, hT_act, hT_dve, qk_proj, v_proj, v_ready, sq_ready, headsq_ready,
         headv_ready, headr_ready, qk_ready, q_weighed, dve_seq, pool_seq, square_done, x4_ready) = (sem(x) for x in
            ("loaded", "const_set", "bo_added", "num_done", "den_ready", "oT_ready", "out_done", "x3_ready", "x3_stored",
             "stats_ready", "rstd_ready", "h4_ready", "ssq_ready", "rms_ready", "xhat_ready", "trans_done", "hT_act", "hT_dve",
             "qk_proj", "v_proj", "v_ready", "sq_ready", "headsq_ready", "headv_ready", "headr_ready", "qk_ready", "q_weighed", "dve_seq",
             "pool_seq", "square_done", "x4_ready"))
        X = s["xres"]
        with nc.Block() as block:
            @block.sync
            def _(sp):
                for dst, src in ((wqkv, d["wqkv"]), (qkw2, d["qkw"]), (nw, d["nw"])):
                    sp.dma_start(dst[:], src).then_inc(loaded, 16)
                x3 = d["x3"].rearrange("(c t p) n -> c p t n", t=TILES, p=P)
                with sp.Fori(0, NC) as c:
                    sp.wait_ge(x3_ready, c * 2 + 2)
                    sp.dma_start(x3[c], X[:, c]).then_inc(x3_stored, 16)

            @block.gpsimd
            def _(g):
                g.memset(halfneg[:], -0.5).then_inc(const_set, 1)
                g.memset(s["vx"][:].rearrange("p c t n -> p (c t) n").rearrange("p a (h n) -> p a h n", h=HEADS)[:, :, :, HD], 1.0).then_inc(const_set, 1)
                g.memset(kn2[:], 0.0).then_inc(const_set, 1)
                g.wait_ge(loaded, 48)
                nc.gpsimd.tensor_tensor(qkw[:], qkw2[:, 0, :], qkw2[:, 1, :], ALU.mult).then_inc(const_set, 1)
                g.wait_ge(const_set, 4)
                nc.gpsimd.tensor_scalar(qkw[:], qkw[:], HD ** -0.5, None, ALU.mult).then_inc(const_set, 1)
                g.wait_ge(const_set, 5)
                with g.Fori(0, NC) as c:
                    seq = Tally(c * 2)
                    nc.gpsimd.tensor_tensor(X[:, c], X[:, c], s["bo1"][:].unsqueeze(1).to_broadcast([P, TILES, D]), ALU.add).then_inc(bo_added, 1)
                    wait_first(g, stats_ready, c + 1)
                    nc.gpsimd.tensor_scalar(rstd[:], mv[:, :, 1], 1e-5, None, ALU.add).then_inc(pool_seq, 1)
                    wait_first(g, pool_seq, seq.up())
                    nc.gpsimd.tensor_tensor(rstd[:], rstd[:], halfneg[:, 0:TILES], ALU.pow).then_inc(rstd_ready, 1)
                    wait_first(g, ssq_ready, c + 1)
                    nc.gpsimd.tensor_scalar(rms[:], ssq[:], 1.0 / D, RMS_EPS, ALU.mult, ALU.add).then_inc(pool_seq, 1)
                    wait_first(g, pool_seq, seq.up())
                    nc.gpsimd.tensor_tensor(rms[:], rms[:], halfneg[:, 0:TILES], ALU.pow).then_inc(rms_ready, 1)
                    wait_first(g, headsq_ready, c * 4 + 4)
                    nc.gpsimd.tensor_scalar(merged(headr[:]), merged(headsq[:]), 1.0 / HD, RMS_EPS, ALU.mult, ALU.add).then_inc(headv_ready, 1)
                    for t in range(TILES):
                        wait_first(g, qk_ready, c * 4 + t + 1 + PRIMED)
                        q = s["qk"][:, c, t, 0:D].rearrange("p (h n) -> p h n", h=HEADS)
                        nc.gpsimd.tensor_tensor(q, q, qkw[:].unsqueeze(1).to_broadcast([P, HEADS, HD]), ALU.mult).then_inc(q_weighed, 1)

            @block.tensor
            def _(pe):
                pe.wait_ge(loaded, 48)
                with pe.Fori(0, NC) as c:
                    pe.wait_ge(qk_ready, c * 4 + PRIMED)
                    for h in range(KH):
                        nc.tensor.matmul(bank[h][:], s["kvb"][:, h, :], s["qfT"][:, c, h, :], start=True, stop=True)
                        nc.tensor.matmul(bank[2 + h][:], s["ksb"][:, h, :], s["qfT"][:, c, h, :], start=True, stop=True).then_inc(num_done, 1)
                    pe.wait_ge(v_ready, c * 2 + PRIMED)
                    pe.wait_ge(oT_ready, c * 2 + 2)
                    for t in range(TILES):
                        for k in range(KH):
                            last = nc.tensor.matmul(bank[4 + t // 2][:, (t % 2) * D:(t % 2 + 1) * D], oT[:, k, t * P:(t + 1) * P], s["wo1"][:, k, :],
                                                    start=k == 0, stop=k == KH - 1)
                        if t % 2:
                            last.then_inc(out_done, 1)
                    pe.wait_ge(xhat_ready, c * 2 + 2)
                    for h in range(KH):
                        for t in range(TILES):
                            last = nc.tensor.transpose(bank[6 + h][:, t * P:(t + 1) * P], xh[:, t, h * P:(h + 1) * P], s["ident"][:])
                        last.then_inc(trans_done, 1)
                    pe.wait_ge(hT_act, c + 1)
                    pe.wait_ge(hT_dve, c + 1)
                    for t in range(TILES):
                        for k in range(KH):
                            last = nc.tensor.matmul(bank[t][:], hT[:, k, t * P:(t + 1) * P], wqkv[:, k, 0:2 * D], start=k == 0, stop=k == KH - 1)
                        last.then_inc(qk_proj, 1)
                    for t in range(TILES):
                        for k in range(KH):
                            last = nc.tensor.matmul(bank[4 + t // 2][:, (t % 2) * D:(t % 2 + 1) * D], hT[:, k, t * P:(t + 1) * P],
                                                    wqkv[:, k, 2 * D:3 * D], start=k == 0, stop=k == KH - 1)
                        if t % 2:
                            last.then_inc(v_proj, 1)

            @block.scalar
            def _(act):
                act.sem_inc(v_ready, PRIMED)
                act.wait_ge(const_set, 3)
                with act.Fori(0, NC) as c:
                    for h in range(KH):
                        act.wait_ge(num_done, c * 2 + h + 1)
                        nc.scalar.activation(den[:, h, :], bank[2 + h][:], ACT.Copy, bias=1e-6).then_inc(den_ready, 1)
                    act.wait_ge(h4_ready, c + 1)
                    for t in range(TILES):
                        last = nc.scalar.activation(sq[:, t, :], X[:, c, t, :], ACT.Square, accum_out=ssq[:, t:t + 1])
                    last.then_inc(ssq_ready, 1)
                    act.wait_ge(trans_done, c * 2 + 1)
                    nc.scalar.activation(hT[:, 0, :], bank[6][:], ACT.Identity, scale=nw[:, 0, 0:1]).then_inc(hT_act, 1)
                    for t in range(TILES):
                        act.wait_ge(qk_proj, c * 4 + t + 1)
                        if t >= 2:
                            act.wait_ge(headsq_ready, c * 4 + t - 1)
                        nc.scalar.activation(merged(sq[:, 2 * (t % 2):2 * (t % 2) + 2, :]), bank[t][:], ACT.Square).then_inc(square_done, 1)
                    act.wait_ge(headv_ready, c + 1)
                    nc.scalar.activation(headr[:], headr[:], ACT.Sqrt).then_inc(headr_ready, 1)
                    for p in range(2):
                        act.wait_ge(v_proj, c * 2 + p + 1)
                        dst = s["vx"][:, c, 2 * p:2 * p + 2, :].rearrange("p t (h n) -> p (t h) n", h=HEADS)[:, :, 0:HD]
                        nc.scalar.activation(dst, bank[4 + p][:].rearrange("p (a n) -> p a n", n=HD), ACT.Copy).then_inc(v_ready, 1)

            @block.vector
            def _(v):
                v.sem_inc(qk_ready, PRIMED)
                v.wait_ge(const_set, 3)
                v.wait_ge(loaded, 48)
                with v.Fori(0, NC) as c:
                    seq = Tally(c * 9)
                    for h in range(KH):
                        v.wait_ge(den_ready, c * 2 + h + 1)
                        nc.vector.reciprocal(den[:, h, :], den[:, h, :]).then_inc(dve_seq, 1)
                        v.wait_ge(dve_seq, seq.up())
                        nc.vector.tensor_tensor(oT[:, h, :], bank[h][:], den[:, h, :], ALU.mult).then_inc(oT_ready, 1)
                    v.wait_ge(bo_added, c + 1)
                    for p in range(2):
                        v.wait_ge(out_done, c * 2 + p + 1)
                        nc.vector.tensor_tensor(merged(X[:, c, 2 * p:2 * p + 2, :]), merged(X[:, c, 2 * p:2 * p + 2, :]), bank[4 + p][:],
                                                ALU.add).then_inc(x3_ready, 1)
                    wait_first(v, x3_ready, c * 2 + 2)
                    for t in range(TILES):
                        last = nc.vector.bn_stats(stats[:, t, :], X[:, c, t, :])
                    last.then_inc(dve_seq, 1)
                    wait_first(v, dve_seq, seq.up())
                    for t in range(TILES):
                        last = nc.vector.bn_aggr(mv[:, t, :], stats[:, t, :])
                    last.then_inc(stats_ready, 1)
                    v.wait_ge(stats_ready, c + 1)
                    v.wait_ge(rstd_ready, c + 1)
                    for t in range(TILES):
                        last = nc.vector.tensor_scalar(xh[:, t, :], X[:, c, t, :], mv[:, t, 0:1], rstd[:, t:t + 1], ALU.subtract, ALU.mult)
                    last.then_inc(xhat_ready, 1)
                    v.wait_ge(xhat_ready, c * 2 + 1)
                    wide = lambda ap: ap.unsqueeze(1).to_broadcast([P, TILES, D])
                    nc.vector.tensor_tensor(xh[:], xh[:], wide(s["cb1"][:]), ALU.mult).then_inc(dve_seq, 1)
                    v.wait_ge(dve_seq, seq.up())
                    v.wait_ge(x3_stored, c * 16 + 16)
                    nc.vector.tensor_tensor(X[:, c], xh[:], wide(s["sb1"][:]), ALU.add).then_inc(h4_ready, 1)
                    v.wait_ge(h4_ready, c + 1)
                    v.wait_ge(rms_ready, c + 1)
                    for t in range(TILES):
                        last = nc.vector.tensor_scalar(xh[:, t, :], X[:, c, t, :], rms[:, t:t + 1], None, ALU.mult)
                    last.then_inc(xhat_ready, 1)
                    v.wait_ge(trans_done, c * 2 + 2)
                    nc.vector.tensor_scalar(hT[:, 1, :], bank[7][:], nw[:, 0, 1:2], None, ALU.mult).then_inc(hT_dve, 1)
                    for t in range(TILES):
                        v.wait_ge(square_done, c * 4 + t + 1)
                        nc.vector.tensor_reduce(headsq[:, t, :], merged(sq[:, 2 * (t % 2):2 * (t % 2) + 2, :]).rearrange("p (h n) -> p h n", n=HD),
                                                AX, ALU.add).then_inc(headsq_ready, 1)
                    v.wait_ge(headr_ready, c + 1)
                    nc.vector.reciprocal(headr[:], headr[:]).then_inc(dve_seq, 1)
                    v.wait_ge(dve_seq, seq.up())
                    for t in range(TILES):
                        nc.vector.tensor_tensor(s["qk"][:, c, t, :].rearrange("p (h n) -> p h n", n=HD), bank[t][:].rearrange("p (h n) -> p h n", n=HD),
                                                headr[:, t, :].unsqueeze(2).to_broadcast([P, 2 * HEADS, HD]), ALU.mult).then_inc(qk_ready, 1)
                    nc.vector.tensor_tensor(kq2[:], headsq[:, :, HEADS:], headr[:, :, HEADS:], ALU.mult).then_inc(dve_seq, 1)
                    v.wait_ge(dve_seq, seq.up())
                    nc.vector.tensor_tensor(kq2[:], kq2[:], headr[:, :, HEADS:], ALU.mult).then_inc(dve_seq, 1)
                    v.wait_ge(dve_seq, seq.up())
                    nc.vector.tensor_reduce(kmax[:], kq2[:].rearrange("p t h -> p h t"), AX, ALU.max).then_inc(dve_seq, 1)
                    v.wait_ge(dve_seq, seq.up())
                    nc.vector.tensor_tensor(kn2[:], kn2[:], kmax[:], ALU.max).then_inc(dve_seq, 1)
                    v.wait_ge(dve_seq, seq.up())
                    assert seq.n == 9, seq.n
                nc.vector.tensor_copy(s["knorm"][:], kn2[:])


RMS_EPS = 1.1920929e-07


def shifts(nc, d, s):
    TT = NC * TILES
    with ExitStack() as ctx:
        sb = lambda n, sh, dt=F32: ctx.enter_context(nc.sbuf_tensor("sh_" + n, sh, dt))
        sem = lambda n: ctx.enter_context(nc.semaphore("sh_" + n))
        ps = [ctx.enter_context(nc.psum_tensor(f"sh_ps{i}", [P, 512], F32)) for i in range(2)]
        prod = sb("prod", [P, 2, TILES, D])
        own = sb("own", [P, NC, TILES, HEADS])
        qn2 = sb("qn2", [P, NC, TILES, HEADS])
        km = sb("km", [HEADS, 1])
        kdiag = sb("kdiag", [HEADS, HEADS])
        ones = sb("ones", [HEADS, P])
        ones_set, km_t, kdiag_ready, km_all, upper2, upper, seq, done = (sem(x) for x in
            ("ones_set", "km_t", "kdiag_ready", "km_all", "upper2", "upper", "seq", "done"))
        prod_ready = sem("prod_ready")
        with nc.Block() as block:
            @block.gpsimd
            def _(g):
                g.memset(ones[:], 1.0).then_inc(ones_set, 1)

            @block.tensor
            def _(pe):
                nc.tensor.transpose(ps[0][0:HEADS, 0:P], s["knorm"][:], s["ident"][:]).then_inc(km_t, 1)
                pe.wait_ge(kdiag_ready, 1)
                pe.wait_ge(ones_set, 1)
                nc.tensor.matmul(ps[1][:, 0:HEADS], ones[:], kdiag[:], start=True, stop=True).then_inc(km_all, 1)

            @block.scalar
            def _(act):
                act.wait_ge(upper2, 1)
                nc.scalar.activation(qn2[:], qn2[:], ACT.Sqrt).then_inc(upper, 1)

            @block.vector
            def _(v):
                v.sem_inc(done, PRIMED)
                v.wait_ge(km_t, 1)
                nc.vector.tensor_reduce(km[:], ps[0][0:HEADS, 0:P], AX, ALU.max).then_inc(seq, 1)
                v.wait_ge(seq, 1)
                nc.vector.tensor_scalar(kdiag[:], s["ident"][0:HEADS, 0:HEADS], km[:], None, ALU.mult).then_inc(kdiag_ready, 1)
                by_head = lambda ap: ap.rearrange("p t (h n) -> p (t h) n", n=HD)
                with v.Fori(0, NC) as c:
                    v.wait_ge(done, c * 2 + PRIMED)
                    for i in range(2):
                        nc.vector.tensor_tensor(prod[:, i], s["qk"][:, c, :, 0:D], s["qk"][:, c, :, (1 - i) * D:(2 - i) * D], ALU.mult).then_inc(prod_ready, 1)
                    for i, dst in enumerate((own, qn2)):
                        v.wait_ge(prod_ready, c * 2 + i + 1)
                        nc.vector.tensor_reduce(merged(dst[:, c]), by_head(prod[:, i]), AX, ALU.add).then_inc(done, 1)
                v.wait_ge(done, NC * 2 + PRIMED)
                v.wait_ge(km_all, 1)
                every = lambda t: t[:].rearrange("p c t h -> p (c t) h")
                nc.vector.tensor_tensor(every(qn2), every(qn2), ps[1][:, 0:HEADS].unsqueeze(1).to_broadcast([P, TT, HEADS]), ALU.mult).then_inc(upper2, 1)
                nc.vector.tensor_scalar(own[:], own[:], -1.0, None, ALU.mult).then_inc(seq, 1)
                v.wait_ge(upper, 1)
                nc.vector.tensor_scalar(qn2[:], qn2[:], -1.0, 80.0, ALU.mult, ALU.add).then_inc(seq, 1)
                v.wait_ge(seq, 3)
                nc.vector.tensor_tensor(own[:], own[:], qn2[:], ALU.min).then_inc(seq, 1)
                v.wait_ge(seq, 4)
                sh = s["shift"][:].rearrange("p c t h k -> p (c t h) k")
                flat = lambda t: t[:].rearrange("p c t h -> p (c t h)")
                nc.vector.tensor_copy(sh[:, :, 0], flat(own)).then_inc(seq, 1)
                v.wait_ge(seq, 5)
                nc.vector.tensor_tensor(flat(own), flat(own), sh[:, :, 0], ALU.subtract).then_inc(seq, 1)
                v.wait_ge(seq, 6)
                nc.vector.tensor_copy(sh[:, :, 1], flat(own)).then_inc(seq, 1)
                v.wait_ge(seq, 7)
                nc.vector.tensor_tensor(sh[:, :, 2], flat(own), sh[:, :, 1], ALU.subtract)


def softmax(nc, d, s):
    PER_G = sum(TILES * (c + 1) for c in range(NC))
    before = lambda c: 2 * c * (c + 1)
    assert before(NC) == PER_G
    VW = HD + 1
    order = [("Q0", 0), ("Q1", 0), ("K0", 0), ("K1", 0)]
    for c in range(NC):
        order += [("D", c - 1)] if c else []
        order += [("Q0", c + 1), ("Q1", c + 1), ("K0", c + 1), ("K1", c + 1)] if c + 1 < NC else []
        order += [("A0", c - 1), ("A1", c - 1)] if c else []
    order += [("D", NC - 1), ("A0", NC - 1), ("A1", NC - 1)]
    number = {job: i for i, job in enumerate(order)}
    JOBS = len(order)
    assert JOBS % 2 == 0
    with ExitStack() as ctx:
        sb = lambda n, sh, dt=F32: ctx.enter_context(nc.sbuf_tensor("sm_" + n, sh, dt))
        sem = lambda n: ctx.enter_context(nc.semaphore("sm_" + n))
        ps_s = [ctx.enter_context(nc.psum_tensor(f"sm_s{i}", [P, 2, CH], F32)) for i in range(2)]
        ps_o = [ctx.enter_context(nc.psum_tensor(f"sm_o{i}", [P, CH], F32)) for i in range(2)]
        side = [ctx.enter_context(nc.psum_tensor(f"sm_j{i}", [P, 512], F32)) for i in range(2)]
        kst = sb("kst", [P, GH, NC, CH], BF16)
        qst = sb("qst", [P, 2, GH, CH], BF16)
        stage = [sb("stage_q", [P, TILES, GH, ROWS], BF16), sb("stage_k", [P, TILES, GH, ROWS], BF16)]
        part_h = sb("part_h", [P, TILES * GH, HD], BF16)
        part_m = sb("part_m", [P, TILES * GH, HD], BF16)
        rest = sb("rest", [P, TILES * GH, HD])
        prob = sb("prob", [P, 2, GH, CH])
        vst = sb("vst", [P, TILES, GH * VW])
        o_sb = sb("o_sb", [P, CH])
        o_n = sb("o_n", [P, CH])
        zero = sb("zero", [P, P], BF16)
        identb = sb("identb", [P, P], BF16)
        den_row = sb("den_row", [P, P])
        wo_pad = sb("wo_pad", [P, GROUPS, KEEP])
        (loaded, zero_set, const_set, split_seq, staged, side_done, side_read, s_done, exp_done, masked, v_staged, pv_done,
         o_read, on_ready, rec_ready) = (sem(x) for x in
            ("loaded", "zero_set", "const_set", "split_seq", "staged", "side_done", "side_read", "s_done", "exp_done", "masked",
             "v_staged", "pv_done", "o_read", "on_ready", "rec_ready"))
        X = s["xres"]
        qk = s["qk"][:].rearrange("p c t (w g n) -> p c t w g n", w=2, g=GROUPS)
        vx = s["vx"][:].rearrange("p c t (g n) -> p c t g n", g=GROUPS)
        with nc.Block() as block:
            @block.sync
            def _(sp):
                for dst, src in ((den_row, d["den_row"]), (wo_pad, d["wo_pad"])):
                    sp.dma_start(dst[:], src).then_inc(loaded, 16)

            @block.gpsimd
            def _(g_):
                g_.memset(zero[:], 0.0).then_inc(zero_set, 1)
                g_.memset(stage[1][:, :, :, SPLIT:ROWS], 1.0).then_inc(const_set, 1)
                with g_.Fori(0, GROUPS) as g:
                    for c in range(NC):
                        n0 = g * PER_G + before(c)

                        def stage_v(n, kc, j):
                            wait_first(g_, pv_done, (g * PER_G if c == 0 else n - 3) + PRIMED, met=zero_set)
                            nc.gpsimd.tensor_copy(vst[:, j, :], vx[:, kc, j, g, :]).then_inc(v_staged, 1)

                        if c:
                            with g_.Fori(0, c) as kc:
                                for j in range(TILES):
                                    stage_v(n0 + kc * TILES + j, kc, j)
                        for j in range(TILES):
                            stage_v(n0 + c * TILES + j, c, j)
                        for j in range(TILES):
                            n = n0 + c * TILES + j
                            wait_first(g_, exp_done, n * 2 + 2 + PRIMED)
                            blk = prob[:, j % 2, :, j * P:(j + 1) * P]
                            nc.gpsimd.affine_select(out=blk, in_=blk, compare_op=ALU.is_ge, fill=0.0, base=0,
                                                    pattern=[[0, GH], [1, P]], channel_multiplier=-1).then_inc(masked, 1)

            @block.tensor
            def _(pe):
                pe.sem_inc(pv_done, PRIMED)
                pe.sem_inc(side_done, PRIMED)
                pe.wait_ge(loaded, 32)
                pe.wait_ge(zero_set, 1)
                pe.wait_ge(const_set, 2)

                with pe.Fori(0, GROUPS) as g:
                    def side_job(kind, c):
                        i = number[kind, c]
                        b = side[i % 2]
                        pe.wait_ge(side_read, g * JOBS + max(i - 1, 0) + PRIMED)
                        if kind in ("Q0", "Q1", "K0", "K1"):
                            w, p = "QK".index(kind[0]), int(kind[1])
                            pe.wait_ge(staged, (g * NC + c) * 2 + w + 1)
                            for t in range(2):
                                for h in range(GH):
                                    m = (t * GH + h) * P
                                    last = nc.tensor.transpose(b[:].bitcast(BF16)[0:ROWS, m:m + P], stage[w][:, 2 * p + t, h, 0:ROWS], identb[:])
                        elif kind == "D":
                            pe.wait_ge(o_read, g * NC + c + 1 + PRIMED)
                            last = nc.tensor.matmul(b[:], den_row[:], o_sb[:], start=True, stop=True)
                        else:
                            pe.wait_ge(on_ready, g * NC + c + 1 + PRIMED)
                            for t in range(2):
                                col = (2 * int(kind[1]) + t) * P
                                last = nc.tensor.matmul(b[:, t * KEEP:(t + 1) * KEEP], o_n[:, col:col + P], wo_pad[:, g, :], start=True, stop=True)
                        last.then_inc(side_done, 1)

                    def scores(n, c, kc, j, q0, first=False):
                        for pair in range(2):
                            pe.wait_ge(exp_done, (n * 2 if first else n * 2 - 1 + pair) + PRIMED)
                            for h in range(2):
                                hh = 2 * pair + h
                                last = nc.tensor.matmul(ps_s[pair][:, h, q0:], kst[0:ROWS, hh, kc, j * P:(j + 1) * P],
                                                        qst[0:ROWS, c % 2, hh, q0:], start=True, stop=True)
                            last.then_inc(s_done, 1)

                    def values(n, c, j, q0, diagonal=False):
                        pe.wait_ge(exp_done, n * 2 + 2 + PRIMED)
                        pe.wait_ge(v_staged, n + 1)
                        if diagonal:
                            pe.wait_ge(masked, (g * NC + c) * TILES + j + 1)
                        for h in range(GH):
                            last = nc.tensor.matmul(ps_o[c % 2][32 * h:32 * h + VW, q0:], vst[:, j, h * VW:(h + 1) * VW],
                                                    prob[:, j % 2, h, q0:], start=False, stop=True, skip_group_check=True)
                        last.then_inc(pv_done, 1)

                    for job in order[:4]:
                        side_job(*job)
                    for c in range(NC):
                        n0 = g * PER_G + before(c)
                        pe.wait_ge(o_read, g * NC + max(c - 1, 0) + PRIMED)
                        nc.tensor.matmul(ps_o[c % 2][:].rearrange("p (t n) -> p t n", t=TILES), zero[:], zero[:].unsqueeze(1).to_broadcast([P, TILES, P]), start=True, stop=False, skip_group_check=True)
                        if c == 0:
                            pe.wait_ge(side_read, g * JOBS + 4 + PRIMED)
                            scores(n0, 0, 0, 0, 0, first=True)
                        if c:
                            with pe.Fori(0, c) as kc:
                                for j in range(TILES):
                                    n = n0 + kc * TILES + j
                                    scores(n + 1, c, kc if j < 3 else kc + 1, (j + 1) % TILES, 0)
                                    values(n, c, j, 0)
                        for j in range(TILES):
                            n = n0 + c * TILES + j
                            if j < 3:
                                scores(n + 1, c, c, j + 1, (j + 1) * P)
                            elif c + 1 < NC:
                                pe.wait_ge(side_read, g * JOBS + number["K1", c + 1] + 1 + PRIMED)
                                scores(n + 1, c + 1, 0, 0, 0)
                            values(n, c, j, j * P, diagonal=True)
                            if j == 0:
                                if c:
                                    side_job("D", c - 1)
                                if c + 1 < NC:
                                    side_job("Q0", c + 1)
                                    side_job("Q1", c + 1)
                            if j == 1:
                                if c + 1 < NC:
                                    side_job("K0", c + 1)
                                    side_job("K1", c + 1)
                                if c:
                                    side_job("A0", c - 1)
                                    side_job("A1", c - 1)
                    for job in order[-3:]:
                        side_job(*job)

            @block.scalar
            def _(act):
                act.sem_inc(exp_done, PRIMED)
                with act.Fori(0, GROUPS) as g:
                    for c in range(NC):
                        n0 = g * PER_G + before(c)

                        def exps(n, j, q0, wait_pv=True):
                            for pair in range(2):
                                act.wait_ge(s_done, n * 2 + pair + 1)
                                if pair == 0:
                                    act.wait_ge(pv_done, (n - 1 if wait_pv else g * PER_G) + PRIMED)
                                nc.scalar.activation(prob[:, j % 2, 2 * pair:2 * pair + 2, q0:], ps_s[pair][:, :, q0:], ACT.Exp).then_inc(exp_done, 1)

                        if c:
                            with act.Fori(0, c) as kc:
                                for j in range(TILES):
                                    exps(n0 + kc * TILES + j, j, 0)
                        for j in range(TILES):
                            exps(n0 + c * TILES + j, j, j * P, wait_pv=c > 0 or j > 0)

            @block.vector
            def _(v):
                v.sem_inc(side_read, PRIMED)
                v.sem_inc(o_read, PRIMED)
                v.sem_inc(on_ready, PRIMED)
                nc.vector.tensor_copy(identb[:], s["ident"][:]).then_inc(const_set, 1)
                with v.Fori(0, GROUPS) as g:
                    seq = Tally(g * NC * 6)

                    def split(w, c):
                        src = qk[:, c, :, w, g, :]
                        slots = stage[w][:, :, :, 0:SPLIT].rearrange("p t h (k n) -> p (t h) k n", n=HD)
                        small = lambda t: t[:].rearrange("p (t h) n -> p t (h n)", t=TILES)
                        copies = lambda t, k: t[:].unsqueeze(2).to_broadcast([P, TILES * GH, k, HD])
                        nc.vector.tensor_copy(small(part_h), src).then_inc(split_seq, 1)
                        v.wait_ge(split_seq, seq.up())
                        nc.vector.tensor_tensor(small(rest), src, small(part_h), ALU.subtract).then_inc(split_seq, 1)
                        v.wait_ge(split_seq, seq.up())
                        nc.vector.tensor_copy(part_m[:], rest[:]).then_inc(split_seq, 1)
                        v.wait_ge(split_seq, seq.up())
                        if c:
                            v.wait_ge(side_done, g * JOBS + number["QK"[w] + "1", c - 1] + 1 + PRIMED)
                        else:
                            v.wait_ge(side_done, g * JOBS + PRIMED)
                        if w == 0:
                            nc.vector.tensor_copy(slots[:, :, 1:4, :], copies(part_h, 3))
                            nc.vector.tensor_copy(slots[:, :, 0:5:4, :], copies(part_m, 2))
                            nc.vector.tensor_copy(stage[0][:, :, :, SPLIT:ROWS], s["shift"][:, c, :, :, :].rearrange("p t (g h) k -> p g t h k", g=GROUPS)[:, g])
                        else:
                            nc.vector.tensor_copy(slots[:, :, 3:6, :], copies(part_h, 3))
                            nc.vector.tensor_copy(slots[:, :, 0:2, :], copies(part_m, 2))
                        nc.vector.tensor_tensor(slots[:, :, 5 if w == 0 else 2, :], rest[:], part_m[:], ALU.subtract).then_inc(staged, 1)
                        v.wait_ge(staged, (g * NC + c) * 2 + w + 1)

                    def read_side(kind, c):
                        i = number[kind, c]
                        b = side[i % 2]
                        v.wait_ge(side_done, g * JOBS + i + 1 + PRIMED)
                        p = int(kind[1:] or 0)
                        if kind[0] in "QK":
                            src = b[:].bitcast(BF16)[0:ROWS, :].rearrange("p (t h n) -> p t h n", t=2, h=GH)
                            dst = (qst[:, c % 2] if kind[0] == "Q" else kst[:, :, c]).rearrange("p h (t n) -> p t h n", t=TILES)
                            nc.vector.tensor_copy(dst[0:ROWS, 2 * p:2 * p + 2], src).then_inc(side_read, 1)
                        elif kind == "D":
                            nc.vector.reciprocal(o_n[:], b[:]).then_inc(side_read, 1)
                            v.wait_ge(side_read, g * JOBS + i + 1 + PRIMED)
                            nc.vector.tensor_tensor(o_n[:], o_n[:], o_sb[:], ALU.mult).then_inc(on_ready, 1)
                        else:
                            x = X[:, c, 2 * p:2 * p + 2, MASKED:]
                            nc.vector.tensor_tensor(x, x, b[:, 0:2 * KEEP].rearrange("p (t n) -> p t n", t=2), ALU.add).then_inc(side_read, 1)

                    def read_out(c):
                        v.wait_ge(pv_done, g * PER_G + before(c + 1) + PRIMED)
                        v.wait_ge(on_ready, g * NC + c + PRIMED)
                        nc.vector.tensor_copy(o_sb[:], ps_o[c % 2][:]).then_inc(o_read, 1)

                    split(0, 0)
                    split(1, 0)
                    for job in order[:4]:
                        read_side(*job)
                    for c in range(NC):
                        if c:
                            read_out(c - 1)
                        if c + 1 < NC:
                            split(0, c + 1)
                            split(1, c + 1)
                        for kind, cc in order:
                            if (kind in ("D", "A0", "A1") and cc == c - 1) or (kind[0] in "QK" and cc == c + 1):
                                read_side(kind, cc)
                    read_out(NC - 1)
                    for job in order[-3:]:
                        read_side(*job)
                    assert seq.n == 6 * NC


def ffn1(nc, d, s):
    HT = H1 // P
    stages = [("e2_l1", KH, HT, "hT", "gelu", "ha"), ("e0_up", KH, HT, "hT", "gelu", "hb"),
              ("e2_l2", HT, HT, "ha", "gelu", "hc"), ("down", 0, "hb"),
              ("e3_down", KH, KH, "hT", "gelu", "hz"), ("e2_l3", HT, HT, "hc", "gelu", "ha"),
              ("e3_up", KH, HT, "hz", "gelu", "hb"), ("e1_w1", KH, HT, "hT", "silu", "hs"), ("down", 2, "ha"),
              ("e1_w2", KH, HT, "hT", "times", "hc"), ("down", 3, "hb"), ("down", 1, "hc")]
    jobs, of_stage = [], {}
    for st in stages:
        if st[0] != "down":
            of_stage[st[0]] = len(jobs)
            jobs += [(st, j) for j in range(st[2])]
    by_act = [st[4] != "times" for st, _ in jobs]
    JOBS, ACTS = len(jobs), sum(by_act)
    DVES = JOBS - ACTS
    last_writer = {}
    with ExitStack() as ctx:
        sb = lambda n, sh, dt=F32: ctx.enter_context(nc.sbuf_tensor("f1_" + n, sh, dt))
        sem = lambda n: ctx.enter_context(nc.semaphore("f1_" + n))
        up_ps = [ctx.enter_context(nc.psum_tensor(f"f1_up{i}", [P, CH], F32)) for i in range(4)]
        down_ps = [ctx.enter_context(nc.psum_tensor(f"f1_dn{i}", [P, 2, KEEP], F32)) for i in range(2)]
        tp = [ctx.enter_context(nc.psum_tensor(f"f1_tp{i}", [P, CH], F32)) for i in range(2)]
        w = {n: sb("w_" + n, list(d["m_" + n].shape)) for n in UPS}
        downs = sb("downs", [P, E1, HT, KEEP])
        wg = sb("wg", [P, KH, E1])
        nw = sb("nw", [P, 2, KH])
        iota = sb("iota", [P, E0])
        halfneg = sb("halfneg", [P, TILES])
        ssq, rms, mx, z = (sb(n, [P, TILES]) for n in ("ssq", "rms", "mx", "z"))
        junk = sb("junk", [P, TILES, D])
        xh = sb("xh", [P, TILES, D])
        x3 = sb("x3", [P, TILES, D])
        buf = dict(hT=sb("hT", [P, KH, CH]), ha=sb("ha", [P, HT, CH]), hb=sb("hb", [P, HT, CH]), hc=sb("hc", [P, HT, CH]),
                   hz=sb("hz", [P, KH, CH]), hs=sb("hs", [P, HT, CH]))
        hT = buf["hT"]
        lgs, notnan, log, pr = (sb(n, [P, TILES, E1]) for n in ("lgs", "notnan", "log", "pr"))
        probs = sb("probs", [P, TILES, 8])
        top = sb("top", [P, TILES, 8])
        idx = sb("idx", [P, TILES, 8], U32)
        idf = sb("idf", [P, TILES, 8])
        cw = sb("cw", [P, TILES, 2])
        eq = sb("eq", [P, 2, TILES, E1])
        we = sb("we", [P, TILES, E1])
        (small_loaded, loaded, const_set, x3_loaded, x3_used, base_ready, ssq_ready, rms_ready, xhat_ready, trans_done, hT_act, hT_dve,
         log_done, log_copied, shifted, exp_done, we_ready, up_done, act_read, dve_read, down_done, added, stored,
         dve_seq, pool_seq) = (sem(x) for x in
            ("small_loaded", "loaded", "const_set", "x3_loaded", "x3_used", "base_ready", "ssq_ready", "rms_ready", "xhat_ready", "trans_done",
             "hT_act", "hT_dve", "log_done", "log_copied", "shifted", "exp_done", "we_ready", "up_done", "act_read", "dve_read",
             "down_done", "added", "stored", "dve_seq", "pool_seq"))
        X = s["xres"]
        small = [(wg, d["wg1"]), (nw, d["nw"]), (iota, d["iota"])]
        large = [(w[st[0]], d["m_" + st[0]]) for st in stages if st[0] != "down"] + [(downs, d["downs"])]

        def read_by(c, u):
            if by_act[u]:
                return act_read, c * ACTS + sum(by_act[:u + 1])
            return dve_read, c * DVES + u + 1 - sum(by_act[:u + 1]) + PRIMED

        with nc.Block() as block:
            @block.sync
            def _(sp):
                for dst, src in small:
                    sp.dma_start(dst[:], src).then_inc(small_loaded, 16)
                for dst, src in large:
                    sp.dma_start(dst[:], src).then_inc(loaded, 16)
                x3_d = d["x3"].rearrange("(c t p) n -> c p t n", t=TILES, p=P)
                out_d = d["out"].rearrange("(c t p) n -> c p t n", t=TILES, p=P)
                with sp.Fori(0, NC) as c:
                    sp.wait_ge(x3_used, c + PRIMED)
                    sp.dma_start(x3[:], x3_d[c]).then_inc(x3_loaded, 16)
                    sp.wait_ge(added, (c + 1) * E1 * 2 + PRIMED)
                    sp.dma_start(out_d[c], X[:, c]).then_inc(stored, 16)
                sp.wait_ge(stored, NC * 16)

            @block.gpsimd
            def _(g):
                g.sem_inc(x3_used, PRIMED)
                g.memset(halfneg[:], -0.5).then_inc(const_set, 1)
                g.memset(probs[:], -1.0).then_inc(const_set, 1)
                g.wait_ge(const_set, 2)
                g.wait_ge(loaded, 16 * len(large))
                nc.gpsimd.tensor_tensor(downs[:].rearrange("p e k n -> p (e k) n"), downs[:].rearrange("p e k n -> p (e k) n"),
                                        s["gb1"][:, MASKED:].unsqueeze(1).to_broadcast([P, E1 * HT, KEEP]), ALU.mult).then_inc(const_set, 1)
                with g.Fori(0, NC) as c:
                    wait_first(g, ssq_ready, c + 1)
                    nc.gpsimd.tensor_scalar(rms[:], ssq[:], 1.0 / D, RMS_EPS, ALU.mult, ALU.add).then_inc(pool_seq, 1)
                    wait_first(g, pool_seq, c * 2 + 1)
                    nc.gpsimd.tensor_tensor(rms[:], rms[:], halfneg[:], ALU.pow).then_inc(rms_ready, 1)
                    wait_first(g, xhat_ready, c + 1)
                    nc.gpsimd.tensor_tensor(X[:, c], X[:, c], s["gb1"][:].unsqueeze(1).to_broadcast([P, TILES, D]), ALU.mult).then_inc(pool_seq, 1)
                    g.wait_ge(pool_seq, c * 2 + 2)
                    wait_first(g, x3_loaded, c * 16 + 16)
                    nc.gpsimd.tensor_tensor(X[:, c], X[:, c], x3[:], ALU.add).then_inc(x3_used, 1)

            @block.tensor
            def _(pe):
                pe.sem_inc(down_done, PRIMED)
                pe.sem_inc(up_done, PRIMED)
                pe.wait_ge(small_loaded, 16 * len(small))
                pe.wait_ge(loaded, 16 * len(large))
                pe.wait_ge(const_set, 3)
                with pe.Fori(0, NC) as c:
                    pe.wait_ge(xhat_ready, c + 1)
                    pe.wait_ge(log_copied, c + PRIMED)
                    for h in range(KH):
                        for t in range(TILES):
                            last = nc.tensor.transpose(tp[h][:, t * P:(t + 1) * P], xh[:, t, h * P:(h + 1) * P], s["ident"][:])
                        last.then_inc(trans_done, 1)
                    pe.wait_ge(hT_act, c + 1)
                    pe.wait_ge(hT_dve, c + 1)
                    for t in range(TILES):
                        for k in range(KH):
                            last = nc.tensor.matmul(tp[0][:, t * E1:(t + 1) * E1], hT[:, k, t * P:(t + 1) * P], wg[:, k, :], start=k == 0, stop=k == KH - 1)
                    last.then_inc(log_done, 1)
                    u = dn = 0
                    for st in stages:
                        if st[0] == "down":
                            _, e, src = st
                            pe.wait_ge(*read_by(c, last_writer[src]))
                            for p in range(2):
                                pe.wait_ge(added, c * E1 * 2 + max(0, dn - 1) + PRIMED)
                                for t in (2 * p, 2 * p + 1):
                                    for k in range(HT):
                                        last = nc.tensor.matmul(down_ps[p][:, t % 2, :], buf[src][:, k, t * P:(t + 1) * P], downs[:, e, k, :],
                                                                start=k == 0, stop=k == HT - 1)
                                last.then_inc(down_done, 1)
                                dn += 1
                            continue
                        name, kt, outs, src, _, dst = st
                        if src != "hT":
                            pe.wait_ge(*read_by(c, last_writer[src]))
                        for j in range(outs):
                            if u >= 4:
                                pe.wait_ge(*read_by(c, u - 4))
                            for k in range(kt):
                                last = nc.tensor.matmul(up_ps[u % 4][:], w[name][:, k, j * P:(j + 1) * P], buf[src][:, k, :],
                                                        start=k == 0, stop=k == kt - 1)
                            last.then_inc(up_done, 1)
                            last_writer[dst] = u
                            u += 1

            free_after = {"e2_l3": ("up", of_stage["e2_l2"] + HT), "e3_up": ("down", 2), "e1_w2": ("up", of_stage["e2_l3"] + HT),
                          "e2_l1": ("down", 0), "e0_up": ("down", 0), "e2_l2": ("down", 0), "e3_down": ("up", 0), "e1_w1": ("up", 0)}

            def target_free(eng, c, name):
                kind, n = free_after[name]
                eng.wait_ge(*((up_done, c * JOBS + n + PRIMED) if kind == "up" else (down_done, c * E1 * 2 + n + PRIMED)))

            @block.scalar
            def _(act):
                act.sem_inc(log_copied, PRIMED)
                act.wait_ge(small_loaded, 16 * len(small))
                with act.Fori(0, NC) as c:
                    for t in range(TILES):
                        last = nc.scalar.activation(junk[:, t, :], X[:, c, t, :], ACT.Square, accum_out=ssq[:, t:t + 1])
                    last.then_inc(ssq_ready, 1)
                    act.wait_ge(trans_done, c * 2 + 1)
                    nc.scalar.activation(hT[:, 0, :], tp[0][:], ACT.Identity, scale=nw[:, 1, 0:1]).then_inc(hT_act, 1)
                    act.wait_ge(log_done, c + 1)
                    nc.scalar.activation(lgs[:], tp[0][:, 0:TILES * E1].rearrange("p (t e) -> p t e", e=E1), ACT.Copy).then_inc(log_copied, 1)
                    act.wait_ge(shifted, c + 1)
                    nc.scalar.activation(pr[:], log[:], ACT.Exp).then_inc(exp_done, 1)
                    for u, (st, j) in enumerate(jobs):
                        name, _, _, _, fn, dst = st
                        if fn == "times":
                            continue
                        if j == 0:
                            target_free(act, c, name)
                            if name == "e1_w1":
                                act.wait_ge(dve_read, c * DVES + PRIMED)
                        act.wait_ge(up_done, c * JOBS + u + 1 + PRIMED)
                        nc.scalar.activation(buf[dst][:, j, :], up_ps[u % 4][:], ACT.Silu if fn == "silu" else ACT.Gelu).then_inc(act_read, 1)

            @block.vector
            def _(v):
                v.sem_inc(added, PRIMED)
                v.sem_inc(dve_read, PRIMED)
                v.wait_ge(small_loaded, 16 * len(small))
                v.wait_ge(const_set, 2)
                STEPS = 12
                with v.Fori(0, NC) as c:
                    seq = Tally(c * STEPS)
                    v.wait_ge(rms_ready, c + 1)
                    for t in range(TILES):
                        last = nc.vector.tensor_scalar(xh[:, t, :], X[:, c, t, :], rms[:, t:t + 1], None, ALU.mult)
                    last.then_inc(xhat_ready, 1)
                    v.wait_ge(trans_done, c * 2 + 2)
                    nc.vector.tensor_scalar(hT[:, 1, :], tp[1][:], nw[:, 1, 1:2], None, ALU.mult).then_inc(hT_dve, 1)
                    v.wait_ge(log_copied, c + 1 + PRIMED)
                    nc.vector.tensor_tensor(notnan[:], lgs[:], lgs[:], ALU.is_equal)
                    nc.vector.tensor_scalar(log[:], lgs[:], -FLT_MAX, FLT_MAX, ALU.max, ALU.min).then_inc(dve_seq, 1)
                    v.wait_ge(dve_seq, seq.up())
                    nc.vector.tensor_tensor(lgs[:], log[:], notnan[:], ALU.mult).then_inc(dve_seq, 1)
                    v.wait_ge(dve_seq, seq.up())
                    top_two(nc, v, lgs[:], dict(mx=mx, log=log, pr=pr, z=z, top=top, idx=idx, idf=idf, cw=cw, eq=eq, iota=iota,
                                                out=we, probs=probs), TILES, E1, 1e-8, dve_seq, seq, shifted, exp_done, c, we_ready)
                    v.wait_ge(we_ready, c + 1)
                    v.wait_ge(x3_used, c + 1 + PRIMED)
                    dn = 0
                    for st in stages:
                        if st[0] == "e1_w2":
                            for j in range(HT):
                                u = of_stage["e1_w2"] + j
                                if j == 0:
                                    target_free(v, c, "e1_w2")
                                v.wait_ge(*read_by(c, of_stage["e1_w1"] + j))
                                v.wait_ge(up_done, c * JOBS + u + 1 + PRIMED)
                                nc.vector.tensor_tensor(buf["hc"][:, j, :], up_ps[u % 4][:], buf["hs"][:, j, :], ALU.mult).then_inc(dve_read, 1)
                        elif st[0] == "down":
                            for p in range(2):
                                v.wait_ge(down_done, c * E1 * 2 + dn + 1 + PRIMED)
                                v.wait_ge(added, c * E1 * 2 + max(0, dn - 1) + PRIMED)
                                for t in (2 * p, 2 * p + 1):
                                    last = nc.vector.scalar_tensor_tensor(X[:, c, t, MASKED:], down_ps[p][:, t % 2, :], we[:, t, st[1]:st[1] + 1],
                                                                          X[:, c, t, MASKED:], ALU.mult, ALU.add)
                                last.then_inc(added, 1)
                                dn += 1
                    assert seq.n == STEPS, seq.n


FLT_MAX = float(np.finfo(np.float32).max)


def rows(a, k):
    return np.ascontiguousarray(a.reshape(k, P, -1).transpose(1, 0, 2))


def layout(i):
    f = {k: np.asarray(v) for k, v in i.items()}
    a = {}
    a["x"] = f["L0_attn_x"].reshape(T, D)
    a["cvec"] = np.stack([f["L0_c"].reshape(KH, P).T, f["L1_c"].reshape(KH, P).T], axis=1)
    a["wmod"] = np.stack([rows(f["L0_wmod"], KH), rows(f["L1_wmod"], KH)], axis=1)
    a["wvT"] = rows(f["L0_attn_Wv"].T, KH)
    a["wo0"] = rows(f["L0_attn_Wo"], KH)
    a["wkq"] = np.stack([rows(f["L0_attn_Wk"], KH), rows(f["L0_attn_Wq"], KH)], axis=1)
    a["bkq"] = np.stack([f["L0_attn_bk"].reshape(KH, P).T, f["L0_attn_bq"].reshape(KH, P).T], axis=1)
    a["wg0"] = rows(f["L0_ffn_Wg"], KH)
    a["w1"] = np.stack([rows(w, KH) for w in f["L0_ffn_W1"]], axis=1)
    a["b1"] = f["L0_ffn_b1"].reshape(E0, H0 // P, P).transpose(2, 0, 1)
    a["w2"] = np.stack([rows(w, H0 // P) for w in f["L0_ffn_W2"]], axis=1)
    a["b2_0"] = f["L0_ffn_b2"]
    a["wo1"] = rows(f["L1_attn_wo"].T, KH)
    a["bo1"] = np.broadcast_to(f["L1_attn_bo"], (P, D))
    a["wkv1"] = rows(np.concatenate([f["L1_attn_wk"].T, f["L1_attn_wv"].T], axis=1), KH)
    a["wq1"] = rows(f["L1_attn_wq"].T, KH)
    a["nw"] = np.stack([f["L1_ffn_n1_w"].reshape(KH, P).T, f["L1_ffn_n2_w"].reshape(KH, P).T], axis=1)
    a["qkw"] = np.broadcast_to(np.stack([f["L1_ffn_qn_w"], f["L1_ffn_kn_w"]]), (P, 2, HD))
    a["wqkv"] = rows(np.concatenate([f["L1_ffn_wq"].T, f["L1_ffn_wk"].T, f["L1_ffn_wv"].T], axis=1), KH)
    wo = np.zeros((GROUPS, GH, 32, KEEP), np.float32)
    wo[:, :, :HD, :] = f["L1_ffn_wo"].T.reshape(GROUPS, GH, HD, D)[..., MASKED:]
    a["wo_pad"] = wo.reshape(GROUPS, P, KEEP).transpose(1, 0, 2)
    a["wg1"] = rows(f["L1_ffn_gate_w"].T, KH)
    up = lambda n: rows(f["L1_ffn_" + n].T, f["L1_ffn_" + n].shape[1] // P)
    down = lambda n: rows(f["L1_ffn_" + n].T[:, MASKED:], f["L1_ffn_" + n].shape[1] // P)
    for n in UPS:
        a["m_" + n] = up(n)
    a["downs"] = np.stack([down(n) for n in DOWNS], axis=1)
    t = np.arange(P, dtype=np.float64)
    a["maskT"] = np.where(t[:, None] <= t[None, :], DECAY ** -t[:, None], 0.0).astype(np.float32)
    a["dcol"] = np.stack([DECAY ** t, DECAY ** (P - t)], axis=1).astype(np.float32)
    a["iota"] = np.broadcast_to(np.arange(E0, dtype=np.float32), (P, E0))
    a["ident"] = np.eye(P, dtype=np.float32)
    head = np.arange(P) // HD
    a["same_head"] = (head[:, None] == head[None, :]).astype(np.float32)
    m = np.arange(P)
    a["den_row"] = (m[:, None] == 32 * (m[None, :] // 32) + HD).astype(np.float32)
    return {k: np.ascontiguousarray(v) for k, v in a.items()}


UPS = ("e0_up", "e1_w1", "e1_w2", "e2_l1", "e2_l2", "e2_l3", "e3_down", "e3_up")
DOWNS = ("e0_down", "e1_down", "e2_l4", "e3_out")


def program(nc, shapes, out, upto=99):
    d = {}
    for name, shape in shapes.items():
        d[name] = nc.dram_tensor(f"in_{name}", shape, F32, kind="ExternalInput").ap()
    d["out"] = out
    d["x3"] = nc.dram_tensor("x3", [T, D], F32, kind="Internal").ap()
    s = {}

    def keep(c, name, shape, dt=F32, side="left"):
        s[name] = c.enter_context(nc.sbuf_tensor("s_" + name, shape, dt, side=side))

    with ExitStack() as base:
        keep(base, "xres", [P, NC, TILES, D])
        keep(base, "ident", [P, P])
        keep(base, "gb1", [P, D])
        mods = ExitStack()
        keep(mods, "modc", [P, 16], side="right")
        keep(mods, "gates", [P, 4, D], side="right")
        keep(mods, "sb1", [P, D], side="right")
        keep(mods, "cb1", [P, D], side="right")
        keep(mods, "wo1", [P, KH, D], side="right")
        keep(mods, "bo1", [P, D], side="right")
        with ExitStack() as layer0:
            keep(layer0, "wv0", [P, KH, D], side="right")
            keep(layer0, "h2T", [P, NC, KH, CH], side="right")
            keep(layer0, "we0", [P, NC, TILES, E0], side="right")
            keep(layer0, "w1", [P, E0, KH, H0], side="right")
            keep(layer0, "w2", [P, E0, H0 // P, D], side="right")
            keep(layer0, "b1", [P, E0, H0 // P], side="right")
            setup(nc, d, s)
            if upto > 2:
                layer0_pass(nc, d, s)
        lin = ExitStack()
        keep(lin, "qfT", [P, NC, KH, CH], side="right")
        keep(lin, "kvb", [P, KH, P], side="right")
        keep(lin, "ksb", [P, KH, P], side="right")
        if upto > 3:
            lin_keys(nc, d, s)
        with ExitStack() as mid:
            keep(mid, "qk", [P, NC, TILES, 2 * D])
            keep(mid, "vx", [P, NC, TILES, HEADS * (HD + 1)])
            keep(mid, "shift", [P, NC, TILES, HEADS, 3], BF16)
            keep(mid, "knorm", [P, HEADS])
            if upto > 4:
                lin_out(nc, d, s)
            lin.close()
            mods.close()
            if upto > 5:
                shifts(nc, d, s)
                softmax(nc, d, s)
        if upto > 6:
            ffn1(nc, d, s)


def kernel(**inputs):
    import concourse.bacc as _bacc
    from concourse.bass_utils import run_bass_kernel_spmd as _run

    nc = _bacc.Bacc("TRN2", target_bir_lowering=False, num_devices=1)
    arrays = layout(inputs)
    out = nc.dram_tensor("out_0_dram", (T, D), F32, kind="ExternalOutput").ap()
    program(nc, {k: v.shape for k, v in arrays.items()}, out)
    r = _run(nc, [{f"in_{k}": v for k, v in arrays.items()}], core_ids=[0])
    return r.results[0]["out_0_dram"].reshape(1, T, D)
```
